# Optimizing a Trainium2 kernel written in Bass

```python
import numpy as np
import jax
import jax.numpy as jnp

def _softmax(x, axis=-1):
    return jax.nn.softmax(x, axis=axis)

def _gelu(x):
    return jax.nn.gelu(x, approximate=True)

def _silu(x):
    return jax.nn.silu(x)

def _sigmoid(x):
    return jax.nn.sigmoid(x)

def _layernorm(x, axis=-1, eps=1e-05):
    m = jnp.mean(x, axis=axis, keepdims=True)
    v = jnp.var(x, axis=axis, keepdims=True)
    return (x - m) / jnp.sqrt(v + eps)

def _scatter_add(tgt, idx, src, axis=0):
    return tgt.at[idx].add(src)

def _segment_sum(src, seg, n):
    return jax.ops.segment_sum(src, seg, n)
kernel_name = 'mk_early_fusion_d2_tok_img256_r4_17d28a'

def setup_inputs(seed: int=0):
    np.random.seed(seed)
    _w = jnp.asarray

    def _rec_inputs():
        import jax
        import jax.numpy as jnp
        _rk = jax.random.key(seed)
        x = 7.22013e-05 + 1.00017 * jax.random.normal(jax.random.fold_in(_rk, 1), (2, 1, 1024, 64), jnp.float32)
        txt = 10 + 10 * jax.random.normal(jax.random.fold_in(_rk, 2), (2, 77, 64), jnp.float32)
        return (x, txt)
    x, txt = _rec_inputs()

    def _L0_tok_setup():
        import jax, jax.numpy as jnp
        import numpy as np
        T, D_IN, D_INT, D_OUT, B = (1024, 64, 64, 64, 8)
        key = jax.random.key(seed)
        ks = jax.random.split(key, 12)
        s_in = 1.0 / np.sqrt(D_IN)
        s_int = 1.0 / np.sqrt(D_INT)
        return {'x_batched': jax.random.normal(ks[0], (B, 1, T, D_IN), dtype=jnp.float32), 'd_gamma_batched': jax.random.uniform(ks[1], (T, T), dtype=jnp.float32), 'Wq': jax.random.uniform(ks[2], (D_IN, D_INT), jnp.float32, -s_in, s_in), 'bq': jax.random.uniform(ks[3], (D_INT,), jnp.float32, -s_in, s_in), 'Wk': jax.random.uniform(ks[4], (D_IN, D_INT), jnp.float32, -s_in, s_in), 'bk': jax.random.uniform(ks[5], (D_INT,), jnp.float32, -s_in, s_in), 'Wv': jax.random.uniform(ks[6], (D_IN, D_INT), jnp.float32, -s_in, s_in), 'bv': jax.random.uniform(ks[7], (D_INT,), jnp.float32, -s_in, s_in), 'Wo': jax.random.uniform(ks[8], (D_INT, D_OUT), jnp.float32, -s_int, s_int), 'bo': jax.random.uniform(ks[9], (D_OUT,), jnp.float32, -s_int, s_int), 'prelu_a': jnp.float32(0.25)}
    _L0_tok_all = _L0_tok_setup()
    _L0_tok_in = {k: v for k, v in _L0_tok_all.items() if k in ('d_gamma_batched', 'Wq', 'bq', 'Wk', 'bk', 'Wv', 'bv', 'Wo', 'bo', 'prelu_a')}
    del _L0_tok_all

    def _L0_attn_setup():
        import jax, jax.numpy as jnp
        import numpy as np
        key = jax.random.key(seed)
        ks = jax.random.split(key, 5)
        b, t, e, h = (8, 256, 64, 8)
        w = lambda k, shape: jax.random.normal(k, shape, dtype=jnp.float32) * 0.02
        return {'x': jax.random.normal(ks[0], (b, t, e), dtype=jnp.float32), 'Wq': w(ks[1], (e, e * h)), 'bq': jnp.zeros((e * h,), jnp.float32), 'Wk': w(ks[2], (e, e * h)), 'bk': jnp.zeros((e * h,), jnp.float32), 'Wv': w(ks[3], (e, e * h)), 'bv': jnp.zeros((e * h,), jnp.float32), 'Wu': w(ks[4], (e * h, e)), 'bu': jnp.zeros((e,), jnp.float32)}
    _L0_attn_all = _L0_attn_setup()
    _L0_attn_in = {k: v for k, v in _L0_attn_all.items() if k in ('Wq', 'bq', 'Wk', 'bk', 'Wv', 'bv', 'Wu', 'bu')}
    del _L0_attn_all

    def _L0_ffn_setup():
        import jax, jax.numpy as jnp
        import numpy as np
        B, S, D = (8, 1024, 64)
        H = 4 * D
        CAPACITY = 0.5
        key = jax.random.key(seed)
        ks = jax.random.split(key, 6)
        x = jax.random.normal(ks[0], (B, S, D), dtype=jnp.float32)
        attention_mask = jnp.zeros((B, 1, 1, S), dtype=jnp.float32)
        wr = jax.random.normal(ks[1], (D, 1), dtype=jnp.float32) * 0.02
        br = jnp.zeros((1,), dtype=jnp.float32)
        w1 = jax.random.normal(ks[2], (D, H), dtype=jnp.float32) * 0.02
        b1 = jnp.zeros((H,), dtype=jnp.float32)
        w2 = jax.random.normal(ks[3], (H, D), dtype=jnp.float32) * 0.02
        b2 = jnp.zeros((D,), dtype=jnp.float32)
        return {'x': x, 'attention_mask': attention_mask, 'wr': wr, 'br': br, 'w1': w1, 'b1': b1, 'w2': w2, 'b2': b2}
    _L0_ffn_all = _L0_ffn_setup()
    _L0_ffn_in = {k: v for k, v in _L0_ffn_all.items() if k in ('attention_mask', 'wr', 'br', 'w1', 'b1', 'w2', 'b2')}
    del _L0_ffn_all

    def _L1_attn_setup():
        import jax, jax.numpy as jnp
        import numpy as np
        B, L, H, C, D = (16, 1024, 64, 1, 64)

        def krylov(L, A, b, c):
            x = b[..., None]
            A_ = A
            while x.shape[-1] < L:
                x = jnp.concatenate([x, jnp.einsum('chij,chjt->chit', A_, x)], axis=-1)
                A_ = jnp.einsum('chij,chjk->chik', A_, A_)
            x = x[..., :L]
            return jnp.einsum('chd,chdl->chl', c, x)
        key = jax.random.key(seed)
        k1, k2 = jax.random.split(key)
        u = jax.random.normal(k1, (B, L, H), dtype=jnp.float32)
        c = jax.random.normal(k2, (C, H, D), dtype=jnp.float32)
        return {'u': u, 'c': c}
    _L1_attn_all = _L1_attn_setup()
    _L1_attn_in = {k: v for k, v in _L1_attn_all.items() if k in ('c',)}
    del _L1_attn_all

    def _L1_ffn_setup():
        import jax, jax.numpy as jnp
        import numpy as np
        B, S, D, H, E, K = (8, 2048, 64, 256, 8, 2)
        key = jax.random.key(seed)
        ks = jax.random.split(key, 7)
        s_in = 1.0 / np.sqrt(D)
        s_hid = 1.0 / np.sqrt(H)
        return {'x': jax.random.normal(ks[0], (B, S, D), dtype=jnp.float32), 'Wg': jax.random.uniform(ks[1], (E, D), jnp.float32, -s_in, s_in), 'bg': jax.random.uniform(ks[2], (E,), jnp.float32, -s_in, s_in), 'W1': jax.random.uniform(ks[3], (E, H, D), jnp.float32, -s_in, s_in), 'b1': jax.random.uniform(ks[4], (E, H), jnp.float32, -s_in, s_in), 'W2': jax.random.uniform(ks[5], (E, D, H), jnp.float32, -s_hid, s_hid), 'b2': jax.random.uniform(ks[6], (E, D), jnp.float32, -s_hid, s_hid)}
    _L1_ffn_all = _L1_ffn_setup()
    _L1_ffn_in = {k: v for k, v in _L1_ffn_all.items() if k in ('Wg', 'bg', 'W1', 'b1', 'W2', 'b2')}
    del _L1_ffn_all
    return {'x': x, 'txt': txt, 'L0_tok_d_gamma_batched': _L0_tok_in['d_gamma_batched'], 'L0_tok_Wq': _L0_tok_in['Wq'], 'L0_tok_bq': _L0_tok_in['bq'], 'L0_tok_Wk': _L0_tok_in['Wk'], 'L0_tok_bk': _L0_tok_in['bk'], 'L0_tok_Wv': _L0_tok_in['Wv'], 'L0_tok_bv': _L0_tok_in['bv'], 'L0_tok_Wo': _L0_tok_in['Wo'], 'L0_tok_bo': _L0_tok_in['bo'], 'L0_tok_prelu_a': _L0_tok_in['prelu_a'], 'L0_attn_Wq': _L0_attn_in['Wq'], 'L0_attn_bq': _L0_attn_in['bq'], 'L0_attn_Wk': _L0_attn_in['Wk'], 'L0_attn_bk': _L0_attn_in['bk'], 'L0_attn_Wv': _L0_attn_in['Wv'], 'L0_attn_bv': _L0_attn_in['bv'], 'L0_attn_Wu': _L0_attn_in['Wu'], 'L0_attn_bu': _L0_attn_in['bu'], 'L0_ffn_attention_mask': _L0_ffn_in['attention_mask'], 'L0_ffn_wr': _L0_ffn_in['wr'], 'L0_ffn_br': _L0_ffn_in['br'], 'L0_ffn_w1': _L0_ffn_in['w1'], 'L0_ffn_b1': _L0_ffn_in['b1'], 'L0_ffn_w2': _L0_ffn_in['w2'], 'L0_ffn_b2': _L0_ffn_in['b2'], 'L1_attn_c': _L1_attn_in['c'], 'L1_ffn_Wg': _L1_ffn_in['Wg'], 'L1_ffn_bg': _L1_ffn_in['bg'], 'L1_ffn_W1': _L1_ffn_in['W1'], 'L1_ffn_b1': _L1_ffn_in['b1'], 'L1_ffn_W2': _L1_ffn_in['W2'], 'L1_ffn_b2': _L1_ffn_in['b2']}

def reference(x, txt, L0_tok_d_gamma_batched, L0_tok_Wq, L0_tok_bq, L0_tok_Wk, L0_tok_bk, L0_tok_Wv, L0_tok_bv, L0_tok_Wo, L0_tok_bo, L0_tok_prelu_a, L0_attn_Wq, L0_attn_bq, L0_attn_Wk, L0_attn_bk, L0_attn_Wv, L0_attn_bv, L0_attn_Wu, L0_attn_bu, L0_ffn_attention_mask, L0_ffn_wr, L0_ffn_br, L0_ffn_w1, L0_ffn_b1, L0_ffn_w2, L0_ffn_b2, L1_attn_c, L1_ffn_Wg, L1_ffn_bg, L1_ffn_W1, L1_ffn_b1, L1_ffn_W2, L1_ffn_b2):
    import jax
    import jax.numpy as jnp

    def _L0_tok_ref(x_batched, d_gamma_batched, Wq, bq, Wk, bk, Wv, bv, Wo, bo, prelu_a):
        import jax, jax.numpy as jnp
        import numpy as np
        T, D_IN, D_INT, D_OUT, B = (1024, 64, 64, 64, 8)
        x = x_batched.reshape(x_batched.shape[0], T, D_IN)
        q = x @ Wq + bq
        k = x @ Wk + bk
        v = x @ Wv + bv
        scores = jnp.einsum('btd,bsd->bts', q, k)
        retained = jnp.einsum('bts,bsd->btd', d_gamma_batched * scores, v)
        y = retained @ Wo + bo
        out = jnp.where(y >= 0, y, prelu_a * y)
        return out

    def _L0_attn_ref(x, Wq, bq, Wk, bk, Wv, bv, Wu, bu):
        import jax, jax.numpy as jnp
        import numpy as np
        b, t, e = x.shape
        h = Wq.shape[1] // e
        q = (x @ Wq + bq).reshape(b, t, h, e)
        k = (x @ Wk + bk).reshape(b, t, h, e)
        v = (x @ Wv + bv).reshape(b, t, h, e)
        scores = jnp.einsum('bihe,bjhe->bhij', q, k) / jnp.sqrt(jnp.asarray(e, jnp.float32))
        i = jnp.arange(t)[:, None]
        j = jnp.arange(t)[None, :]
        scores = jnp.where(j >= i, -jnp.inf, scores)
        scores = jnp.where(i == 0, 0.0, scores)
        att = jax.nn.softmax(scores, axis=-1)
        att = jnp.where(i == 0, 0.0, att)
        out = jnp.einsum('bhij,bjhe->bihe', att, v).reshape(b, t, h * e)
        return out @ Wu + bu

    def _L0_ffn_ref(x, attention_mask, wr, br, w1, b1, w2, b2):
        import jax, jax.numpy as jnp
        import numpy as np
        B, S, D = (8, 1024, 64)
        H = 4 * D
        CAPACITY = 0.5
        b, s, d = x.shape
        weights = (jnp.einsum('bsd,do->bso', x, wr) + br)[..., 0]
        k = max(1, int(CAPACITY * s))
        kk = k - 1 if k > 1 else 1
        _, idx = jax.lax.top_k(weights, k)
        sel_idx = idx[:, :kk]
        sel = jnp.take_along_axis(x, sel_idx[:, :, None], axis=1)
        h = jax.nn.gelu(jnp.einsum('bkd,dh->bkh', sel, w1) + b1)
        y = jnp.einsum('bkh,hd->bkd', h, w2) + b2
        w_sel = jnp.take_along_axis(weights, sel_idx, axis=1)
        y = y * w_sel[..., None]
        batch_idx = jnp.arange(b)[:, None]
        processed = jnp.zeros_like(x).at[batch_idx, sel_idx].set(y)
        return processed + x

    def _L1_attn_ref(u, c):
        import jax, jax.numpy as jnp
        import numpy as np
        B, L, H, C, D = (16, 1024, 64, 1, 64)

        def krylov(L, A, b, c):
            x = b[..., None]
            A_ = A
            while x.shape[-1] < L:
                x = jnp.concatenate([x, jnp.einsum('chij,chjt->chit', A_, x)], axis=-1)
                A_ = jnp.einsum('chij,chjk->chik', A_, A_)
            x = x[..., :L]
            return jnp.einsum('chd,chdl->chl', c, x)
        Cc, Hh, Dd = c.shape
        A = jnp.zeros((Dd, Dd), c.dtype).at[1:, :-1].set(jnp.eye(Dd - 1, dtype=c.dtype))
        A = jnp.broadcast_to(A, (Cc, Hh, Dd, Dd))
        b = jnp.zeros((Dd,), c.dtype).at[0].set(1.0)
        b = jnp.broadcast_to(b, (Cc, Hh, Dd))
        ub = jnp.transpose(u, (0, 2, 1))
        l = ub.shape[-1]
        f = krylov(l, A, b, c)
        n = 2 * l
        u_f = jnp.fft.rfft(ub, n=n)
        v_f = jnp.fft.rfft(f, n=n)
        y_f = jnp.einsum('bhl,chl->bchl', u_f, v_f)
        y = jnp.fft.irfft(y_f, n=n)[..., :l]
        y = y.reshape(y.shape[0], -1, l)
        return jnp.transpose(y, (0, 2, 1))

    def _L1_ffn_ref(x, Wg, bg, W1, b1, W2, b2):
        import jax, jax.numpy as jnp
        import numpy as np
        B, S, D, H, E, K = (8, 2048, 64, 256, 8, 2)
        gate_scores = jnp.einsum('bsd,ed->bse', x, Wg) + bg
        topk_scores, topk_idx = jax.lax.top_k(gate_scores, K)
        topk_probs = jax.nn.softmax(topk_scores, axis=-1)
        combine = jnp.sum(topk_probs[..., None] * jax.nn.one_hot(topk_idx, E, dtype=x.dtype), axis=-2)
        out = jnp.zeros_like(x)
        for e in range(E):
            h = jax.nn.relu(jnp.einsum('bsd,hd->bsh', x, W1[e]) + b1[e])
            y = jnp.einsum('bsh,dh->bsd', h, W2[e]) + b2[e]
            out = out + combine[..., e:e + 1] * y
        return out
    h = _L0_tok_ref(x, L0_tok_d_gamma_batched, L0_tok_Wq, L0_tok_bq, L0_tok_Wk, L0_tok_bk, L0_tok_Wv, L0_tok_bv, L0_tok_Wo, L0_tok_bo, L0_tok_prelu_a)
    h = jnp.concatenate([h, txt], axis=1)
    h = h + _L0_attn_ref(_layernorm(h, axis=-1), L0_attn_Wq, L0_attn_bq, L0_attn_Wk, L0_attn_bk, L0_attn_Wv, L0_attn_bv, L0_attn_Wu, L0_attn_bu)
    h = h + _L0_ffn_ref(_layernorm(h, axis=-1), L0_ffn_attention_mask, L0_ffn_wr, L0_ffn_br, L0_ffn_w1, L0_ffn_b1, L0_ffn_w2, L0_ffn_b2)
    h = h + _L1_attn_ref(_layernorm(h, axis=-1), L1_attn_c)
    h = h + _L1_ffn_ref(_layernorm(h, axis=-1), L1_ffn_Wg, L1_ffn_bg, L1_ffn_W1, L1_ffn_b1, L1_ffn_W2, L1_ffn_b2)
    return h

_drawn_inputs = setup_inputs


def setup_inputs(seed=0):
    import zlib

    import numpy as np

    out = dict(_drawn_inputs(seed))
    spreads = {'L0_attn_bq': (0.0, 0.8),
     'L0_attn_bk': (0.0, 2.0),
     'L0_attn_bv': (0.0, 0.8),
     'L0_attn_bu': (0.0, 0.8),
     'L0_ffn_b1': (0.0, 0.8),
     'L0_ffn_b2': (0.0, 2.0)}
    factors = {'L0_tok_bo': 25.954,
     'L0_attn_Wq': 8.0,
     'L0_attn_Wk': 8.0,
     'L0_attn_Wv': 8.0,
     'L0_attn_Wu': 8.0,
     'L0_ffn_wr': 8.0,
     'L0_ffn_w1': 8.0,
     'L0_ffn_w2': 8.0,
     'L1_ffn_Wg': 8.0,
     'L1_ffn_bg': 8.0,
     'L1_ffn_W1': 8.0,
     'L1_ffn_b1': 8.0,
     'L1_ffn_W2': 8.0,
     'L1_ffn_b2': 64.0}
    for name, (base, spread) in spreads.items():
        noise = np.random.default_rng([zlib.crc32(name.encode()), seed]).standard_normal(out[name].shape)
        drawn = base * np.exp(spread * noise) if base else spread * noise
        out[name] = jnp.asarray(drawn.astype(out[name].dtype))
    for name, factor in factors.items():
        out[name] = (out[name] * factor).astype(out[name].dtype)
    return out
```

```python
from contextlib import ExitStack

import concourse.bass as bass
from concourse import mybir

F32 = mybir.dt.float32
F32R = mybir.dt.float32r
BF16 = mybir.dt.bfloat16
ALU = mybir.AluOpType
ACT = mybir.ActivationFunctionType
AX = mybir.AxisListType

P = 128
D = 64
B = 2
T = 1024
TXT = 77
S = T + TXT
NT = -(-S // P)
SP_ = NT * P
G = B * NT
NH = 8
HID = 256
NE = 8
KK = max(1, int(0.5 * S)) - 1
EPS = 1e-5
NEG = -1e30
CW = 384
NC = SP_ // CW
TPC = CW // P
TT = T // P

O_TQ, O_TK, O_TV = 0, 128, 256
O_Q, O_K = 320, 832
O_W1 = 1344
O_G = 1600
O_E = 1608
O_WR = O_E + NE * HID
NW = O_WR + 1
C_TBQ, C_TBK, C_BQ, C_BK, C_B1, C_EB1, C_A, C_BR = 0, 1, 2, 10, 18, 20, 36, 37
NCOL = 38
R_TBV, R_TBO, R_BU, R_B2, R_BG = 0, 64, 128, 192, 256
NROW = 264

STEPS = [(c, j) for c in range(NC) for j in range(TPC * (c + 1))]
NS = len(STEPS)
SMAX = [(i, a, min(a + 512, P * (i + 1))) for i in range(NT) for a in range(0, P * (i + 1), 512)]
NM = len(SMAX)
NA = 2 * NC + NM + 1
LAG = 2
PROJECT_AT = {0: (0, 1), 1: (2,), 2: (3,), 3: (4,), 4: (5,)}
MAX_AT = {6 + k // 2: tuple(x for x in (k, k + 1) if x < NM) for k in range(0, NM, 2)}
WHOLE_AT, TURN_MAX_AT = 14, 15
LAST = [STEPS.index((c, TPC * (c + 1) - 1)) for c in range(NC)]
COPY_AT = [x + LAG for x in LAST]
BACK_AT = [x + LAG + 2 for x in LAST]


def ln_range(k):
    return (k % 2) * NT, (k % 2) * NT + NT


def early_fusion(nc, ins, out):
    ctx = ExitStack()
    with ctx:
        def sb(name, shape, dt=F32, where=None):
            return (where or ctx).enter_context(nc.sbuf_tensor(name, shape, dt))

        def sem(name):
            return ctx.enter_context(nc.semaphore(name))

        WH = sb("w_hi", [P, NW], F32R)
        WL = sb("w_lo", [D, NW], F32R)
        WRH = sb("wr_hi", [P, P], F32R)
        WRL = sb("wr_lo", [D, P], F32R)
        cols = sb("cols", [P, NCOL])
        rows = sb("rows", [P, NROW])
        ident = sb("ident", [P, P])
        ones = sb("ones", [P, P])
        identb = sb("identb", [P, P], BF16)
        zerob = sb("zerob", [P, P], BF16)
        mask_s = sb("mask_s", [P, P], BF16)
        mask_t = sb("mask_t", [P, P], BF16)
        before = sb("before", [P, P])
        after = sb("after", [P, P])
        ebefore = sb("ebefore", [P, NE, NE])
        h = sb("h", [P, G, D])
        UU = sb("UU", [P, 2, G, D])
        sq = sb("sq", [P, G, D])
        acc = sb("acc", [P, G, D])
        US = sb("US", [P, B * SP_], F32R)
        stat = sb("stat", [P, 10, G])
        toep = sb("toep", [P, D, D])
        WPH = sb("WPH", [P, NH * D], F32R)
        WPL = sb("WPL", [D, NH * D], F32R)
        bp = sb("bp", [P, NH, D])
        w2 = sb("w2", [P, 2, D])
        ew2 = sb("ew2", [P, 2, NE, D])
        b2raw = sb("b2raw", [65, NE * D])
        b2p = sb("b2p", [65, NE * D], BF16)
        onesb = sb("onesb", [65, P], BF16)
        bvT = sb("bvT", [D, NH])
        two = sb("two", [D, D])
        u = UU[:, 1]

        st1 = ExitStack()
        XR = sb("x_raw", [P, B * T], F32, st1)
        XS = sb("x_split", [P, B * T], F32R, st1)
        WR = sb("w_raw", [P, NW], F32, st1)
        wvT = sb("wvT", [D, NH, 2, D], F32, st1)
        bvrep = sb("bvrep", [D, NH, P], F32, st1)
        wu = sb("wu", [D, NH, D], F32, st1)
        wr_rep = sb("wr_rep", [P, P], F32, st1)
        gam = sb("gam", [P, TT, T], F32, st1)
        tq = sb("tq", [P, T], F32R, st1)
        tk = sb("tk", [P, T], F32R, st1)
        tql = sb("tql", [D, T], F32R, st1)
        tv = sb("tv", [P, TT, D], F32, st1)
        ptt = sb("ptt", [P, 4, 512], F32, st1)
        tret = sb("tret", [D, T], F32, st1)
        st1.close()

        st2 = ExitStack()
        VX = sb("VX", [P, B, NT, NH, D + 1], F32, st2)
        qs = [sb(f"qs{b}", [P, SP_], F32R, st2) for b in range(B)]
        ks = [sb(f"ks{b}", [P, SP_], F32R, st2) for b in range(B)]
        ql = [sb(f"ql{b}", [D + 1, SP_], F32R, st2) for b in range(B)]
        kh = [sb(f"kh{b}", [D + 1, SP_], F32R, st2) for b in range(B)]
        vs = [sb(f"vs{b}", [P, NT, D + 1], F32, st2) for b in range(B)]
        ot = sb("ot", [D + 1, 2, CW], F32, st2)
        pt = sb("pt", [P, 6, CW], F32, st2)
        wh4 = sb("wh4", [P, 2, 2, D], F32R, st2)
        wl4 = sb("wl4", [D, 2, 2, D], F32R, st2)
        mpart = sb("mpart", [P, B, NT, 3], F32, st2)
        mneg = sb("mneg", [P, B, NT], F32, st2)
        mrow = [sb(f"mrow{b}", [NT, P], F32R, st2) for b in range(B)]
        rden = sb("rden", [P, 2, TPC], F32, st2)
        onrm = sb("onrm", [P, 2, TPC, D], F32, st2)
        hank = sb("hank", [P, D, D], F32, st2)
        st2.close()

        st3 = ExitStack()
        hT = sb("hT", [P, 2, SP_], F32, st3)
        wbc = sb("wbc", [P, B, SP_], F32, st3)
        scr = sb("scr", [P, SP_], F32, st3)
        rank4 = sb("rank4", [P, B, NT, 4], F32, st3)
        wcol = sb("wcol", [P, B, NT], F32, st3)
        rank = sb("rank", [P, B, NT], F32, st3)
        sel = sb("sel", [P, B, NT], F32, st3)
        eh = sb("eh", [P, NE, 2, 256], F32, st3)
        gate = sb("gate", [P, G, NE], F32, st3)
        gt = sb("gt", [P, G, NE, NE], F32, st3)
        eq = sb("eq", [P, G, NE, NE], F32, st3)
        erank = sb("erank", [P, G, NE], F32, st3)
        is0 = sb("is0", [P, G, NE], F32, st3)
        is1 = sb("is1", [P, G, NE], F32, st3)
        comb = sb("comb", [P, G, NE], F32, st3)
        yw = sb("yw", [P, 2, NE, D], F32, st3)
        ysum = sb("ysum", [P, 2, D], F32, st3)
        st3.close()

        ps = ctx.enter_context(nc.psum_tensor("ps", [P, 8, 512], F32))

        d_x, d_wtok, d_w, d_cols, d_rows, d_txt = (sem(n) for n in ("d_x", "d_wtok", "d_w", "d_cols", "d_rows", "d_txt"))
        d_gam = [sem(f"d_gam{s}") for s in range(TT)]
        d_wv, d_late, d_two, d_mrow, d_out = (sem(n) for n in ("d_wv", "d_late", "d_two", "d_mrow", "d_out"))
        s_const = sem("s_const")
        s_const_act = sem("s_const_act")
        s_split1 = sem("s_split1")
        s_split2 = sem("s_split2")
        s_tproj = sem("s_tproj")
        s_tround = sem("s_tround")
        s_tlow = sem("s_tlow")
        s_tv = sem("s_tv")
        s_tsc = sem("s_tsc")
        s_tpt = sem("s_tpt")
        s_tpv = sem("s_tpv")
        s_tret = sem("s_tret")
        s_ty = sem("s_ty")
        s_th = sem("s_th")
        s_var = sem("s_var")
        s_sd = sem("s_sd")
        s_u = sem("s_u")
        s_tr = sem("s_tr")
        s_uhi = sem("s_uhi")
        s_us = sem("s_us")
        s_wp = sem("s_wp")
        s_wps = sem("s_wps")
        s_bvr = sem("s_bvr")
        s_v = sem("s_v")
        s_vx = sem("s_vx")
        s_wsl = sem("s_wsl")
        s_a = sem("s_a")
        s_ar = sem("s_ar")
        s_af = sem("s_af")
        s_kh = sem("s_kh")
        s_mneg = sem("s_mneg")
        s_st = sem("s_st")
        s_vs = sem("s_vs")
        s_ex = sem("s_ex")
        s_pv = sem("s_pv")
        s_of = sem("s_of")
        s_to = sem("s_to")
        s_nf = sem("s_nf")
        s_h1 = sem("s_h1")
        s_r = sem("s_r")
        s_rd = sem("s_rd")
        s_gelu = sem("s_gelu")
        s_cv = sem("s_cv")
        s_cvf = sem("s_cvf")
        s_ush = sem("s_ush")
        s_g = sem("s_g")
        s_gf = sem("s_gf")
        s_d = sem("s_d")
        s_ed = sem("s_ed")
        s_hh = sem("s_hh")
        s_ha = sem("s_ha")
        s_hd = sem("s_hd")
        s_hu = sem("s_hu")
        s_y = sem("s_y")
        s_yf = sem("s_yf")
        s_fin = sem("s_fin")
        s_toep = sem("s_toep")
        s_b2 = sem("s_b2")
        s_dve = sem("s_dve")
        s_dvl = sem("s_dvl")
        s_dvm = sem("s_dvm")
        s_pool = sem("s_pool")
        s_step = sem("s_step")

        block = ctx.enter_context(nc.Block())

        @block.sync
        def _(sp):
            for half in range(2):
                sp.dma_start(XR[64 * half:64 * half + 64, :], ins["xT"]).then_inc(d_x, 16)
                sp.dma_start(WR[64 * half:64 * half + 64, 0:O_Q], ins["w64"][:, 0:O_Q]).then_inc(d_wtok, 16)
            sp.dma_start(cols[:], ins["cols"]).then_inc(d_cols, 16)
            sp.dma_start(rows[:], ins["rows"].broadcast_to([P, NROW])).then_inc(d_rows, 16)
            for s in range(TT):
                sp.dma_start(gam[:, s, :], ins["gammaT"][P * s:P * s + P, :]).then_inc(d_gam[s], 16)
            sp.dma_start(two[:], ins["two"]).then_inc(d_two, 16)
            sp.wait_ge(s_const, 1)
            for b in range(B):
                sp.dma_start(h[0:TXT, b * NT + TT, :], ins["txt"][b]).then_inc(d_txt, 16)
            for half in range(2):
                sp.dma_start(WR[64 * half:64 * half + 64, O_Q:NW], ins["w64"][:, O_Q:NW]).then_inc(d_w, 16)
            for half in range(2):
                sp.dma_start(wvT[:, :, half, :], ins["wvT"]).then_inc(d_wv, 16)
            sp.dma_start(bvT[:], ins["bvT"]).then_inc(d_wv, 16)
            sp.dma_start(wu[:], ins["wu"]).then_inc(d_wv, 16)
            sp.dma_start(w2[:], ins["w2"]).then_inc(d_late, 16)
            sp.dma_start(ew2[:], ins["ew2"]).then_inc(d_late, 16)
            for k in range(3):
                sp.dma_start(b2raw[32 * k:32 * k + 1, :], ins["eb2"]).then_inc(d_late, 16)
            sp.wait_ge(s_th, B)
            sp.wait_ge(s_split2, 1)
            sp.wait_ge(s_wps, 1)
            sp.dma_start(hank[:], bass.AP(ins["cpad"].tensor, 0, [[1, P], [3 * D, D], [1, D]])).then_inc(d_late, 16)

            def put_mrow(v, b):
                sp.wait_ge(s_af, NA * (v + 1) + 2)
                sp.dma_start(ql[b][D:D + 1, :].bitcast(F32).rearrange("o (t p) -> o t p", p=P),
                             mrow[b][:].bitcast(F32)).then_inc(d_mrow, 16)

            put_mrow(0, 0)
            put_mrow(1, 1)
            with sp.Fori(0, NH - 1) as i:
                put_mrow(2 * i + 2, 0)
                put_mrow(2 * i + 3, 1)

            for b in range(B):
                sp.wait_ge(s_fin, -(-(b * NT + TT) // 2))
                sp.dma_start(out[b, 0:T, :].rearrange("(t p) d -> p t d", p=P),
                             h[:, b * NT:b * NT + TT, :]).then_inc(d_out, 16)
                sp.wait_ge(s_fin, -(-(b * NT + NT) // 2))
                sp.dma_start(out[b, T:S, :], h[0:TXT, b * NT + TT, :]).then_inc(d_out, 16)
            sp.wait_ge(d_out, 16 * 2 * B)

        @block.gpsimd
        def _(pool):
            n = [0]

            def link(instruction):
                n[0] += 1
                instruction.then_inc(s_pool, 1)
                pool.wait_ge(s_pool, n[0])

            nc.gpsimd.memset(h[:, TT:G:NT, :], 0.0).then_inc(s_const, 1)
            link(nc.gpsimd.memset(ones[:], 1.0))
            link(nc.gpsimd.memset(zerob[:], 0.0))
            link(nc.gpsimd.affine_select(out=ident[:], in_=ones[:], compare_op=ALU.is_equal, fill=0.0,
                                         base=0, pattern=[[-1, P]], channel_multiplier=1))
            link(nc.gpsimd.affine_select(out=mask_s[:], in_=zerob[:], compare_op=ALU.is_gt, fill=NEG,
                                         base=0, pattern=[[-1, P]], channel_multiplier=1))
            link(nc.gpsimd.affine_select(out=mask_t[:], in_=zerob[:], compare_op=ALU.is_gt, fill=NEG,
                                         base=0, pattern=[[1, P]], channel_multiplier=-1))
            link(nc.gpsimd.affine_select(out=before[:], in_=ones[:], compare_op=ALU.is_gt, fill=0.0,
                                         base=0, pattern=[[-1, P]], channel_multiplier=1))
            link(nc.gpsimd.affine_select(out=after[:], in_=ones[:], compare_op=ALU.is_gt, fill=0.0,
                                         base=0, pattern=[[1, P]], channel_multiplier=-1))
            link(nc.gpsimd.affine_select(out=ebefore[:], in_=ones[:, 0:NE * NE].rearrange("p (e f) -> p e f", f=NE),
                                         compare_op=ALU.is_gt, fill=0.0,
                                         base=0, pattern=[[1, NE], [-1, NE]], channel_multiplier=0))
            link(nc.gpsimd.tensor_copy(identb[:], ident[:]))
            link(nc.gpsimd.memset(onesb[:], 1.0))
            nc.gpsimd.memset(b2p[:], 0.0).then_inc(s_const, 1)
            pool.wait_ge(d_w, 32)
            link(nc.gpsimd.tensor_copy(WH[:, O_Q:O_WR], WR[:, O_Q:O_WR]))
            nc.gpsimd.tensor_tensor(WL[:, O_Q:O_WR], WR[0:D, O_Q:O_WR], WH[0:D, O_Q:O_WR],
                                    ALU.subtract).then_inc(s_split2, 1)
            pool.wait_ge(s_split2, 1)

            pool.wait_ge(s_th, B)
            pool.wait_ge(s_wps, 1)
            for b in range(B):
                link(nc.gpsimd.memset(kh[b][D:D + 1, :].bitcast(F32), 1.0))
            link(nc.gpsimd.memset(VX[:, :, :, :, D:D + 1], 1.0))

            def slices(hd, guard):
                if guard is not None:
                    pool.wait_ge(s_a, guard)
                    pool.sem_inc(s_step, 1)
                for k, off in enumerate((O_Q, O_K)):
                    nc.gpsimd.tensor_copy(wh4[:, k], WH[:, bass.ds(hd * D + off, D)].unsqueeze(1)
                                          .broadcast_to([P, 2, D])).then_inc(s_wsl, 1)
                    nc.gpsimd.tensor_copy(wl4[:, k], WL[:, bass.ds(hd * D + off, D)].unsqueeze(1)
                                          .broadcast_to([D, 2, D])).then_inc(s_wsl, 1)

            def copy_keys(v, b):
                pool.wait_ge(s_ar, 2 * NC * (v + 1))
                pool.sem_inc(s_step, 1)
                nc.gpsimd.tensor_copy(kh[b][0:D, :], ks[b][0:D, :]).then_inc(s_kh, 1)

            def copy_values(v, b):
                pool.wait_ge(s_pv, NS * (v - 1) + 6)
                pool.sem_inc(s_step, 1)
                nc.gpsimd.tensor_copy(vs[b][:], VX[:, b, :, bass.ds(head_of[0], 1), :]
                                      .rearrange("p t o d -> p t (o d)")).then_inc(s_vs, 1)

            head_of = [0]
            slices(0, None)
            pool.wait_ge(s_vx, G)
            for b in range(B):
                nc.gpsimd.tensor_copy(vs[b][:], VX[:, b, :, 0, :]).then_inc(s_vs, 1)
            copy_keys(0, 0)
            copy_keys(1, 1)
            with pool.Fori(0, NH - 1) as i:
                head_of[0] = i + 1
                slices(i + 1, NA * (2 * i + 1) + 2 * NC)
                copy_values(2 * i + 2, 0)
                copy_keys(2 * i + 2, 0)
                copy_values(2 * i + 3, 1)
                copy_keys(2 * i + 3, 1)

            pool.wait_ge(d_late, 16 * 6)
            nc.gpsimd.tensor_copy(toep[:], hank[:, :, ::-1]).then_inc(s_toep, 1)
            pool.wait_ge(s_toep, 1)
            for k in range(3):
                r = slice(32 * k, 32 * k + 1)
                for _ in range(k):
                    link(nc.gpsimd.tensor_copy(b2p[r], b2raw[r]))
                    link(nc.gpsimd.tensor_tensor(b2raw[r], b2raw[r], b2p[r], ALU.subtract))
                nc.gpsimd.tensor_copy(b2p[r], b2raw[r]).then_inc(s_b2, 1)
                pool.wait_ge(s_b2, k + 1)

        @block.scalar
        def _(act):
            act.wait_ge(d_cols, 16)
            for b in range(B):
                for k in range(4):
                    act.wait_ge(s_tproj, 5 * b + k + 1)
                    dst = (tq if k < 2 else tk)[:, 512 * (k % 2):512 * (k % 2) + 512]
                    bias = cols[:, C_TBQ:C_TBQ + 1] if k < 2 else cols[:, C_TBK:C_TBK + 1]
                    nc.scalar.activation(dst, ps[:, k, :], ACT.Identity, bias=bias).then_inc(s_tround, 1)
                act.wait_ge(s_tpv, 16 * (b + 1))
                for k in range(2):
                    nc.scalar.activation(tret[:, 512 * k:512 * k + 512], ps[0:D, k, :], ACT.Copy).then_inc(s_tret, 1)

            def root(k):
                act.wait_ge(s_var, k + 1)
                g0, g1 = ln_range(k)
                nc.scalar.activation(stat[:, 3, g0:g1], stat[:, 2, g0:g1], ACT.Sqrt).then_inc(s_sd, 1)

            def high(k):
                for c in range(NC):
                    b, m = k % 2, NC * k + c
                    act.wait_ge(s_tr, m + 1)
                    nc.scalar.activation(US[0:D, b * SP_ + CW * c:b * SP_ + CW * c + CW], ps[0:D, c, 0:CW],
                                         ACT.Copy).then_inc(s_uhi, 1)

            root(0)
            root(1)
            high(0)
            high(1)

            def rounding(v, b, k):
                act.wait_ge(s_a, NA * v + k + 1)
                act.sem_inc(s_step, 1)
                c = k % NC
                dst = (qs if k < NC else ks)[b][:, CW * c:CW * c + CW]
                col = (C_BQ if k < NC else C_BK) + head_of[0]
                nc.scalar.activation(dst, ps[:, 4 + k % 2, 0:CW], ACT.Identity,
                                     bias=cols[:, bass.ds(col, 1)]).then_inc(s_ar, 1)

            def exp(w, s):
                c, j = STEPS[s]
                lo = max(P * j, CW * c) - CW * c
                act.wait_ge(s_st, NS * w + s + 1)
                act.wait_ge(s_pv, NS * w + s + 1)
                nc.scalar.activation(pt[:, s % 6, lo:CW], ps[:, s % 3, lo:CW],
                                     ACT.Exp, scale=D ** -0.5).then_inc(s_ex, 1)

            def copy_output(w, b, c):
                o = (c + NC * b) % 2
                act.wait_ge(s_pv, NS * w + LAST[c] + 1 + 6)
                act.wait_ge(s_to, NC * w + c + 1)
                nc.scalar.activation(ot[:, o, :], ps[0:D + 1, 6 + o, 0:CW], ACT.Copy).then_inc(s_of, 1)

            def slot(w, b, first=False, follow=True):
                for s in range(NS):
                    if follow:
                        for k in PROJECT_AT.get(s, ()):
                            rounding(w + 1, 1 - b, k)
                    exp(w, s)
                    for c in range(NC):
                        if COPY_AT[c] == s:
                            copy_output(w, b, c)
                        if COPY_AT[c] == s + NS and not first:
                            copy_output(w - 1, 1 - b, c)

            head_of = [0]
            act.sem_inc(s_ex, 3)
            act.sem_inc(s_of, 2)
            for k in range(2 * NC):
                rounding(0, 0, k)
            slot(0, 0, first=True)
            with act.Fori(0, NH - 1) as i:
                head_of[0] = i + 1
                slot(2 * i + 1, 1)
                slot(2 * i + 2, 0)
            slot(2 * NH - 1, 1, follow=False)
            copy_output(2 * NH - 1, 1, NC - 1)

            root(2)
            root(3)
            for b in range(B):
                high(2 + b)
            for b in range(B):
                for m in range(2):
                    for c in range(NC):
                        act.wait_ge(s_r, 12 * b + NC + NC * m + c + 1)
                        nc.scalar.activation(hT[:, m, CW * c:CW * c + CW], ps[:, 3 + (NC + NC * m + c) % 4, 0:CW],
                                             ACT.Gelu_apprx_tanh,
                                             bias=cols[:, C_B1 + m:C_B1 + m + 1]).then_inc(s_gelu, 1)
            root(4)
            root(5)
            root(6)
            root(7)
            act.sem_inc(s_ha, 2)
            act.sem_inc(s_hd, 2)
            for b in range(B):
                high(4 + b)

            def relu(t, e):
                act.wait_ge(s_hh, NE * t + e + 1)
                act.wait_ge(s_hu, NE * t + e + 1)
                for m in range(2):
                    ins_ = nc.scalar.activation(eh[:, e, m, :], ps[:, 4 + e % 4, 256 * m:256 * m + 256], ACT.Relu,
                                                bias=cols[:, C_EB1 + 2 * e + m:C_EB1 + 2 * e + m + 1])
                ins_.then_inc((s_ha, s_hd)[e % 2], 1)

            for e in range(NE):
                relu(0, e)
            act.wait_ge(s_d, 1)
            nc.scalar.activation(stat[:, 5, :], stat[:, 4, :], ACT.Exp).then_inc(s_ed, 1)
            with act.Fori(0, G // 2 - 1) as t:
                for e in range(0, NE, 2):
                    relu(t + 1, e)

        @block.tensor
        def _(pe):
            mm = nc.tensor.matmul

            def split2(dst, hi2, split, lo, split_hi, start, stop):
                mm(dst, hi2, split, start=start, stop=False)
                return mm(dst, lo, split_hi, start=False, stop=stop)

            pe.wait_ge(s_split1, 2)
            for b in range(B):
                x0 = b * T
                for k in range(4):
                    if b and k < 2:
                        pe.wait_ge(s_tret, 2 * b)
                    off = O_TQ if k < 2 else O_TK
                    cs = slice(x0 + 512 * (k % 2), x0 + 512 * (k % 2) + 512)
                    split2(ps[:, k, :], WH[:, off:off + P], XS[:, cs], WL[:, off:off + P], XS[0:D, cs],
                           True, True).then_inc(s_tproj, 1)
                if b:
                    pe.wait_ge(s_th, b)
                for t in range(TT):
                    cs = slice(x0 + P * t, x0 + P * t + P)
                    last = split2(ps[:, 4, D * t:D * t + D], XS[:, cs], WH[:, O_TV:O_TV + D],
                                  XS[0:D, cs], WL[:, O_TV:O_TV + D], t == 0, t == TT - 1)
                last.then_inc(s_tproj, 1)
                pe.wait_ge(s_tlow, 4 * (b + 1))
                pe.wait_ge(s_tv, b + 1)

                def retain(n):
                    m = 16 * b + n
                    pe.wait_ge(s_tpt, m + 1)
                    mm(ps[0:D, n % 2, :], tv[:, n // 2, :], ptt[:, m % 4, :], start=n < 2, stop=n >= 14).then_inc(s_tpv, 1)

                for n in range(16):
                    m = 16 * b + n
                    s, half = n // 2, n % 2
                    if m >= 3:
                        pe.wait_ge(s_tpt, m - 2)
                    ss, hs = slice(P * s, P * s + P), slice(512 * half, 512 * half + 512)
                    split2(ps[:, 5 + m % 3, :], tk[:, ss], tq[:, hs], tk[0:D, ss], tql[:, hs],
                           True, True).then_inc(s_tsc, 1)
                    if n >= LAG:
                        retain(n - LAG)
                for n in range(16 - LAG, 16):
                    retain(n)
                pe.wait_ge(s_tret, 2 * (b + 1))
                pe.wait_ge(d_two, 16)
                for t in range(TT):
                    last = mm(ps[:, 4, D * t:D * t + D], tret[:, P * t:P * t + P], two[:],
                              start=t == 0, stop=t == TT - 1)
                last.then_inc(s_ty, 1)

            pe.wait_ge(s_const, 2)
            pe.wait_ge(d_wv, 64)
            pe.wait_ge(s_bvr, 1)
            pe.wait_ge(s_tpt, 32)
            for hd in range(NH):
                mm(ps[:, 5, D * hd:D * hd + D], wvT[:, hd], wu[:, hd, :], start=hd == 0, stop=hd == NH - 1)
                last = mm(ps[:, 6, D * hd:D * hd + D], bvrep[:, hd, :], wu[:, hd, :], start=hd == 0, stop=hd == NH - 1)
            last.then_inc(s_wp, 1)

            def turn(k):
                for c in range(NC):
                    pe.wait_ge(s_u, k + 1 if k < 4 else k + 3)
                    if k:
                        pe.wait_ge(s_us, NC * (k - 1) + c + 1)
                    for t in range(TPC):
                        last = nc.tensor.transpose(ps[0:D, c, P * t:P * t + P], u[:, (k % 2) * NT + TPC * c + t, :], ident[:])
                    last.then_inc(s_tr, 1)

            pe.wait_ge(s_th, B)
            pe.wait_ge(s_wps, 1)
            turn(0)
            turn(1)
            for b in range(B):
                for t in range(NT):
                    n = b * NT + t
                    pe.wait_ge(s_us, NC * b + t // TPC + 1)
                    if n >= 4:
                        pe.wait_ge(s_vx, n - 3)
                    cs = slice(n * P, n * P + P)
                    split2(ps[:, 3 + n % 4, :], US[:, cs], WPH[:], US[0:D, cs], WPL[:], True, True).then_inc(s_v, 1)

            pe.sem_inc(s_pv, 6)
            pe.sem_inc(s_to, 2)

            def a_bank(k):
                return ps[:, 4 + k % 2]

            def project(v, b, k):
                if k == 0:
                    pe.wait_ge(s_wsl, 4 * (head_of[0] + 1))
                pe.wait_ge(s_af, NA * v + k + 1)
                cs = slice(b * SP_ + CW * (k % NC), b * SP_ + CW * (k % NC) + CW)
                split2(a_bank(k)[:, 0:CW], wh4[:, k // NC], US[:, cs], wl4[:, k // NC], US[0:D, cs],
                       True, True).then_inc(s_a, 1)

            def scores_for_max(v, b, k):
                i, a, z = SMAX[k]
                if k == 0:
                    pe.wait_ge(s_af, NA * v + 2 * NC + 2)
                pe.wait_ge(s_af, NA * v + 2 * NC + k + 1)
                bank = a_bank(2 * NC + k)
                diag = z == P * (i + 1)
                last = mm(bank[:, 0:z - a], qs[b][:, P * i:P * i + P], ks[b][:, a:z], start=True, stop=not diag)
                if diag:
                    last = mm(bank[:, z - a - P:z - a], identb[:], mask_s[:], start=False, stop=True)
                last.then_inc(s_a, 1)

            def turn_max(v, b):
                pe.wait_ge(s_af, NA * v + NA)
                pe.wait_ge(s_mneg, v + 1)
                nc.tensor.transpose(a_bank(NA - 1)[0:NT, 0:P], mneg[:, b], ident[:]).then_inc(s_a, 1)

            def scores(w, b, s):
                c, j = STEPS[s]
                lo = max(P * j, CW * c)
                z = CW * (c + 1)
                bank = ps[:, s % 3]
                if s == 0:
                    pe.wait_ge(d_mrow, 16 * (w + 1))
                    pe.wait_ge(s_kh, w + 1)
                pe.wait_ge(s_ex, NS * w + s + 1)
                dst = bank[:, lo - CW * c:CW]
                js = slice(P * j, P * j + P)
                mm(dst, ks[b][:, js], qs[b][:, lo:z], start=True, stop=False)
                last = mm(dst, kh[b][:, js], ql[b][:, lo:z], start=False, stop=j < TPC * c)
                if j >= TPC * c:
                    last = mm(bank[:, lo - CW * c:lo - CW * c + P], identb[:], mask_t[:], start=False, stop=True)
                last.then_inc(s_st, 1)

            def weigh(w, b, s):
                c, j = STEPS[s]
                o = (c + NC * b) % 2
                lo = max(P * j, CW * c) - CW * c
                pe.wait_ge(s_ex, NS * w + s + 4)
                if s == 0:
                    pe.wait_ge(s_vs, w + 1)
                if j == 0:
                    pe.wait_ge(s_of, NC * w + c + 1)
                mm(ps[0:D + 1, 6 + o, lo:CW], vs[b][:, j, :], pt[:, s % 6, lo:CW], start=j == 0,
                   stop=s == LAST[c]).then_inc(s_pv, 1)

            def turn_back(w, b, c):
                o = (c + NC * b) % 2
                pe.wait_ge(s_of, NC * w + c + 3)
                pe.wait_ge(s_nf, NC * w + c + 1)
                for r in range(TPC):
                    last = nc.tensor.transpose(ps[:, 3, (D + 1) * r:(D + 1) * (r + 1)], ot[:, o, P * r:P * r + P],
                                               ident[0:D + 1, 0:D + 1])
                last.then_inc(s_to, 1)

            def slot(w, b, first=False, follow=True):
                for s in range(NS):
                    scores(w, b, s)
                    if follow:
                        for k in PROJECT_AT.get(s, ()):
                            project(w + 1, 1 - b, k)
                        for k in MAX_AT.get(s, ()):
                            scores_for_max(w + 1, 1 - b, k)
                        if s == TURN_MAX_AT:
                            turn_max(w + 1, 1 - b)
                    if s >= LAG:
                        weigh(w, b, s - LAG)
                    elif not first:
                        weigh(w - 1, 1 - b, s - LAG + NS)
                    for c in range(NC):
                        if BACK_AT[c] == s:
                            turn_back(w, b, c)
                        if BACK_AT[c] == s + NS and not first:
                            turn_back(w - 1, 1 - b, c)

            head_of = [0]
            pe.wait_ge(s_vx, G)
            pe.wait_ge(s_split2, 1)
            for k in range(2 * NC):
                project(0, 0, k)
            for k in range(NM):
                scores_for_max(0, 0, k)
            turn_max(0, 0)
            slot(0, 0, first=True)
            with pe.Fori(0, NH - 1) as i:
                head_of[0] = i + 1
                slot(2 * i + 1, 1)
                slot(2 * i + 2, 0)
            slot(2 * NH - 1, 1, follow=False)
            for s in range(NS - LAG, NS):
                weigh(2 * NH - 1, 1, s)
            turn_back(2 * NH - 1, 1, NC - 1)

            turn(2)
            turn(3)
            pe.wait_ge(d_late, 16 * 6)
            for b in range(B):
                def item(k):
                    if 12 * b + k >= 4:
                        ob, ok = divmod(12 * b + k - 4, 12)
                        if ok < NC:
                            pe.wait_ge(s_rd, 2 * NC * ob + ok + 1)
                        elif ok < 3 * NC:
                            pe.wait_ge(s_gelu, 2 * NC * ob + ok - NC + 1)
                        else:
                            pe.wait_ge(s_rd, 2 * NC * ob + ok - 2 * NC + 1)
                    return ps[:, 3 + k % 4, 0:CW]

                pe.wait_ge(s_us, NC * (3 + b))
                for k in range(NC):
                    cs = slice(b * SP_ + CW * k, b * SP_ + CW * k + CW)
                    split2(item(k), WRH[:], US[:, cs], WRL[:], US[0:D, cs], True, True).then_inc(s_r, 1)
                for m in range(2):
                    for c in range(NC):
                        cs = slice(b * SP_ + CW * c, b * SP_ + CW * c + CW)
                        ws = slice(O_W1 + P * m, O_W1 + P * m + P)
                        split2(item(NC + NC * m + c), WH[:, ws], US[:, cs], WL[:, ws], US[0:D, cs],
                               True, True).then_inc(s_r, 1)
                for c in range(NC):
                    bank = item(3 * NC + c)
                    pe.wait_ge(s_gelu, 6 * b + NC + c + 1)
                    for t in range(TPC):
                        for m in range(2):
                            ts = slice(P * (TPC * c + t), P * (TPC * c + t) + P)
                            last = mm(bank[:, D * t:D * t + D], hT[:, m, ts], w2[:, m, :],
                                      start=(t == 0 and m == 0), stop=(t == TPC - 1 and m == 1), skip_group_check=True)
                    last.then_inc(s_r, 1)

            pe.wait_ge(s_ush, B)
            pe.wait_ge(s_toep, 1)
            for ch in range(D):
                k, r = divmod(ch, 14)
                if r == 0 and k >= 3:
                    pe.wait_ge(s_rd, 4 * NC)
                last = mm(ps[0:D, k, 2 * G * r:2 * G * (r + 1)], toep[:, ch, :], UU[:, :, :, ch],
                          start=r == 0, stop=(r == 13 or ch == D - 1), skip_group_check=True)
                if r == 13 or ch == D - 1:
                    last.then_inc(s_cv, 1)

            pe.wait_ge(s_cvf, 5)
            turn(4)
            turn(5)
            pe.wait_ge(s_us, NC * 6)
            for g in range(G):
                cs = slice(P * g, P * g + P)
                last = split2(ps[:, 3, NE * g:NE * g + NE], US[:, cs], WH[:, O_G:O_G + NE],
                              US[0:D, cs], WL[:, O_G:O_G + NE], g == 0, g == G - 1)
            last.then_inc(s_g, 1)
            pe.wait_ge(s_b2, 3)
            pe.sem_inc(s_hu, NE)
            relu_done = (s_ha, s_hd)

            def hidden(t, e):
                tokens = bass.ds(t * 256, 256)
                pe.wait_ge(relu_done[e % 2], (NE // 2) * t + e // 2 + 1)
                for m in range(2):
                    ws = slice(O_E + HID * e + P * m, O_E + HID * e + P * m + P)
                    last = split2(ps[:, 4 + e % 4, 256 * m:256 * m + 256], WH[:, ws], US[:, tokens], WL[:, ws],
                                  US[0:D, tokens], m == 0, m == 1)
                last.then_inc(s_hh, 1)

            def down(t, e, y):
                pe.wait_ge(relu_done[e % 2], (NE // 2) * t + e // 2 + 3)
                for r in range(2):
                    for m in range(2):
                        last = mm(ps[:, 2 * y + r, D * e:D * e + D], eh[:, e, m, P * r:P * r + P], ew2[:, m, e, :],
                                  start=False, stop=(e == NE - 1 and m == 1), skip_group_check=True)
                last.then_inc(s_hu, 1)

            def bias_rows(t, y):
                pe.wait_ge(s_yf, t + 1)
                for r in range(2):
                    mm(ps[:, 2 * y + r, :], onesb[:], b2p[:], start=True, stop=False, skip_group_check=True)

            def chunk(t, y):
                for e in range(NE):
                    hidden(t, e)
                bias_rows(t, y)
                for e in range(NE):
                    down(t, e, y)

            chunk(0, 0)
            with pe.Fori(0, G // 4) as i:
                chunk(2 * i + 1, 1)
                chunk(2 * i + 2, 0)

        @block.vector
        def _(dve):
            n = [0]
            tt, ts, stt = nc.vector.tensor_tensor, nc.vector.tensor_scalar, nc.vector.scalar_tensor_tensor

            def link(instruction):
                n[0] += 1
                instruction.then_inc(s_dve, 1)
                dve.wait_ge(s_dve, n[0])

            def wide(col, k):
                return col.unsqueeze(2).broadcast_to([P, k, D])

            def split_weights(a, z):
                link(nc.vector.tensor_copy(WH[:, a:z], WR[:, a:z]))
                link(tt(WL[:, a:z], WR[0:D, a:z], WH[0:D, a:z], ALU.subtract))

            dve.wait_ge(d_wtok, 32)
            split_weights(0, O_Q)
            dve.wait_ge(d_x, 32)
            nc.vector.tensor_copy(XS[:], XR[:]).then_inc(s_split1, 1)
            dve.wait_ge(s_split1, 1)
            tt(XS[D:P, :], XR[D:P, :], XS[D:P, :], ALU.subtract).then_inc(s_split1, 1)
            dve.wait_ge(d_rows, 16)
            dve.wait_ge(d_cols, 16)
            for b in range(B):
                for k in range(4):
                    dve.wait_ge(s_tround, 4 * b + k + 1)
                    cs = slice(512 * (k % 2), 512 * (k % 2) + 512)
                    if k < 2:
                        stt(tql[:, cs], ps[0:D, k, :], cols[0:D, C_TBQ:C_TBQ + 1], tq[0:D, cs], ALU.add,
                            ALU.subtract).then_inc(s_tlow, 1)
                    else:
                        stt(tk[D:P, cs], ps[D:P, k, :], cols[D:P, C_TBK:C_TBK + 1], tk[D:P, cs], ALU.add,
                            ALU.subtract).then_inc(s_tlow, 1)
                dve.wait_ge(s_tproj, 5 * (b + 1))
                tt(tv[:], ps[:, 4, :].rearrange("p (t d) -> p t d", d=D),
                   rows[:, R_TBV:R_TBV + D].unsqueeze(1).broadcast_to([P, TT, D]), ALU.add).then_inc(s_tv, 1)
                for k in range(16):
                    m = 16 * b + k
                    s, half = k // 2, k % 2
                    if b == 0 and half == 0:
                        dve.wait_ge(d_gam[s], 16)
                    dve.wait_ge(s_tsc, m + 1)
                    if m >= 4:
                        dve.wait_ge(s_tpv, m - 3)
                    tt(ptt[:, m % 4, :], ps[:, 5 + m % 3, :], gam[:, s, 512 * half:512 * half + 512],
                       ALU.mult).then_inc(s_tpt, 1)
                dve.wait_ge(s_ty, b + 1)
                hb, yb = h[:, b * NT:b * NT + TT, :], sq[:, 0:TT, :]
                link(tt(yb, ps[:, 4, :].rearrange("p (t d) -> p t d", d=D),
                        rows[:, R_TBO:R_TBO + D].unsqueeze(1).broadcast_to([P, TT, D]), ALU.add))
                link(ts(hb, yb, 0.0, cols[:, C_A:C_A + 1], ALU.min, ALU.mult))
                stt(hb, yb, 0.0, hb, ALU.max, ALU.add).then_inc(s_th, 1)
                dve.wait_ge(s_th, b + 1)

            def layernorm(k):
                g0, g1 = ln_range(k)
                hb, ub, sb_ = h[:, g0:g1, :], UU[:, 1, g0:g1, :], sq[:, g0:g1, :]
                st = [stat[:, r, g0:g1] for r in range(10)]
                link(nc.vector.tensor_reduce(st[0], hb, AX.X, ALU.add))
                link(ts(st[1], st[0], -1.0 / D, None, ALU.mult))
                link(tt(ub, hb, wide(st[1], NT), ALU.add))
                link(tt(sb_, ub, ub, ALU.mult))
                link(nc.vector.tensor_reduce(st[0], sb_, AX.X, ALU.add))
                ts(st[2], st[0], 1.0 / D, EPS, ALU.mult, ALU.add).then_inc(s_var, 1)
                dve.wait_ge(s_var, k + 1)
                dve.wait_ge(s_sd, k + 1)
                link(nc.vector.reciprocal(st[6], st[3]))
                link(tt(st[7], st[2], st[6], ALU.mult))
                link(tt(st[8], st[7], st[3], ALU.add))
                link(nc.vector.reciprocal(st[6], st[8]))
                stt(ub, ub, 2.0, wide(st[6], NT), ALU.mult, ALU.mult).then_inc(s_u, 1)
                dve.wait_ge(s_u, k + 1)

            def low(k):
                for c in range(NC):
                    m, b = NC * k + c, k % 2
                    cs = slice(b * SP_ + CW * c, b * SP_ + CW * c + CW)
                    dve.wait_ge(s_uhi, m + 1)
                    tt(US[D:P, cs], ps[0:D, c, 0:CW], US[0:D, cs], ALU.subtract).then_inc(s_us, 1)

            dve.wait_ge(s_const, 2)
            dve.wait_ge(d_wv, 64)
            nc.vector.tensor_copy(bvrep[:], bvT[:].unsqueeze(2).broadcast_to([D, NH, P])).then_inc(s_bvr, 1)
            dve.wait_ge(d_w, 32)
            link(ts(wr_rep[:], ones[:], WR[:, O_WR:O_WR + 1], None, ALU.mult))
            link(nc.vector.tensor_copy(WRH[:], wr_rep[:]))
            link(tt(WRL[:], wr_rep[0:D, :], WRH[0:D, :], ALU.subtract))
            dve.wait_ge(s_wp, 1)
            link(nc.vector.tensor_copy(WPH[:], ps[:, 5, :]))
            link(nc.vector.tensor_copy(bp[:], ps[:, 6, :].rearrange("p (h d) -> p h d", d=D)))
            tt(WPL[:], ps[0:D, 5, :], WPH[0:D, :], ALU.subtract).then_inc(s_wps, 1)
            dve.wait_ge(s_wps, 1)
            link(nc.vector.memset(acc[:], 0.0))
            link(nc.vector.memset(mpart[:], -3e38))
            for b in range(B):
                link(nc.vector.memset(UU[0:D, 0, b * NT, :], 0.0))
            dve.wait_ge(d_txt, 32)
            layernorm(0)
            layernorm(1)
            low(0)
            low(1)
            dve.wait_ge(s_split2, 1)
            for g in range(G):
                dve.wait_ge(s_v, g + 1)
                tt(VX[:, g // NT, g % NT, :, 0:D], ps[:, 3 + g % 4, :].rearrange("p (h d) -> p h d", d=D), bp[:],
                   ALU.add).then_inc(s_vx, 1)

            dve.sem_inc(s_yf, 2)
            dve.sem_inc(s_af, 2)
            dve.sem_inc(s_nf, 1)
            base, m = [0], [0]

            def chain(instruction):
                m[0] += 1
                instruction.then_inc(s_dvl, 1)
                dve.wait_ge(s_dvl, base[0] + m[0])

            def low_part(v, b, k):
                cs = slice(CW * (k % NC), CW * (k % NC) + CW)
                dve.wait_ge(s_ar, 2 * NC * v + k + 1)
                src = ps[:, 4 + k % 2, 0:CW]
                if k < NC:
                    ins_ = stt(ql[b][0:D, cs], src[0:D], head_col(C_BQ)[0:D], qs[b][0:D, cs], ALU.add, ALU.subtract)
                else:
                    ins_ = stt(ks[b][D:P, cs], src[D:P], head_col(C_BK)[D:P], ks[b][D:P, cs], ALU.add, ALU.subtract)
                ins_.then_inc(s_af, 1)

            def head_col(col):
                return cols[:, bass.ds(head_of[0] + col, 1)]

            def maximum(v, b, k):
                i, a, z = SMAX[k]
                dve.wait_ge(s_a, NA * v + 2 * NC + k + 1)
                nc.vector.tensor_reduce(mpart[:, b, i, a // 512:a // 512 + 1], ps[:, 4 + k % 2, 0:z - a], AX.X,
                                        ALU.max).then_inc(s_af, 1)

            def whole_maximum(v, b):
                dve.wait_ge(s_af, NA * v + NA + 1)
                chain(nc.vector.tensor_reduce(mneg[:, b], mpart[:, b], AX.X, ALU.max))
                ts(mneg[:, b], mneg[:, b], -1.0, None, ALU.mult).then_inc(s_mneg, 1)

            def take_row(v, b):
                dve.wait_ge(s_a, NA * v + NA)
                nc.vector.tensor_copy(mrow[b][:], ps[0:NT, 5, 0:P]).then_inc(s_af, 1)

            def output(w, b, c):
                dve.wait_ge(s_to, NC * w + c + 3)
                o = ps[:, 3, 0:TPC * (D + 1)].rearrange("p (r d) -> p r d", d=D + 1)
                chain(nc.vector.reciprocal(rden[:, c % 2], o[:, :, D]))
                tt(onrm[:, c % 2], o[:, :, 0:D], wide(rden[:, c % 2], TPC), ALU.mult).then_inc(s_nf, 1)
                dve.wait_ge(s_nf, NC * w + c + 2)
                ac = acc[:, b * NT + TPC * c:b * NT + TPC * c + TPC, :]
                chain(tt(ac, ac, onrm[:, c % 2], ALU.add))

            def slot(w, b, first=False, follow=True):
                for s in range(NS):
                    if follow:
                        for k in PROJECT_AT.get(s, ()):
                            low_part(w + 1, 1 - b, k)
                        for k in MAX_AT.get(s, ()):
                            maximum(w + 1, 1 - b, k)
                        if s == WHOLE_AT:
                            whole_maximum(w + 1, 1 - b)
                        if s == TURN_MAX_AT:
                            take_row(w + 1, 1 - b)
                    for c in range(NC):
                        if BACK_AT[c] == s:
                            output(w, b, c)
                        if BACK_AT[c] == s + NS and not first:
                            output(w - 1, 1 - b, c)

            head_of = [0]
            for k in range(2 * NC):
                low_part(0, 0, k)
            for k in range(NM):
                maximum(0, 0, k)
            whole_maximum(0, 0)
            take_row(0, 0)
            slot(0, 0, first=True)
            before_loop, per_slot = m[0], 1 + 2 * NC
            with dve.Fori(0, NH - 1) as i:
                head_of[0], base[0], m[0] = i + 1, i * (2 * per_slot) + before_loop, 0
                slot(2 * i + 1, 1)
                slot(2 * i + 2, 0)
                assert m[0] == 2 * per_slot
            base[0], m[0] = (NH - 1) * 2 * per_slot + before_loop, 0
            slot(2 * NH - 1, 1, follow=False)
            output(2 * NH - 1, 1, NC - 1)

            for b in range(B):
                g = slice(b * NT, b * NT + NT)
                link(nc.vector.memset(acc[0:1, b * NT, :], 0.0))
                link(tt(acc[:, g], acc[:, g], rows[:, R_BU:R_BU + D].unsqueeze(1).broadcast_to([P, NT, D]), ALU.add))
                link(tt(h[:, g], h[:, g], acc[:, g], ALU.add))

            layernorm(2)
            layernorm(3)
            low(2)
            low(3)
            link(nc.vector.memset(rank4[:], 0.0))
            for b in range(B):
                for k in range(NC):
                    dve.wait_ge(s_r, 12 * b + k + 1)
                    ts(wbc[:, b, CW * k:CW * k + CW], ps[:, 3 + k % 4, 0:CW], cols[:, C_BR:C_BR + 1], None,
                       ALU.add).then_inc(s_rd, 1)
                dve.wait_ge(s_rd, 2 * NC * b + NC)
                for t in range(NT):
                    w = wcol[:, b, t:t + 1]
                    dw = min(P, S - P * t)
                    dg = wbc[:, b, P * t:P * t + dw]
                    link(stt(scr[:, 0:P], wbc[:, b, P * t:P * t + P], 1.0, ident[:], ALU.mult, ALU.mult, accum_out=w))
                    if t:
                        link(ts(scr[:, 0:P * t], wbc[:, b, 0:P * t], w, 0.0, ALU.is_ge, ALU.add,
                                accum_out=rank4[:, b, t, 0:1]))
                    if t < NT - 1:
                        link(ts(scr[:, 0:S - P * t - P], wbc[:, b, P * t + P:S], w, 0.0, ALU.is_gt, ALU.add,
                                accum_out=rank4[:, b, t, 1:2]))
                    link(stt(scr[:, 0:dw], dg, w, before[:, 0:dw], ALU.is_ge, ALU.mult, accum_out=rank4[:, b, t, 2:3]))
                    link(stt(scr[:, 0:dw], dg, w, after[:, 0:dw], ALU.is_gt, ALU.mult, accum_out=rank4[:, b, t, 3:4]))
                link(nc.vector.tensor_reduce(rank[:, b], rank4[:, b], AX.X, ALU.add))
                link(stt(sel[:, b], rank[:, b], float(KK), wcol[:, b], ALU.is_lt, ALU.mult))
                g = slice(b * NT, b * NT + NT)
                link(tt(h[:, g], h[:, g], UU[:, 1, g], ALU.add))
                for c in range(NC):
                    dve.wait_ge(s_r, 12 * b + 3 * NC + c + 1)
                    gc = slice(b * NT + TPC * c, b * NT + TPC * c + TPC)
                    tt(sq[:, gc], ps[:, 3 + (3 * NC + c) % 4, 0:TPC * D].rearrange("p (t d) -> p t d", d=D),
                       rows[:, R_B2:R_B2 + D].unsqueeze(1).broadcast_to([P, TPC, D]), ALU.add).then_inc(s_rd, 1)
                dve.wait_ge(s_rd, 2 * NC * (b + 1))
                link(tt(sq[:, g], sq[:, g], wide(sel[:, b], NT), ALU.mult))
                link(tt(h[:, g], h[:, g], sq[:, g], ALU.add))

            for b in range(B):
                layernorm(4 + b)
                g0, g1 = ln_range(b)
                link(nc.vector.tensor_copy(UU[0:D, 0, g0 + 1:g1, :], UU[D:P, 1, g0:g1 - 1, :]))
                nc.vector.tensor_copy(UU[D:P, 0, g0:g1, :], UU[0:D, 1, g0:g1, :]).then_inc(s_ush, 1)
            for k in range(5):
                c0, c1 = 14 * k, min(14 * k + 14, D)
                dve.wait_ge(s_cv, k + 1)
                y = ps[0:D, k, 0:2 * G * (c1 - c0)].rearrange("p (c g) -> p g c", g=2 * G)
                link(tt(h[0:D, :, c0:c1], y[:, 0:G, :], h[0:D, :, c0:c1], ALU.add))
                tt(h[D:P, :, c0:c1], y[:, G:2 * G, :], h[D:P, :, c0:c1], ALU.add).then_inc(s_cvf, 1)
            dve.wait_ge(s_cvf, 5)

            layernorm(6)
            layernorm(7)
            low(4)
            low(5)
            dve.wait_ge(s_g, 1)
            tt(gate[:], ps[:, 3, 0:G * NE].rearrange("p (g e) -> p g e", e=NE),
               rows[:, R_BG:R_BG + NE].unsqueeze(1).broadcast_to([P, G, NE]), ALU.add).then_inc(s_gf, 1)
            dve.wait_ge(s_gf, 1)
            full = [P, G, NE, NE]
            gf, ge = gate[:].unsqueeze(2).broadcast_to(full), gate[:].unsqueeze(3).broadcast_to(full)
            narrow = lambda r: stat[:, r, :].unsqueeze(2).broadcast_to([P, G, NE])
            link(tt(gt[:], gf, ge, ALU.is_gt))
            link(tt(eq[:], gf, ge, ALU.is_equal))
            link(tt(eq[:], eq[:], ebefore[:].unsqueeze(1).broadcast_to(full), ALU.mult))
            link(tt(gt[:], gt[:], eq[:], ALU.add))
            link(nc.vector.tensor_reduce(erank[:], gt[:], AX.X, ALU.add))
            link(ts(is0[:], erank[:], 0.0, None, ALU.is_equal))
            link(ts(is1[:], erank[:], 1.0, None, ALU.is_equal))
            link(tt(comb[:], is1[:], gate[:], ALU.mult))
            link(nc.vector.tensor_reduce(stat[:, 0, :], comb[:], AX.X, ALU.add))
            link(nc.vector.tensor_reduce(stat[:, 1, :], gate[:], AX.X, ALU.max))
            tt(stat[:, 4, :], stat[:, 0, :], stat[:, 1, :], ALU.subtract).then_inc(s_d, 1)
            dve.wait_ge(s_ed, 1)
            link(ts(stat[:, 6, :], stat[:, 5, :], 1.0, None, ALU.add))
            link(nc.vector.reciprocal(stat[:, 7, :], stat[:, 6, :]))
            link(tt(stat[:, 8, :], stat[:, 7, :], stat[:, 5, :], ALU.mult))
            link(tt(comb[:], is0[:], narrow(7), ALU.mult))
            link(tt(is1[:], is1[:], narrow(8), ALU.mult))
            link(tt(comb[:], comb[:], is1[:], ALU.add))
            def relu(t, e):
                dve.wait_ge(s_hh, NE * t + e + 1)
                dve.wait_ge(s_hu, NE * t + e + 1)
                for k in range(2):
                    ins_ = ts(eh[:, e, k, :], ps[:, 4 + e % 4, 256 * k:256 * k + 256],
                              cols[:, C_EB1 + 2 * e + k:C_EB1 + 2 * e + k + 1], 0.0, ALU.add, ALU.max)
                ins_.then_inc(s_hd, 1)

            def combine(t, y):
                dve.wait_ge(s_hu, NE * t + 2 * NE)
                for r in range(2):
                    ins_ = tt(yw[:, r], ps[:, 2 * y + r, :].rearrange("p (e d) -> p e d", d=D),
                              comb[:, bass.ds(2 * t + r, 1), :].rearrange("p o e -> p (o e)").unsqueeze(2)
                              .broadcast_to([P, NE, D]), ALU.mult)
                ins_.then_inc(s_yf, 1)
                dve.wait_ge(s_yf, t + 3)
                nc.vector.tensor_reduce(ysum[:], yw[:].rearrange("p r e d -> p r d e"), AX.X,
                                        ALU.add).then_inc(s_dvm, 1)
                dve.wait_ge(s_dvm, t + 1)
                hb = h[:, bass.ds(2 * t, 2), :]
                tt(hb, hb, ysum[:], ALU.add).then_inc(s_fin, 1)
                dve.wait_ge(s_fin, t + 1)

            with dve.Fori(0, G // 4) as i:
                for y in range(2):
                    for e in range(1, NE, 2):
                        relu(2 * i + y + 1, e)
                    combine(2 * i + y, y)
            combine(G // 2 - 1, 0)


def kernel(**inputs):
    import numpy as np
    import concourse.bacc as bacc
    from concourse.bass_utils import run_bass_kernel_spmd

    a = {k: np.asarray(v) for k, v in inputs.items()}
    cat = np.concatenate
    t_q, t_k = a["L0_tok_Wq"], a["L0_tok_Wk"]
    column = lambda v: v.reshape(-1, D).T
    twice = lambda m: cat([m, m], axis=0)
    laid = {
        "xT": a["x"].reshape(B, T, D).transpose(2, 0, 1).reshape(D, B * T),
        "txt": a["txt"],
        "gammaT": a["L0_tok_d_gamma_batched"].T,
        "w64": cat([t_q, t_q, t_k, t_k, a["L0_tok_Wv"], a["L0_attn_Wq"], a["L0_attn_Wk"], a["L0_ffn_w1"],
                    a["L1_ffn_Wg"].T, a["L1_ffn_W1"].transpose(2, 0, 1).reshape(D, NE * HID), a["L0_ffn_wr"]], axis=1),
        "cols": cat([twice(column(a["L0_tok_bq"])), twice(column(a["L0_tok_bk"])),
                     twice(column(a["L0_attn_bq"])), twice(column(a["L0_attn_bk"])),
                     a["L0_ffn_b1"].reshape(2, P).T, a["L1_ffn_b1"].reshape(2 * NE, P).T,
                     np.tile(a["L0_tok_prelu_a"].reshape(1, 1), (P, 1)),
                     np.tile(a["L0_ffn_br"].reshape(1, 1), (P, 1))], axis=1),
        "rows": cat([a["L0_tok_bv"], a["L0_tok_bo"], a["L0_attn_bu"], a["L0_ffn_b2"], a["L1_ffn_bg"]]).reshape(1, NROW),
        "wvT": a["L0_attn_Wv"].reshape(D, NH, D).transpose(2, 1, 0),
        "bvT": column(a["L0_attn_bv"]),
        "wu": a["L0_attn_Wu"].reshape(NH, D, D).transpose(1, 0, 2),
        "two": a["L0_tok_Wo"],
        "w2": a["L0_ffn_w2"].reshape(2, P, D).transpose(1, 0, 2),
        "ew2": a["L1_ffn_W2"].transpose(2, 0, 1).reshape(2, P, NE, D).transpose(1, 0, 2, 3),
        "eb2": a["L1_ffn_b2"].reshape(1, NE * D),
        "cpad": np.pad(a["L1_attn_c"][0][:, ::-1], ((0, 0), (D, D))).reshape(-1),
    }
    laid = {k: np.ascontiguousarray(v) for k, v in laid.items()}
    nc = bacc.Bacc("TRN2", target_bir_lowering=False, num_devices=1)
    ins = {k: nc.dram_tensor(f"in_{k}", v.shape, F32, kind="ExternalInput").ap() for k, v in laid.items()}
    out = nc.dram_tensor("out", (B, S, D), F32, kind="ExternalOutput").ap()
    early_fusion(nc, ins, out)
    r = run_bass_kernel_spmd(nc, [{f"in_{k}": v for k, v in laid.items()}], core_ids=[0])
    return r.results[0]["out"]
```

```python
from contextlib import ExitStack

import concourse.bass as bass
from concourse import mybir

F32 = mybir.dt.float32
F32R = mybir.dt.float32r
BF16 = mybir.dt.bfloat16
ALU = mybir.AluOpType
ACT = mybir.ActivationFunctionType
AX = mybir.AxisListType

P = 128
D = 64
B = 2
T = 1024
TXT = 77
S = T + TXT
NT = -(-S // P)
SP_ = NT * P
G = B * NT
NH = 8
HID = 256
NE = 8
KK = max(1, int(0.5 * S)) - 1
EPS = 1e-5
NEG = -1e30
CW = 384
NC = SP_ // CW
TPC = CW // P
TT = T // P

O_TQ, O_TK, O_TV = 0, 128, 256
O_Q, O_K = 320, 832
O_W1 = 1344
O_G = 1600
O_E = 1608
O_WR = O_E + NE * HID
NW = O_WR + 1
C_TBQ, C_TBK, C_BQ, C_BK, C_B1, C_EB1, C_A, C_BR = 0, 1, 2, 10, 18, 20, 36, 37
NCOL = 38
R_TBV, R_TBO, R_BU, R_B2, R_BG = 0, 64, 128, 192, 256
NROW = 264

STEPS = [(c, j) for c in range(NC) for j in range(TPC * (c + 1))]
NS = len(STEPS)
SMAX = [(i, a, min(a + 512, P * (i + 1))) for i in range(NT) for a in range(0, P * (i + 1), 512)]
NM = len(SMAX)
NA = 2 * NC + NM + 1
LAG = 2
PROJECT_AT = {0: (0, 1), 1: (2,), 2: (3,), 3: (4,), 4: (5,)}
MAX_AT = {6 + k // 2: tuple(x for x in (k, k + 1) if x < NM) for k in range(0, NM, 2)}
WHOLE_AT, TURN_MAX_AT = 14, 15
LAST = [STEPS.index((c, TPC * (c + 1) - 1)) for c in range(NC)]
COPY_AT = [x + LAG for x in LAST]
BACK_AT = [x + LAG + 2 for x in LAST]
V_BANKS = (3, 6, 7)
GATE_BANKS = (3, 0, 1, 2, 7)


def early_fusion(nc, ins, out):
    ctx = ExitStack()
    with ctx:
        def sb(name, shape, dt=F32, where=None):
            return (where or ctx).enter_context(nc.sbuf_tensor(name, shape, dt))

        def sem(name):
            return ctx.enter_context(nc.semaphore(name))

        WH = sb("w_hi", [P, NW], F32R)
        WL = sb("w_lo", [D, NW], F32R)
        WRH = sb("wr_hi", [P, P], F32R)
        WRL = sb("wr_lo", [D, P], F32R)
        cols = sb("cols", [P, NCOL])
        rows = sb("rows", [P, NROW])
        ident = sb("ident", [P, P])
        ones = sb("ones", [P, P])
        identb = sb("identb", [P, P], BF16)
        zerob = sb("zerob", [P, P], BF16)
        mask_s = sb("mask_s", [P, P], BF16)
        mask_t = sb("mask_t", [P, P], BF16)
        before = sb("before", [P, P])
        after = sb("after", [P, P])
        desc = sb("desc", [P, NE])
        h = sb("h", [P, G, D])
        UU = sb("UU", [P, 2, G, D])
        sq = sb("sq", [P, G, D])
        cst = sb("cst", [P, D])
        alone = sb("alone", [1, B, D])
        US = sb("US", [P, B * SP_], F32R)
        stat = sb("stat", [P, 10, G])
        toep = sb("toep", [P, D, D])
        WPH = sb("WPH", [P, NH * D], F32R)
        WPL = sb("WPL", [D, NH * D], F32R)
        w2 = sb("w2", [P, 2, D])
        ew2 = sb("ew2", [P, 2, NE, D])
        b2raw = sb("b2raw", [65, NE * D])
        b2p = sb("b2p", [65, NE * D], BF16)
        onesb = sb("onesb", [P, P], BF16)
        bvT = sb("bvT", [D, NH])
        two = sb("two", [D, D])
        u = UU[:, 1]

        st1 = ExitStack()
        XR = sb("x_raw", [P, B * T], F32, st1)
        XS = sb("x_split", [P, B * T], F32R, st1)
        WR = sb("w_raw", [P, NW], F32, st1)
        wvT = sb("wvT", [D, NH, 2, D], F32, st1)
        bvrep = sb("bvrep", [D, NH, P], F32, st1)
        wu = sb("wu", [D, NH, D], F32, st1)
        wr_rep = sb("wr_rep", [P, P], F32, st1)
        gam = sb("gam", [P, TT, T], F32, st1)
        tq = sb("tq", [P, T], F32R, st1)
        tk = sb("tk", [P, T], F32R, st1)
        tql = sb("tql", [D, T], F32R, st1)
        tv = sb("tv", [P, TT, D], F32, st1)
        ptt = sb("ptt", [P, 4, 512], F32, st1)
        tret = sb("tret", [D, T], F32, st1)
        st1.close()

        st2 = ExitStack()
        VX = sb("VX", [P, B, NT, NH, D + 1], F32, st2)
        qs = [sb(f"qs{b}", [P, SP_], F32R, st2) for b in range(B)]
        ks = [sb(f"ks{b}", [P, SP_], F32R, st2) for b in range(B)]
        ql = [sb(f"ql{b}", [D + 1, SP_], F32R, st2) for b in range(B)]
        kh = [sb(f"kh{b}", [D + 1, SP_], F32R, st2) for b in range(B)]
        vs = [sb(f"vs{b}", [P, NT, D + 1], F32, st2) for b in range(B)]
        ot = sb("ot", [D + 1, 2, CW], F32, st2)
        pt = sb("pt", [P, 6, CW], F32, st2)
        wh4 = sb("wh4", [P, 2, 2, D], F32R, st2)
        wl4 = sb("wl4", [D, 2, 2, D], F32R, st2)
        mpart = sb("mpart", [P, B, NT, 3], F32, st2)
        mneg = sb("mneg", [P, B, NT], F32, st2)
        mrow = [sb(f"mrow{b}", [NT, P], F32R, st2) for b in range(B)]
        rden = sb("rden", [P, 2, TPC], F32, st2)
        onrm = sb("onrm", [P, 2, TPC, D], F32, st2)
        hank = sb("hank", [P, D, D], F32, st2)
        st2.close()

        st3 = ExitStack()
        hT = sb("hT", [P, 2, SP_], F32, st3)
        wbc = sb("wbc", [P, B, SP_], F32, st3)
        above = sb("above", [P, 3, SP_], BF16, st3)
        tie = sb("tie", [P, 3, P], BF16, st3)
        wcol = sb("wcol", [P, B, NT], F32, st3)
        sel = sb("sel", [P, B, NT], F32, st3)
        eh = sb("eh", [P, NE, 2, 256], F32, st3)
        gT = sb("gT", [NE, B * SP_], F32, st3)
        gate = sb("gate", [P, G, NE], F32, st3)
        eq = sb("eq", [P, G, NE], F32, st3)
        is0 = sb("is0", [P, G, NE], F32, st3)
        is1 = sb("is1", [P, G, NE], F32, st3)
        comb = sb("comb", [P, G, NE], F32, st3)
        yw = sb("yw", [P, 2, NE, D], F32, st3)
        ysum = sb("ysum", [P, 2, D], F32, st3)
        st3.close()

        ps = ctx.enter_context(nc.psum_tensor("ps", [P, 8, 512], F32))

        d_x, d_wtok, d_w, d_cols, d_rows, d_txt = (sem(n) for n in ("d_x", "d_wtok", "d_w", "d_cols", "d_rows", "d_txt"))
        d_gam = [sem(f"d_gam{s}") for s in range(TT)]
        d_wv, d_late, d_two, d_mrow, d_out = (sem(n) for n in ("d_wv", "d_late", "d_two", "d_mrow", "d_out"))
        s_const = sem("s_const")
        s_const_act = sem("s_const_act")
        s_split1 = sem("s_split1")
        s_split2 = sem("s_split2")
        s_tproj = sem("s_tproj")
        s_tround = sem("s_tround")
        s_tlow = sem("s_tlow")
        s_tv = sem("s_tv")
        s_tsc = sem("s_tsc")
        s_tpt = sem("s_tpt")
        s_tpv = sem("s_tpv")
        s_tret = sem("s_tret")
        s_ty = sem("s_ty")
        s_th = sem("s_th")
        s_cen = sem("s_cen")
        s_sq = sem("s_sq")
        s_var = sem("s_var")
        s_sd = sem("s_sd")
        s_u = sem("s_u")
        s_tr = sem("s_tr")
        s_uhi = sem("s_uhi")
        s_us = sem("s_us")
        s_wp = sem("s_wp")
        s_wph = sem("s_wph")
        s_wps = sem("s_wps")
        s_bvr = sem("s_bvr")
        s_cst = sem("s_cst")
        s_v = sem("s_v")
        s_vx = [sem("s_vx_act"), sem("s_vx_dve")]
        s_wsl = sem("s_wsl")
        s_a = sem("s_a")
        s_ar = sem("s_ar")
        s_af = sem("s_af")
        s_kh = sem("s_kh")
        s_mneg = sem("s_mneg")
        s_st = sem("s_st")
        s_vs = sem("s_vs")
        s_ex = sem("s_ex")
        s_pv = sem("s_pv")
        s_of = sem("s_of")
        s_to = sem("s_to")
        s_nf = sem("s_nf")
        s_h1 = sem("s_h1")
        s_r = sem("s_r")
        s_wb = sem("s_wb")
        s_gelu = sem("s_gelu")
        s_rd = sem("s_rd")
        s_wt = sem("s_wt")
        s_cmp = sem("s_cmp")
        s_rk = sem("s_rk")
        s_skip = sem("s_skip")
        s_cv = sem("s_cv")
        s_cvf = sem("s_cvf")
        s_ush = sem("s_ush")
        s_gt_mm = sem("s_gt_mm")
        s_gt = sem("s_gt")
        s_g = sem("s_g")
        s_gf = sem("s_gf")
        s_d = sem("s_d")
        s_ed = sem("s_ed")
        s_hh = sem("s_hh")
        s_ha = sem("s_ha")
        s_hd = sem("s_hd")
        s_hu = sem("s_hu")
        s_y = sem("s_y")
        s_yf = sem("s_yf")
        s_fin = sem("s_fin")
        s_toep = sem("s_toep")
        s_b2 = sem("s_b2")
        s_dve = sem("s_dve")
        s_dvl = sem("s_dvl")
        s_dvm = sem("s_dvm")
        s_pool = sem("s_pool")
        s_step = sem("s_step")

        block = ctx.enter_context(nc.Block())

        @block.sync
        def _(sp):
            for half in range(2):
                sp.dma_start(XR[64 * half:64 * half + 64, :], ins["xT"]).then_inc(d_x, 16)
                sp.dma_start(WR[64 * half:64 * half + 64, 0:O_Q], ins["w64"][:, 0:O_Q]).then_inc(d_wtok, 16)
            sp.dma_start(cols[:], ins["cols"]).then_inc(d_cols, 16)
            sp.dma_start(rows[:], ins["rows"].broadcast_to([P, NROW])).then_inc(d_rows, 16)
            for s in range(TT):
                sp.dma_start(gam[:, s, :], ins["gammaT"][P * s:P * s + P, :]).then_inc(d_gam[s], 16)
            sp.dma_start(two[:], ins["two"]).then_inc(d_two, 16)
            sp.wait_ge(s_const, 1)
            for b in range(B):
                sp.dma_start(h[0:TXT, b * NT + TT, :], ins["txt"][b]).then_inc(d_txt, 16)
            for half in range(2):
                sp.dma_start(WR[64 * half:64 * half + 64, O_Q:NW], ins["w64"][:, O_Q:NW]).then_inc(d_w, 16)
            for half in range(2):
                sp.dma_start(wvT[:, :, half, :], ins["wvT"]).then_inc(d_wv, 16)
            sp.dma_start(bvT[:], ins["bvT"]).then_inc(d_wv, 16)
            sp.dma_start(wu[:], ins["wu"]).then_inc(d_wv, 16)
            sp.dma_start(w2[:], ins["w2"]).then_inc(d_late, 16)
            sp.dma_start(ew2[:], ins["ew2"]).then_inc(d_late, 16)
            for k in range(3):
                sp.dma_start(b2raw[32 * k:32 * k + 1, :], ins["eb2"]).then_inc(d_late, 16)
            sp.wait_ge(s_th, B)
            sp.wait_ge(s_split2, 1)
            sp.wait_ge(s_wps, 2)
            sp.dma_start(hank[:], bass.AP(ins["cpad"].tensor, 0, [[1, P], [3 * D, D], [1, D]])).then_inc(d_late, 16)

            def put_mrow(v, b):
                sp.wait_ge(s_af, NA * (v + 1) + 2)
                sp.dma_start(ql[b][D:D + 1, :].bitcast(F32).rearrange("o (t p) -> o t p", p=P),
                             mrow[b][:].bitcast(F32)).then_inc(d_mrow, 16)

            put_mrow(0, 0)
            put_mrow(1, 1)
            with sp.Fori(0, NH - 1) as i:
                put_mrow(2 * i + 2, 0)
                put_mrow(2 * i + 3, 1)

            for b in range(B):
                sp.wait_ge(s_fin, -(-(b * NT + TT) // 2))
                sp.dma_start(out[b, 0:T, :].rearrange("(t p) d -> p t d", p=P),
                             h[:, b * NT:b * NT + TT, :]).then_inc(d_out, 16)
                sp.wait_ge(s_fin, -(-(b * NT + NT) // 2))
                sp.dma_start(out[b, T:S, :], h[0:TXT, b * NT + TT, :]).then_inc(d_out, 16)
            sp.wait_ge(d_out, 16 * 2 * B)

        @block.gpsimd
        def _(pool):
            n = [0]

            def link(instruction):
                n[0] += 1
                instruction.then_inc(s_pool, 1)
                pool.wait_ge(s_pool, n[0])

            nc.gpsimd.memset(h[:, TT:G:NT, :], 0.0).then_inc(s_const, 1)
            link(nc.gpsimd.memset(ones[:], 1.0))
            link(nc.gpsimd.memset(zerob[:], 0.0))
            link(nc.gpsimd.affine_select(out=ident[:], in_=ones[:], compare_op=ALU.is_equal, fill=0.0,
                                         base=0, pattern=[[-1, P]], channel_multiplier=1))
            link(nc.gpsimd.affine_select(out=mask_s[:], in_=zerob[:], compare_op=ALU.is_gt, fill=NEG,
                                         base=0, pattern=[[-1, P]], channel_multiplier=1))
            link(nc.gpsimd.affine_select(out=mask_t[:], in_=zerob[:], compare_op=ALU.is_gt, fill=NEG,
                                         base=0, pattern=[[1, P]], channel_multiplier=-1))
            link(nc.gpsimd.affine_select(out=before[:], in_=ones[:], compare_op=ALU.is_gt, fill=0.0,
                                         base=0, pattern=[[-1, P]], channel_multiplier=1))
            link(nc.gpsimd.affine_select(out=after[:], in_=ones[:], compare_op=ALU.is_gt, fill=0.0,
                                         base=0, pattern=[[1, P]], channel_multiplier=-1))
            for e in range(NE):
                nc.gpsimd.memset(desc[:, e:e + 1], float(NE - e))
            link(nc.gpsimd.tensor_copy(identb[:], ident[:]))
            link(nc.gpsimd.memset(onesb[:], 1.0))
            nc.gpsimd.memset(b2p[:], 0.0).then_inc(s_const, 1)
            pool.wait_ge(d_w, 32)
            pool.wait_ge(d_wv, 64)
            nc.gpsimd.tensor_copy(bvrep[:], bvT[:].unsqueeze(2).broadcast_to([D, NH, P])).then_inc(s_bvr, 1)
            link(nc.gpsimd.tensor_copy(WH[:, O_Q:O_WR], WR[:, O_Q:O_WR]))
            nc.gpsimd.tensor_tensor(WL[:, O_Q:O_WR], WR[0:D, O_Q:O_WR], WH[0:D, O_Q:O_WR],
                                    ALU.subtract).then_inc(s_split2, 1)
            pool.wait_ge(s_split2, 1)

            pool.wait_ge(s_th, B)
            pool.wait_ge(s_wps, 2)
            for b in range(B):
                link(nc.gpsimd.memset(kh[b][D:D + 1, :].bitcast(F32), 1.0))
            link(nc.gpsimd.memset(VX[:, :, :, :, D:D + 1], 1.0))

            def slices(hd, guard):
                if guard is not None:
                    pool.wait_ge(s_a, guard)
                    pool.sem_inc(s_step, 1)
                for k, off in enumerate((O_Q, O_K)):
                    nc.gpsimd.tensor_copy(wh4[:, k], WH[:, bass.ds(hd * D + off, D)].unsqueeze(1)
                                          .broadcast_to([P, 2, D])).then_inc(s_wsl, 1)
                    nc.gpsimd.tensor_copy(wl4[:, k], WL[:, bass.ds(hd * D + off, D)].unsqueeze(1)
                                          .broadcast_to([D, 2, D])).then_inc(s_wsl, 1)

            def copy_keys(v, b):
                pool.wait_ge(s_ar, 2 * NC * (v + 1))
                pool.sem_inc(s_step, 1)
                nc.gpsimd.tensor_copy(kh[b][0:D, :], ks[b][0:D, :]).then_inc(s_kh, 1)

            def copy_values(v, b):
                pool.wait_ge(s_pv, NS * (v - 1) + 6)
                pool.sem_inc(s_step, 1)
                nc.gpsimd.tensor_copy(vs[b][:], VX[:, b, :, bass.ds(head_of[0], 1), :]
                                      .rearrange("p t o d -> p t (o d)")).then_inc(s_vs, 1)

            head_of = [0]
            slices(0, None)
            pool.wait_ge(s_cen, B)
            for b in range(B):
                link(nc.gpsimd.tensor_tensor(alone[:, b], h[0:1, b * NT, :], rows[0:1, R_BU:R_BU + D], ALU.add))
            nc.gpsimd.tensor_tensor(h[:], h[:], cst[:].unsqueeze(1).broadcast_to([P, G, D]),
                                    ALU.add).then_inc(s_cst, 1)
            copy_keys(0, 0)
            for parity in range(2):
                pool.wait_ge(s_vx[parity], G // 2)
            for b in range(B):
                nc.gpsimd.tensor_copy(vs[b][:], VX[:, b, :, 0, :]).then_inc(s_vs, 1)
            copy_keys(1, 1)
            with pool.Fori(0, NH - 1) as i:
                head_of[0] = i + 1
                slices(i + 1, NA * (2 * i + 1) + 2 * NC)
                copy_values(2 * i + 2, 0)
                copy_keys(2 * i + 2, 0)
                copy_values(2 * i + 3, 1)
                copy_keys(2 * i + 3, 1)

            for b in range(B):
                pool.wait_ge(s_u, B + b + 1)
                g = slice(b * NT, b * NT + NT)
                nc.gpsimd.tensor_tensor(h[:, g], h[:, g], u[:, g], ALU.add).then_inc(s_skip, 1)

            pool.wait_ge(d_late, 16 * 6)
            nc.gpsimd.tensor_copy(toep[:], hank[:, :, ::-1]).then_inc(s_toep, 1)
            pool.wait_ge(s_toep, 1)
            for k in range(3):
                r = slice(32 * k, 32 * k + 1)
                for _ in range(k):
                    link(nc.gpsimd.tensor_copy(b2p[r], b2raw[r]))
                    link(nc.gpsimd.tensor_tensor(b2raw[r], b2raw[r], b2p[r], ALU.subtract))
                nc.gpsimd.tensor_copy(b2p[r], b2raw[r]).then_inc(s_b2, 1)
                pool.wait_ge(s_b2, k + 1)

        @block.scalar
        def _(act):
            act.wait_ge(d_cols, 16)
            for b in range(B):
                for k in range(4):
                    act.wait_ge(s_tproj, 5 * b + k + 1)
                    dst = (tq if k < 2 else tk)[:, 512 * (k % 2):512 * (k % 2) + 512]
                    bias = cols[:, C_TBQ:C_TBQ + 1] if k < 2 else cols[:, C_TBK:C_TBK + 1]
                    nc.scalar.activation(dst, ps[:, k, :], ACT.Identity, bias=bias).then_inc(s_tround, 1)
                act.wait_ge(s_tpv, 16 * (b + 1))
                for k in range(2):
                    nc.scalar.activation(tret[:, 512 * k:512 * k + 512], ps[0:D, k, :], ACT.Copy).then_inc(s_tret, 1)
                if b == 0:
                    act.wait_ge(s_wp, 1)
                    nc.scalar.activation(WPH[:], ps[:, 5, :], ACT.Copy).then_inc(s_wph, 1)

            def squares_and_root(k):
                for b in range(B):
                    act.wait_ge(s_cen, B * k + b + 1)
                    g = slice(b * NT, b * NT + NT)
                    nc.scalar.activation(sq[:, g], u[:, g], ACT.Square).then_inc(s_sq, 1)
                act.wait_ge(s_var, k + 1)
                nc.scalar.activation(stat[:, 3], stat[:, 2], ACT.Sqrt).then_inc(s_sd, 1)

            def high(k):
                for c in range(NC):
                    b, m = k % 2, NC * k + c
                    act.wait_ge(s_tr, m + 1)
                    nc.scalar.activation(US[0:D, b * SP_ + CW * c:b * SP_ + CW * c + CW], ps[0:D, c, 0:CW],
                                         ACT.Copy).then_inc(s_uhi, 1)

            squares_and_root(0)
            high(0)
            high(1)

            def rounding(v, b, k):
                act.wait_ge(s_a, NA * v + k + 1)
                act.sem_inc(s_step, 1)
                c = k % NC
                dst = (qs if k < NC else ks)[b][:, CW * c:CW * c + CW]
                col = (C_BQ if k < NC else C_BK) + head_of[0]
                nc.scalar.activation(dst, ps[:, 4 + k % 2, 0:CW], ACT.Identity,
                                     bias=cols[:, bass.ds(col, 1)]).then_inc(s_ar, 1)

            def exp(w, s):
                c, j = STEPS[s]
                lo = max(P * j, CW * c) - CW * c
                act.wait_ge(s_st, NS * w + s + 1)
                act.wait_ge(s_pv, NS * w + s + 1)
                nc.scalar.activation(pt[:, s % 6, lo:CW], ps[:, s % 3, lo:CW],
                                     ACT.Exp, scale=D ** -0.5).then_inc(s_ex, 1)

            def copy_output(w, b, c):
                o = (c + NC * b) % 2
                act.wait_ge(s_pv, NS * w + LAST[c] + 1 + 6)
                act.wait_ge(s_to, NC * w + c + 1)
                nc.scalar.activation(ot[:, o, :], ps[0:D + 1, 6 + o, 0:CW], ACT.Copy).then_inc(s_of, 1)

            def slot(w, b, first=False, follow=True):
                for s in range(NS):
                    if follow:
                        for k in PROJECT_AT.get(s, ()):
                            rounding(w + 1, 1 - b, k)
                    exp(w, s)
                    for c in range(NC):
                        if COPY_AT[c] == s:
                            copy_output(w, b, c)
                        if COPY_AT[c] == s + NS and not first:
                            copy_output(w - 1, 1 - b, c)

            head_of = [0]
            act.sem_inc(s_ex, 3)
            act.sem_inc(s_of, 2)
            for k in range(G):
                if k < 2 * NC:
                    rounding(0, 0, k)
                if k % 2 == 0:
                    act.wait_ge(s_v, k + 1)
                    nc.scalar.activation(VX[:, k // NT, k % NT, :, 0:D], ps[:, V_BANKS[k % 3], :]
                                         .rearrange("p (h d) -> p h d", d=D), ACT.Copy).then_inc(s_vx[0], 1)
            slot(0, 0, first=True)
            with act.Fori(0, NH - 1) as i:
                head_of[0] = i + 1
                slot(2 * i + 1, 1)
                slot(2 * i + 2, 0)
            slot(2 * NH - 1, 1, follow=False)
            copy_output(2 * NH - 1, 1, NC - 1)

            squares_and_root(1)
            for b in range(B):
                high(2 + b)
            for k in range(B * NC):
                act.wait_ge(s_r, k + 1)
                nc.scalar.activation(wbc[:, k // NC, CW * (k % NC):CW * (k % NC) + CW], ps[:, 3 + k % 4, 0:CW],
                                     ACT.Identity, bias=cols[:, C_BR:C_BR + 1]).then_inc(s_wb, 1)
            for b in range(B):
                for k in range(2 * NC):
                    m, c = divmod(k, NC)
                    item = B * NC + 3 * NC * b + k
                    act.wait_ge(s_r, item + 1)
                    nc.scalar.activation(hT[:, m, CW * c:CW * c + CW], ps[:, 3 + item % 4, 0:CW],
                                         ACT.Gelu_apprx_tanh,
                                         bias=cols[:, C_B1 + m:C_B1 + m + 1]).then_inc(s_gelu, 1)
            squares_and_root(2)
            squares_and_root(3)
            act.sem_inc(s_ha, 2)
            act.sem_inc(s_hd, 2)
            for b in range(B):
                high(4 + b)
            for k, bank in enumerate(GATE_BANKS):
                act.wait_ge(s_gt_mm, k + 1)
                cs = slice(512 * k, min(512 * k + 512, B * SP_))
                nc.scalar.activation(gT[:, cs], ps[0:NE, bank, 0:cs.stop - cs.start], ACT.Copy).then_inc(s_gt, 1)

            def relu(t, e):
                act.wait_ge(s_hh, NE * t + e + 1)
                act.wait_ge(s_hu, NE * t + e + 1)
                for m in range(2):
                    ins_ = nc.scalar.activation(eh[:, e, m, :], ps[:, 4 + e % 4, 256 * m:256 * m + 256], ACT.Relu,
                                                bias=cols[:, C_EB1 + 2 * e + m:C_EB1 + 2 * e + m + 1])
                ins_.then_inc((s_ha, s_hd)[e % 2], 1)

            for e in range(NE):
                relu(0, e)
            act.wait_ge(s_d, 1)
            nc.scalar.activation(stat[:, 5, :], stat[:, 4, :], ACT.Exp).then_inc(s_ed, 1)
            with act.Fori(0, G // 2 - 1) as t:
                for e in range(0, NE, 2):
                    relu(t + 1, e)

        @block.tensor
        def _(pe):
            mm = nc.tensor.matmul

            def split2(dst, hi2, split, lo, split_hi, start, stop):
                mm(dst, hi2, split, start=start, stop=False)
                return mm(dst, lo, split_hi, start=False, stop=stop)

            pe.wait_ge(s_split1, 2)
            for b in range(B):
                x0 = b * T
                for k in range(4):
                    if b and k < 2:
                        pe.wait_ge(s_tret, 2 * b)
                    off = O_TQ if k < 2 else O_TK
                    cs = slice(x0 + 512 * (k % 2), x0 + 512 * (k % 2) + 512)
                    split2(ps[:, k, :], WH[:, off:off + P], XS[:, cs], WL[:, off:off + P], XS[0:D, cs],
                           True, True).then_inc(s_tproj, 1)
                if b:
                    pe.wait_ge(s_th, b)
                for t in range(TT):
                    cs = slice(x0 + P * t, x0 + P * t + P)
                    last = split2(ps[:, 4, D * t:D * t + D], XS[:, cs], WH[:, O_TV:O_TV + D],
                                  XS[0:D, cs], WL[:, O_TV:O_TV + D], t == 0, t == TT - 1)
                last.then_inc(s_tproj, 1)
                pe.wait_ge(s_tlow, 4 * (b + 1))
                pe.wait_ge(s_tv, b + 1)

                def retain(n):
                    m = 16 * b + n
                    pe.wait_ge(s_tpt, m + 1)
                    mm(ps[0:D, n % 2, :], tv[:, n // 2, :], ptt[:, m % 4, :], start=n < 2, stop=n >= 14).then_inc(s_tpv, 1)

                for n in range(16):
                    m = 16 * b + n
                    s, half = n // 2, n % 2
                    if m >= 3:
                        pe.wait_ge(s_tpt, m - 2)
                    if m == 16:
                        pe.wait_ge(s_wps, 2)
                    ss, hs = slice(P * s, P * s + P), slice(512 * half, 512 * half + 512)
                    split2(ps[:, 5 + m % 3, :], tk[:, ss], tq[:, hs], tk[0:D, ss], tql[:, hs],
                           True, True).then_inc(s_tsc, 1)
                    if n >= LAG:
                        retain(n - LAG)
                for n in range(16 - LAG, 16):
                    retain(n)
                pe.wait_ge(s_tret, 2 * (b + 1))
                pe.wait_ge(d_two, 16)
                for t in range(TT):
                    last = mm(ps[:, 4, D * t:D * t + D], tret[:, P * t:P * t + P], two[:],
                              start=t == 0, stop=t == TT - 1)
                last.then_inc(s_ty, 1)
                if b == 0:
                    pe.wait_ge(d_wv, 64)
                    pe.wait_ge(s_bvr, 1)
                    pe.wait_ge(s_tpt, 16)
                    for hd in range(NH):
                        mm(ps[:, 5, D * hd:D * hd + D], wvT[:, hd], wu[:, hd, :], start=hd == 0, stop=hd == NH - 1)
                    for hd in range(NH):
                        last = mm(ps[:, 6, 0:D], bvrep[:, hd, :], wu[:, hd, :], start=hd == 0, stop=hd == NH - 1)
                    last.then_inc(s_wp, 1)

            def turn(k):
                for c in range(NC):
                    pe.wait_ge(s_u, k + 1 if k < 4 else k + 3)
                    if k:
                        pe.wait_ge(s_us, NC * (k - 1) + c + 1)
                    for t in range(TPC):
                        last = nc.tensor.transpose(ps[0:D, c, P * t:P * t + P], u[:, (k % 2) * NT + TPC * c + t, :], ident[:])
                    last.then_inc(s_tr, 1)

            pe.wait_ge(s_th, B)
            pe.wait_ge(s_const, 2)
            turn(0)
            turn(1)

            def values(n):
                pe.wait_ge(s_us, NC * (n // NT) + n % NT // TPC + 1)
                if n >= 3:
                    pe.wait_ge(s_vx[(n - 3) % 2], (n - 3) // 2 + 1)
                cs = slice(n * P, n * P + P)
                split2(ps[:, V_BANKS[n % 3], :], US[:, cs], WPH[:], US[0:D, cs], WPL[:], True, True).then_inc(s_v, 1)

            pe.sem_inc(s_pv, 6)
            pe.sem_inc(s_to, 2)

            def a_bank(k):
                return ps[:, 4 + k % 2]

            def project(v, b, k):
                if k == 0:
                    pe.wait_ge(s_wsl, 4 * (head_of[0] + 1))
                pe.wait_ge(s_af, NA * v + k + 1)
                cs = slice(b * SP_ + CW * (k % NC), b * SP_ + CW * (k % NC) + CW)
                split2(a_bank(k)[:, 0:CW], wh4[:, k // NC], US[:, cs], wl4[:, k // NC], US[0:D, cs],
                       True, True).then_inc(s_a, 1)

            def scores_for_max(v, b, k):
                i, a, z = SMAX[k]
                if k == 0:
                    pe.wait_ge(s_af, NA * v + 2 * NC + 2)
                pe.wait_ge(s_af, NA * v + 2 * NC + k + 1)
                bank = a_bank(2 * NC + k)
                diag = z == P * (i + 1)
                last = mm(bank[:, 0:z - a], qs[b][:, P * i:P * i + P], ks[b][:, a:z], start=True, stop=not diag)
                if diag:
                    last = mm(bank[:, z - a - P:z - a], identb[:], mask_s[:], start=False, stop=True)
                last.then_inc(s_a, 1)

            def turn_max(v, b):
                pe.wait_ge(s_af, NA * v + NA)
                pe.wait_ge(s_mneg, v + 1)
                nc.tensor.transpose(a_bank(NA - 1)[0:NT, 0:P], mneg[:, b], ident[:]).then_inc(s_a, 1)

            def scores(w, b, s):
                c, j = STEPS[s]
                lo = max(P * j, CW * c)
                z = CW * (c + 1)
                bank = ps[:, s % 3]
                if s == 0:
                    pe.wait_ge(d_mrow, 16 * (w + 1))
                    pe.wait_ge(s_kh, w + 1)
                pe.wait_ge(s_ex, NS * w + s + 1)
                dst = bank[:, lo - CW * c:CW]
                js = slice(P * j, P * j + P)
                mm(dst, ks[b][:, js], qs[b][:, lo:z], start=True, stop=False)
                last = mm(dst, kh[b][:, js], ql[b][:, lo:z], start=False, stop=j < TPC * c)
                if j >= TPC * c:
                    last = mm(bank[:, lo - CW * c:lo - CW * c + P], identb[:], mask_t[:], start=False, stop=True)
                last.then_inc(s_st, 1)

            def weigh(w, b, s):
                c, j = STEPS[s]
                o = (c + NC * b) % 2
                lo = max(P * j, CW * c) - CW * c
                pe.wait_ge(s_ex, NS * w + s + 4)
                if s == 0:
                    pe.wait_ge(s_vs, w + 1)
                if j == 0:
                    pe.wait_ge(s_of, NC * w + c + 1)
                mm(ps[0:D + 1, 6 + o, lo:CW], vs[b][:, j, :], pt[:, s % 6, lo:CW], start=j == 0,
                   stop=s == LAST[c]).then_inc(s_pv, 1)

            def turn_back(w, b, c):
                o = (c + NC * b) % 2
                pe.wait_ge(s_of, NC * w + c + 3)
                pe.wait_ge(s_nf, NC * w + c + 1)
                for r in range(TPC):
                    last = nc.tensor.transpose(ps[:, 3, (D + 1) * r:(D + 1) * (r + 1)], ot[:, o, P * r:P * r + P],
                                               ident[0:D + 1, 0:D + 1])
                last.then_inc(s_to, 1)

            def slot(w, b, first=False, follow=True):
                for s in range(NS):
                    scores(w, b, s)
                    if follow:
                        for k in PROJECT_AT.get(s, ()):
                            project(w + 1, 1 - b, k)
                        for k in MAX_AT.get(s, ()):
                            scores_for_max(w + 1, 1 - b, k)
                        if s == TURN_MAX_AT:
                            turn_max(w + 1, 1 - b)
                    if s >= LAG:
                        weigh(w, b, s - LAG)
                    elif not first:
                        weigh(w - 1, 1 - b, s - LAG + NS)
                    for c in range(NC):
                        if BACK_AT[c] == s:
                            turn_back(w, b, c)
                        if BACK_AT[c] == s + NS and not first:
                            turn_back(w - 1, 1 - b, c)

            head_of = [0]
            pe.wait_ge(s_split2, 1)
            pe.wait_ge(s_us, NC)
            for k in range(NA):
                if k < 2 * NC:
                    project(0, 0, k)
                elif k < 2 * NC + NM:
                    scores_for_max(0, 0, k - 2 * NC)
                else:
                    turn_max(0, 0)
                if k < G:
                    values(k)
            for parity in range(2):
                pe.wait_ge(s_vx[parity], G // 2)
            slot(0, 0, first=True)
            with pe.Fori(0, NH - 1) as i:
                head_of[0] = i + 1
                slot(2 * i + 1, 1)
                slot(2 * i + 2, 0)
            slot(2 * NH - 1, 1, follow=False)
            for s in range(NS - LAG, NS):
                weigh(2 * NH - 1, 1, s)
            turn_back(2 * NH - 1, 1, NC - 1)

            turn(2)
            turn(3)
            pe.wait_ge(d_late, 16 * 6)

            def free_bank(item):
                old = item - 4
                if 0 <= old < B * NC:
                    pe.wait_ge(s_wb, old + 1)
                elif old >= 0:
                    b, k = divmod(old - B * NC, 3 * NC)
                    if k < 2 * NC:
                        pe.wait_ge(s_gelu, 2 * NC * b + k + 1)
                    else:
                        pe.wait_ge(s_rd, NC * b + k - 2 * NC + 1)
                return ps[:, 3 + item % 4, 0:CW]

            for k in range(B * NC):
                pe.wait_ge(s_us, B * NC + k + 1)
                cs = slice(CW * k, CW * k + CW)
                split2(free_bank(k), WRH[:], US[:, cs], WRL[:], US[0:D, cs], True, True).then_inc(s_r, 1)
            for b in range(B):
                pe.wait_ge(s_wb, NC * (b + 1))
                for t in range(NT):
                    last = nc.tensor.transpose(ps[:, 7, NT * b + t:NT * b + t + 1], wbc[0:1, b, P * t:P * t + P],
                                               ident[0:1, 0:1])
                last.then_inc(s_wt, 1)

            def rank(b, t):
                k = min(P, S - P * t)
                pe.wait_ge(s_cmp, NT * b + t + 1)
                sl = (NT * b + t) % 3
                for r in range(NT):
                    last = mm(ps[:, b, r:r + 1], above[0:k, sl, P * r:P * r + P], onesb[0:k, 0:1],
                              start=(t == 0 and r == 0), stop=(t == NT - 1 and r < NT - 1), skip_group_check=True)
                    if r == t:
                        last = mm(ps[:, b, r:r + 1], tie[0:k, sl, :], onesb[0:k, 0:1],
                                  start=False, stop=t == NT - 1, skip_group_check=True)
                last.then_inc(s_rk, 1)

            def ffn_hidden(b, k):
                m, c = divmod(k, NC)
                bank = free_bank(B * NC + 3 * NC * b + k)
                cs = slice(b * SP_ + CW * c, b * SP_ + CW * c + CW)
                ws = slice(O_W1 + P * m, O_W1 + P * m + P)
                split2(bank, WH[:, ws], US[:, cs], WL[:, ws], US[0:D, cs], True, True).then_inc(s_r, 1)

            for b in range(B):
                for t in range(NT):
                    if t < 2 * NC:
                        ffn_hidden(b, t)
                        rank(b, t)
                        continue
                    c = t - 2 * NC
                    bank = free_bank(B * NC + 3 * NC * b + 2 * NC + c)
                    pe.wait_ge(s_gelu, 2 * NC * b + NC + c + 1)
                    for i in range(TPC):
                        for m in range(2):
                            ts = slice(P * (TPC * c + i), P * (TPC * c + i) + P)
                            last = mm(bank[:, D * i:D * i + D], hT[:, m, ts], w2[:, m, :],
                                      start=(i == 0 and m == 0), stop=(i == TPC - 1 and m == 1), skip_group_check=True)
                    last.then_inc(s_r, 1)
                    rank(b, t)

            pe.wait_ge(s_ush, B)
            pe.wait_ge(s_toep, 1)
            for ch in range(D):
                k, r = divmod(ch, 14)
                if r == 0 and k >= 3:
                    pe.wait_ge(s_rd, B * NC)
                last = mm(ps[0:D, k, 2 * G * r:2 * G * (r + 1)], toep[:, ch, :], UU[:, :, :, ch],
                          start=r == 0, stop=(r == 13 or ch == D - 1), skip_group_check=True)
                if r == 13 or ch == D - 1:
                    last.then_inc(s_cv, 1)

            pe.wait_ge(s_cvf, 10)
            turn(4)
            turn(5)
            pe.wait_ge(s_us, NC * 6)
            pe.sem_inc(s_hu, NE)
            relu_done = (s_ha, s_hd)

            def hidden(t, e, guard=False):
                if guard:
                    pe.wait_ge(s_gt, len(GATE_BANKS))
                tokens = bass.ds(t * 256, 256)
                pe.wait_ge(relu_done[e % 2], (NE // 2) * t + e // 2 + 1)
                for m in range(2):
                    ws = slice(O_E + HID * e + P * m, O_E + HID * e + P * m + P)
                    last = split2(ps[:, 4 + e % 4, 256 * m:256 * m + 256], WH[:, ws], US[:, tokens], WL[:, ws],
                                  US[0:D, tokens], m == 0, m == 1)
                last.then_inc(s_hh, 1)

            def down(t, e, y):
                pe.wait_ge(relu_done[e % 2], (NE // 2) * t + e // 2 + 3)
                for r in range(2):
                    for m in range(2):
                        last = mm(ps[:, 2 * y + r, D * e:D * e + D], eh[:, e, m, P * r:P * r + P], ew2[:, m, e, :],
                                  start=False, stop=(e == NE - 1 and m == 1), skip_group_check=True)
                last.then_inc(s_hu, 1)

            def bias_rows(t, y):
                pe.wait_ge(s_yf, t + 1)
                for r in range(2):
                    mm(ps[:, 2 * y + r, :], onesb[0:65], b2p[:], start=True, stop=False, skip_group_check=True)

            def hiddens(t, first=False):
                for e in range(NE):
                    hidden(t, e, guard=first and e == 3)

            def downs(t, y):
                bias_rows(t, y)
                for e in range(NE):
                    down(t, e, y)

            for k, bank in enumerate(GATE_BANKS):
                cs = slice(512 * k, min(512 * k + 512, B * SP_))
                split2(ps[0:NE, bank, 0:cs.stop - cs.start], WH[:, O_G:O_G + NE], US[:, cs], WL[:, O_G:O_G + NE],
                       US[0:D, cs], True, True).then_inc(s_gt_mm, 1)
            hiddens(0, first=True)
            for g in range(G):
                if g % 4 == 0:
                    pe.wait_ge(s_gt, g // 4 + 1)
                last = nc.tensor.transpose(ps[:, 3, NE * g:NE * g + NE], gT[:, P * g:P * g + P], ident[0:NE, 0:NE])
            last.then_inc(s_g, 1)
            pe.wait_ge(s_b2, 3)
            downs(0, 0)
            with pe.Fori(0, G // 4) as i:
                for y in range(1, 3):
                    hiddens(2 * i + y)
                    downs(2 * i + y, y % 2)

        @block.vector
        def _(dve):
            n = [0]
            tt, ts, stt = nc.vector.tensor_tensor, nc.vector.tensor_scalar, nc.vector.scalar_tensor_tensor

            def link(instruction):
                n[0] += 1
                instruction.then_inc(s_dve, 1)
                dve.wait_ge(s_dve, n[0])

            def wide(col, k):
                return col.unsqueeze(2).broadcast_to([P, k, D])

            def split_weights(a, z):
                link(nc.vector.tensor_copy(WH[:, a:z], WR[:, a:z]))
                link(tt(WL[:, a:z], WR[0:D, a:z], WH[0:D, a:z], ALU.subtract))

            dve.wait_ge(d_wtok, 32)
            split_weights(0, O_Q)
            dve.wait_ge(d_x, 32)
            nc.vector.tensor_copy(XS[:], XR[:]).then_inc(s_split1, 1)
            dve.wait_ge(s_split1, 1)
            tt(XS[D:P, :], XR[D:P, :], XS[D:P, :], ALU.subtract).then_inc(s_split1, 1)
            dve.wait_ge(d_rows, 16)
            dve.wait_ge(d_cols, 16)
            for b in range(B):
                for k in range(4):
                    dve.wait_ge(s_tround, 4 * b + k + 1)
                    cs = slice(512 * (k % 2), 512 * (k % 2) + 512)
                    if k < 2:
                        stt(tql[:, cs], ps[0:D, k, :], cols[0:D, C_TBQ:C_TBQ + 1], tq[0:D, cs], ALU.add,
                            ALU.subtract).then_inc(s_tlow, 1)
                    else:
                        stt(tk[D:P, cs], ps[D:P, k, :], cols[D:P, C_TBK:C_TBK + 1], tk[D:P, cs], ALU.add,
                            ALU.subtract).then_inc(s_tlow, 1)
                dve.wait_ge(s_tproj, 5 * (b + 1))
                tt(tv[:], ps[:, 4, :].rearrange("p (t d) -> p t d", d=D),
                   rows[:, R_TBV:R_TBV + D].unsqueeze(1).broadcast_to([P, TT, D]), ALU.add).then_inc(s_tv, 1)
                for k in range(16):
                    m = 16 * b + k
                    s, half = k // 2, k % 2
                    if b == 0 and half == 0:
                        dve.wait_ge(d_gam[s], 16)
                    dve.wait_ge(s_tsc, m + 1)
                    if m >= 4:
                        dve.wait_ge(s_tpv, m - 3)
                    tt(ptt[:, m % 4, :], ps[:, 5 + m % 3, :], gam[:, s, 512 * half:512 * half + 512],
                       ALU.mult).then_inc(s_tpt, 1)
                dve.wait_ge(s_ty, b + 1)
                hb, yb = h[:, b * NT:b * NT + TT, :], sq[:, 0:TT, :]
                link(tt(yb, ps[:, 4, :].rearrange("p (t d) -> p t d", d=D),
                        rows[:, R_TBO:R_TBO + D].unsqueeze(1).broadcast_to([P, TT, D]), ALU.add))
                link(ts(hb, yb, 0.0, cols[:, C_A:C_A + 1], ALU.min, ALU.mult))
                stt(hb, yb, 0.0, hb, ALU.max, ALU.add).then_inc(s_th, 1)
                dve.wait_ge(s_th, b + 1)
                if b == 0:
                    dve.wait_ge(s_wp, 1)
                    tt(cst[:], ps[:, 6, 0:D], rows[:, R_BU:R_BU + D], ALU.add).then_inc(s_wps, 1)
                    dve.wait_ge(s_wph, 1)
                    tt(WPL[:], ps[0:D, 5, :], WPH[0:D, :], ALU.subtract).then_inc(s_wps, 1)

            def layernorm(k):
                st = [stat[:, r] for r in range(10)]
                halves = [slice(b * NT, b * NT + NT) for b in range(B)]
                link(nc.vector.tensor_reduce(st[0], h[:], AX.X, ALU.add))
                link(ts(st[1], st[0], -1.0 / D, None, ALU.mult))
                for g in halves:
                    tt(u[:, g], h[:, g], wide(stat[:, 1, g], NT), ALU.add).then_inc(s_cen, 1)
                for b, g in enumerate(halves):
                    dve.wait_ge(s_sq, B * k + b + 1)
                    last = nc.vector.tensor_reduce(stat[:, 0, g], sq[:, g], AX.X, ALU.add)
                    last.then_inc(s_dve, 1)
                n[0] += B
                dve.wait_ge(s_dve, n[0])
                ts(st[2], st[0], 1.0 / D, EPS, ALU.mult, ALU.add).then_inc(s_var, 1)
                dve.wait_ge(s_var, k + 1)
                dve.wait_ge(s_sd, k + 1)
                link(nc.vector.reciprocal(st[6], st[3]))
                link(tt(st[7], st[2], st[6], ALU.mult))
                link(tt(st[8], st[7], st[3], ALU.add))
                link(nc.vector.reciprocal(st[6], st[8]))
                for b, g in enumerate(halves):
                    stt(u[:, g], u[:, g], 2.0, wide(stat[:, 6, g], NT), ALU.mult, ALU.mult).then_inc(s_u, 1)

            def low(k):
                for c in range(NC):
                    m, b = NC * k + c, k % 2
                    cs = slice(b * SP_ + CW * c, b * SP_ + CW * c + CW)
                    dve.wait_ge(s_uhi, m + 1)
                    tt(US[D:P, cs], ps[0:D, c, 0:CW], US[0:D, cs], ALU.subtract).then_inc(s_us, 1)

            dve.wait_ge(s_const, 2)
            dve.wait_ge(d_w, 32)
            link(ts(wr_rep[:], ones[:], WR[:, O_WR:O_WR + 1], None, ALU.mult))
            link(nc.vector.tensor_copy(WRH[:], wr_rep[:]))
            link(tt(WRL[:], wr_rep[0:D, :], WRH[0:D, :], ALU.subtract))
            link(nc.vector.memset(mpart[:], -3e38))
            for b in range(B):
                link(nc.vector.memset(UU[0:D, 0, b * NT, :], 0.0))
            dve.wait_ge(d_txt, 32)
            layernorm(0)
            low(0)
            low(1)
            dve.wait_ge(s_split2, 1)

            dve.sem_inc(s_yf, 2)
            dve.sem_inc(s_af, 2)
            dve.sem_inc(s_nf, 1)
            base, m = [0], [0]

            def chain(instruction):
                m[0] += 1
                instruction.then_inc(s_dvl, 1)
                dve.wait_ge(s_dvl, base[0] + m[0])

            def low_part(v, b, k):
                cs = slice(CW * (k % NC), CW * (k % NC) + CW)
                dve.wait_ge(s_ar, 2 * NC * v + k + 1)
                src = ps[:, 4 + k % 2, 0:CW]
                if k < NC:
                    ins_ = stt(ql[b][0:D, cs], src[0:D], head_col(C_BQ)[0:D], qs[b][0:D, cs], ALU.add, ALU.subtract)
                else:
                    ins_ = stt(ks[b][D:P, cs], src[D:P], head_col(C_BK)[D:P], ks[b][D:P, cs], ALU.add, ALU.subtract)
                ins_.then_inc(s_af, 1)

            def head_col(col):
                return cols[:, bass.ds(head_of[0] + col, 1)]

            def maximum(v, b, k):
                i, a, z = SMAX[k]
                dve.wait_ge(s_a, NA * v + 2 * NC + k + 1)
                nc.vector.tensor_reduce(mpart[:, b, i, a // 512:a // 512 + 1], ps[:, 4 + k % 2, 0:z - a], AX.X,
                                        ALU.max).then_inc(s_af, 1)

            def whole_maximum(v, b):
                dve.wait_ge(s_af, NA * v + NA + 1)
                chain(nc.vector.tensor_reduce(mneg[:, b], mpart[:, b], AX.X, ALU.max))
                ts(mneg[:, b], mneg[:, b], -1.0, None, ALU.mult).then_inc(s_mneg, 1)

            def take_row(v, b):
                dve.wait_ge(s_a, NA * v + NA)
                nc.vector.tensor_copy(mrow[b][:], ps[0:NT, 5, 0:P]).then_inc(s_af, 1)

            def output(w, b, c):
                dve.wait_ge(s_to, NC * w + c + 3)
                o = ps[:, 3, 0:TPC * (D + 1)].rearrange("p (r d) -> p r d", d=D + 1)
                chain(nc.vector.reciprocal(rden[:, c % 2], o[:, :, D]))
                tt(onrm[:, c % 2], o[:, :, 0:D], wide(rden[:, c % 2], TPC), ALU.mult).then_inc(s_nf, 1)
                dve.wait_ge(s_nf, NC * w + c + 2)
                hc = h[:, b * NT + TPC * c:b * NT + TPC * c + TPC, :]
                chain(tt(hc, hc, onrm[:, c % 2], ALU.add))

            def slot(w, b, first=False, follow=True):
                for s in range(NS):
                    if follow:
                        for k in PROJECT_AT.get(s, ()):
                            low_part(w + 1, 1 - b, k)
                        for k in MAX_AT.get(s, ()):
                            maximum(w + 1, 1 - b, k)
                        if s == WHOLE_AT:
                            whole_maximum(w + 1, 1 - b)
                        if s == TURN_MAX_AT:
                            take_row(w + 1, 1 - b)
                    for c in range(NC):
                        if BACK_AT[c] == s:
                            output(w, b, c)
                        if BACK_AT[c] == s + NS and not first:
                            output(w - 1, 1 - b, c)

            head_of = [0]
            for k in range(G):
                if k < 2 * NC:
                    low_part(0, 0, k)
                elif k < 2 * NC + NM:
                    maximum(0, 0, k - 2 * NC)
                if k % 2:
                    dve.wait_ge(s_v, k + 1)
                    nc.vector.tensor_copy(VX[:, k // NT, k % NT, :, 0:D], ps[:, V_BANKS[k % 3], :]
                                          .rearrange("p (h d) -> p h d", d=D)).then_inc(s_vx[1], 1)
            for k in range(G - 2 * NC, NM):
                maximum(0, 0, k)
            whole_maximum(0, 0)
            take_row(0, 0)
            dve.wait_ge(s_cst, 1)
            slot(0, 0, first=True)
            before_loop, per_slot = m[0], 1 + 2 * NC
            with dve.Fori(0, NH - 1) as i:
                head_of[0], base[0], m[0] = i + 1, i * (2 * per_slot) + before_loop, 0
                slot(2 * i + 1, 1)
                slot(2 * i + 2, 0)
                assert m[0] == 2 * per_slot
            base[0], m[0] = (NH - 1) * 2 * per_slot + before_loop, 0
            slot(2 * NH - 1, 1, follow=False)
            output(2 * NH - 1, 1, NC - 1)

            link(nc.vector.tensor_copy(h[0:1, 0:G:NT, :], alone[:]))

            layernorm(1)
            low(2)
            low(3)

            def compare(b, t):
                m = NT * b + t
                sl, w = m % 3, wcol[:, b, t:t + 1]
                if m >= 3:
                    dve.wait_ge(s_rk, m - 2)
                if t:
                    ts(above[:, sl, 0:P * t], wbc[:, b, 0:P * t], w, None, ALU.is_lt)
                if t < NT - 1:
                    ts(above[:, sl, P * t + P:SP_], wbc[:, b, P * t + P:SP_], w, None, ALU.is_le)
                own = wbc[:, b, P * t:P * t + P]
                stt(above[:, sl, P * t:P * t + P], own, w, before[:], ALU.is_lt, ALU.mult)
                stt(tie[:, sl, :], own, w, after[:], ALU.is_le, ALU.mult).then_inc(s_cmp, 1)

            def take_y(b):
                for c in range(NC):
                    item = B * NC + 3 * NC * b + 2 * NC + c
                    dve.wait_ge(s_r, item + 1)
                    gc = slice(b * NT + TPC * c, b * NT + TPC * c + TPC)
                    tt(sq[:, gc], ps[:, 3 + item % 4, 0:TPC * D].rearrange("p (t d) -> p t d", d=D),
                       rows[:, R_B2:R_B2 + D].unsqueeze(1).broadcast_to([P, TPC, D]), ALU.add).then_inc(s_rd, 1)

            def add_y(b):
                g = slice(b * NT, b * NT + NT)
                dve.wait_ge(s_rk, NT * (b + 1))
                link(stt(sel[:, b], ps[:, b, 0:NT], float(KK), wcol[:, b], ALU.is_lt, ALU.mult))
                dve.wait_ge(s_rd, NC * (b + 1))
                link(tt(sq[:, g], sq[:, g], wide(sel[:, b], NT), ALU.mult))
                dve.wait_ge(s_skip, b + 1)
                link(tt(h[:, g], h[:, g], sq[:, g], ALU.add))

            for b in range(B):
                dve.wait_ge(s_wt, b + 1)
            link(nc.vector.tensor_copy(wcol[:], ps[:, 7, 0:G].rearrange("p (b t) -> p b t", t=NT)))
            for t in range(NT):
                compare(0, t)
            for t in range(NT):
                compare(1, t)
                if t == 2:
                    take_y(0)
            add_y(0)
            take_y(1)
            add_y(1)

            layernorm(2)
            for b in range(B):
                dve.wait_ge(s_u, 2 * B + b + 1)
                g0, g1 = b * NT, b * NT + NT
                link(nc.vector.tensor_copy(UU[0:D, 0, g0 + 1:g1, :], UU[D:P, 1, g0:g1 - 1, :]))
                nc.vector.tensor_copy(UU[D:P, 0, g0:g1, :], UU[0:D, 1, g0:g1, :]).then_inc(s_ush, 1)
            for k in range(5):
                c0, c1 = 14 * k, min(14 * k + 14, D)
                dve.wait_ge(s_cv, k + 1)
                y = ps[0:D, k, 0:2 * G * (c1 - c0)].rearrange("p (c g) -> p g c", g=2 * G)
                tt(h[0:D, :, c0:c1], y[:, 0:G, :], h[0:D, :, c0:c1], ALU.add).then_inc(s_cvf, 1)
                tt(h[D:P, :, c0:c1], y[:, G:2 * G, :], h[D:P, :, c0:c1], ALU.add).then_inc(s_cvf, 1)
            dve.wait_ge(s_cvf, 10)

            layernorm(3)
            low(4)
            low(5)
            dve.wait_ge(s_g, 1)
            tt(gate[:], ps[:, 3, 0:G * NE].rearrange("p (g e) -> p g e", e=NE),
               rows[:, R_BG:R_BG + NE].unsqueeze(1).broadcast_to([P, G, NE]), ALU.add).then_inc(s_gf, 1)
            dve.wait_ge(s_gf, 1)
            narrow = lambda r: stat[:, r, :].unsqueeze(2).broadcast_to([P, G, NE])
            order = desc[:].unsqueeze(1).broadcast_to([P, G, NE])

            def first_of(gates, top, where):
                link(nc.vector.tensor_reduce(stat[:, top, :], gates, AX.X, ALU.max))
                link(tt(eq[:], gates, narrow(top), ALU.is_equal))
                link(tt(eq[:], eq[:], order, ALU.mult))
                link(nc.vector.tensor_reduce(stat[:, 9, :], eq[:], AX.X, ALU.max))
                link(tt(where, order, narrow(9), ALU.is_equal))

            first_of(gate[:], 1, is0[:])
            link(stt(gate[:], is0[:], -3e38, gate[:], ALU.mult, ALU.add))
            first_of(gate[:], 0, is1[:])
            tt(stat[:, 4, :], stat[:, 0, :], stat[:, 1, :], ALU.subtract).then_inc(s_d, 1)
            dve.wait_ge(s_ed, 1)
            link(ts(stat[:, 6, :], stat[:, 5, :], 1.0, None, ALU.add))
            link(nc.vector.reciprocal(stat[:, 7, :], stat[:, 6, :]))
            link(tt(stat[:, 8, :], stat[:, 7, :], stat[:, 5, :], ALU.mult))
            link(tt(comb[:], is0[:], narrow(7), ALU.mult))
            link(tt(is1[:], is1[:], narrow(8), ALU.mult))
            link(tt(comb[:], comb[:], is1[:], ALU.add))
            def relu(t, e):
                dve.wait_ge(s_hh, NE * t + e + 1)
                dve.wait_ge(s_hu, NE * t + e + 1)
                for k in range(2):
                    ins_ = ts(eh[:, e, k, :], ps[:, 4 + e % 4, 256 * k:256 * k + 256],
                              cols[:, C_EB1 + 2 * e + k:C_EB1 + 2 * e + k + 1], 0.0, ALU.add, ALU.max)
                ins_.then_inc(s_hd, 1)

            def combine(t, y):
                dve.wait_ge(s_hu, NE * t + 2 * NE)
                for r in range(2):
                    ins_ = tt(yw[:, r], ps[:, 2 * y + r, :].rearrange("p (e d) -> p e d", d=D),
                              comb[:, bass.ds(2 * t + r, 1), :].rearrange("p o e -> p (o e)").unsqueeze(2)
                              .broadcast_to([P, NE, D]), ALU.mult)
                ins_.then_inc(s_yf, 1)
                dve.wait_ge(s_yf, t + 3)
                nc.vector.tensor_reduce(ysum[:], yw[:].rearrange("p r e d -> p r d e"), AX.X,
                                        ALU.add).then_inc(s_dvm, 1)
                dve.wait_ge(s_dvm, t + 1)
                hb = h[:, bass.ds(2 * t, 2), :]
                tt(hb, hb, ysum[:], ALU.add).then_inc(s_fin, 1)
                dve.wait_ge(s_fin, t + 1)

            with dve.Fori(0, G // 4) as i:
                for y in range(2):
                    for e in range(1, NE, 2):
                        relu(2 * i + y + 1, e)
                    combine(2 * i + y, y)
            combine(G // 2 - 1, 0)


def kernel(**inputs):
    import numpy as np
    import concourse.bacc as bacc
    from concourse.bass_utils import run_bass_kernel_spmd

    a = {k: np.asarray(v) for k, v in inputs.items()}
    cat = np.concatenate
    t_q, t_k = a["L0_tok_Wq"], a["L0_tok_Wk"]
    column = lambda v: v.reshape(-1, D).T
    twice = lambda m: cat([m, m], axis=0)
    laid = {
        "xT": a["x"].reshape(B, T, D).transpose(2, 0, 1).reshape(D, B * T),
        "txt": a["txt"],
        "gammaT": a["L0_tok_d_gamma_batched"].T,
        "w64": cat([t_q, t_q, t_k, t_k, a["L0_tok_Wv"], a["L0_attn_Wq"], a["L0_attn_Wk"], a["L0_ffn_w1"],
                    a["L1_ffn_Wg"].T, a["L1_ffn_W1"].transpose(2, 0, 1).reshape(D, NE * HID), a["L0_ffn_wr"]], axis=1),
        "cols": cat([twice(column(a["L0_tok_bq"])), twice(column(a["L0_tok_bk"])),
                     twice(column(a["L0_attn_bq"])), twice(column(a["L0_attn_bk"])),
                     a["L0_ffn_b1"].reshape(2, P).T, a["L1_ffn_b1"].reshape(2 * NE, P).T,
                     np.tile(a["L0_tok_prelu_a"].reshape(1, 1), (P, 1)),
                     np.tile(a["L0_ffn_br"].reshape(1, 1), (P, 1))], axis=1),
        "rows": cat([a["L0_tok_bv"], a["L0_tok_bo"], a["L0_attn_bu"], a["L0_ffn_b2"], a["L1_ffn_bg"]]).reshape(1, NROW),
        "wvT": a["L0_attn_Wv"].reshape(D, NH, D).transpose(2, 1, 0),
        "bvT": column(a["L0_attn_bv"]),
        "wu": a["L0_attn_Wu"].reshape(NH, D, D).transpose(1, 0, 2),
        "two": a["L0_tok_Wo"],
        "w2": a["L0_ffn_w2"].reshape(2, P, D).transpose(1, 0, 2),
        "ew2": a["L1_ffn_W2"].transpose(2, 0, 1).reshape(2, P, NE, D).transpose(1, 0, 2, 3),
        "eb2": a["L1_ffn_b2"].reshape(1, NE * D),
        "cpad": np.pad(a["L1_attn_c"][0][:, ::-1], ((0, 0), (D, D))).reshape(-1),
    }
    laid = {k: np.ascontiguousarray(v) for k, v in laid.items()}
    nc = bacc.Bacc("TRN2", target_bir_lowering=False, num_devices=1)
    ins = {k: nc.dram_tensor(f"in_{k}", v.shape, F32, kind="ExternalInput").ap() for k, v in laid.items()}
    out = nc.dram_tensor("out", (B, S, D), F32, kind="ExternalOutput").ap()
    early_fusion(nc, ins, out)
    r = run_bass_kernel_spmd(nc, [{f"in_{k}": v for k, v in laid.items()}], core_ids=[0])
    return r.results[0]["out"]
```

```python
from contextlib import ExitStack

import concourse.bass as bass
from concourse import mybir

F32 = mybir.dt.float32
F32R = mybir.dt.float32r
BF16 = mybir.dt.bfloat16
ALU = mybir.AluOpType
ACT = mybir.ActivationFunctionType
AX = mybir.AxisListType

P = 128
D = 64
B = 2
T = 1024
TXT = 77
S = T + TXT
NT = -(-S // P)
SP_ = NT * P
G = B * NT
NH = 8
HID = 256
NE = 8
KK = max(1, int(0.5 * S)) - 1
EPS = 1e-5
NEG = -1e30
CW = 384
NC = SP_ // CW
TPC = CW // P
TT = T // P

O_TQ, O_TK, O_TV = 0, 128, 256
O_Q, O_K = 320, 832
O_W1 = 1344
O_G = 1600
O_E = 1608
O_WR = O_E + NE * HID
NW = O_WR + 1
C_TBQ, C_TBK, C_BQ, C_BK, C_B1, C_EB1, C_A, C_BR = 0, 1, 2, 10, 18, 20, 36, 37
NCOL = 38
R_TBV, R_TBO, R_BU, R_B2, R_BG = 0, 64, 128, 192, 256
NROW = 264

NB = 2 * TT
TSLOTS, TLAG = 5, 4
TORDER = (2, 3, 0, 1)
TPROJ = (2, 3, "v", 0, 1)


def lows(m):
    return (0, m // 3 + 1) if m % 3 == 0 else (1, m - m // 3)


STEPS = [(c, j) for c in range(NC) for j in range(TPC * (c + 1))]
NS = len(STEPS)
SMAX = [(i, a, min(a + 512, P * (i + 1))) for i in range(NT) for a in range(0, P * (i + 1), 512)]
NM = len(SMAX)
NA = NC + NM + 1
LAG = 2
PROJECT_AT = {0: (0,), 1: (1,), 3: (2,)}
MAX_AT = {7 + k // 2: tuple(x for x in (k, k + 1) if x < NM) for k in range(0, NM, 2)}
WHOLE_AT = TURN_MAX_AT = 15
LAST = [STEPS.index((c, TPC * (c + 1) - 1)) for c in range(NC)]
COPY_AT = [x + LAG for x in LAST]
BACK_AT = [LAST[0] + 4, LAST[1] + 8, LAST[2] + 4]
EARLY_LN = 7
V_BANKS = (3, 6, 7)
V_ON_DVE = (0, 1, 2, 3, 8, 13)


def v_taken(n):
    dve = sum(x <= n for x in V_ON_DVE)
    return (1, dve) if n in V_ON_DVE else (0, n + 1 - dve)


GATE_BANKS = (3, 0, 1, 2, 7)


def early_fusion(nc, ins, out):
    ctx = ExitStack()
    with ctx:
        def sb(name, shape, dt=F32, where=None):
            return (where or ctx).enter_context(nc.sbuf_tensor(name, shape, dt))

        def sem(name):
            return ctx.enter_context(nc.semaphore(name))

        WH = sb("w_hi", [P, NW], F32R)
        WL = sb("w_lo", [D, NW], F32R)
        WRH = sb("wr_hi", [P, P], F32R)
        WRL = sb("wr_lo", [D, P], F32R)
        cols = sb("cols", [P, NCOL])
        rows = sb("rows", [P, NROW])
        ident = sb("ident", [P, P])
        ones = sb("ones", [P, P])
        identb = sb("identb", [P, P], BF16)
        zerob = sb("zerob", [P, P], BF16)
        mask_s = sb("mask_s", [P, P], BF16)
        mask_t = sb("mask_t", [P, P], BF16)
        after = sb("after", [P, P])
        desc = sb("desc", [P, NE])
        h = sb("h", [P, G, D])
        UU = sb("UU", [P, 2, G, D])
        sq = sb("sq", [P, G, D])
        cst = sb("cst", [P, D])
        alone = sb("alone", [1, B, D])
        US = sb("US", [P, B * SP_], F32R)
        stat = sb("stat", [P, 10, G])
        toep = sb("toep", [P, D, D])
        WPH = sb("WPH", [P, NH * D], F32R)
        WPL = sb("WPL", [D, NH * D], F32R)
        w2 = sb("w2", [P, 2, D])
        ew2 = sb("ew2", [P, 2, NE, D])
        b2raw = sb("b2raw", [65, NE * D])
        b2p = sb("b2p", [65, NE * D], BF16)
        onesb = sb("onesb", [P, P], BF16)
        bvT = sb("bvT", [D, NH])
        two = sb("two", [P, D])
        u = UU[:, 1]

        st1 = ExitStack()
        XS = sb("x_split", [P, B * T], F32R, st1)
        WR = sb("w_raw", [P, NW], F32, st1)
        wvT = sb("wvT", [D, NH, 2, D], F32, st1)
        bvrep = sb("bvrep", [D, NH, P], F32, st1)
        wu = sb("wu", [D, NH, D], F32, st1)
        wr_rep = sb("wr_rep", [P, P], F32, st1)
        gam = sb("gam", [P, TT, T], F32, st1)
        tq = sb("tq", [P, T], F32R, st1)
        tk = sb("tk", [P, T], F32R, st1)
        tql = sb("tql", [D, T], F32R, st1)
        tv = sb("tv", [P, TT, D], F32, st1)
        tvs = sb("tvs", [P, TT, 2, D], F32R, st1)
        ptt = sb("ptt", [P, TSLOTS, 512], F32, st1)
        pth = sb("pth", [P, TSLOTS, 512], F32R, st1)
        raw = ExitStack()
        XR = sb("x_raw", [P, B * T], F32, raw)
        raw.close()
        ptl = sb("ptl", [P, TSLOTS, 512], F32R, st1)
        tret = sb("tret", [P, T], F32, st1)
        st1.close()

        st2 = ExitStack()
        VX = sb("VX", [P, B, NT, NH, D + 1], F32, st2)
        qs = [sb(f"qs{b}", [P, SP_], F32R, st2) for b in range(B)]
        ks = [sb(f"ks{b}", [P, SP_], F32R, st2) for b in range(B)]
        ql = [sb(f"ql{b}", [D + 1, SP_], F32R, st2) for b in range(B)]
        kh = [sb(f"kh{b}", [D + 1, SP_], F32R, st2) for b in range(B)]
        vs = [sb(f"vs{b}", [P, NT, D + 1], F32, st2) for b in range(B)]
        ot = sb("ot", [D + 1, 2, CW], F32, st2)
        pt = sb("pt", [P, 6, CW], F32, st2)
        wqk_h = sb("wqk_h", [P, 2, D], F32R, st2)
        wqk_l = sb("wqk_l", [D, 2, D], F32R, st2)
        mpart = sb("mpart", [P, B, NT, 3], F32, st2)
        mneg = sb("mneg", [P, B, NT], F32, st2)
        mrow = [sb(f"mrow{b}", [NT, P], F32R, st2) for b in range(B)]
        rden = sb("rden", [P, 2, TPC], F32, st2)
        onrm = sb("onrm", [P, 2, TPC, D], F32, st2)
        hank = sb("hank", [P, D, D], F32, st2)
        st2.close()

        st3 = ExitStack()
        hT = sb("hT", [P, 2, SP_], F32, st3)
        wbc = sb("wbc", [P, B, SP_], F32, st3)
        above = sb("above", [P, 3, SP_], BF16, st3)
        tie = sb("tie", [P, 3, P], BF16, st3)
        wcol = sb("wcol", [P, B, NT], F32, st3)
        sel = sb("sel", [P, B, NT], F32, st3)
        eh = sb("eh", [P, NE, 2, 256], F32, st3)
        rrow = sb("rrow", [1, B, SP_], F32, st3)
        gT = sb("gT", [NE, B * SP_], F32, st3)
        gate = sb("gate", [P, G, NE], F32, st3)
        eq = sb("eq", [P, G, NE], F32, st3)
        is0 = sb("is0", [P, G, NE], F32, st3)
        is1 = sb("is1", [P, G, NE], F32, st3)
        comb = sb("comb", [P, G, NE], F32, st3)
        yw = sb("yw", [P, 2, NE, D], F32, st3)
        ysum = sb("ysum", [P, 2, D], F32, st3)
        st3.close()

        ps = ctx.enter_context(nc.psum_tensor("ps", [P, 8, 512], F32))

        def a_bank(b, k):
            return ps[:, 4 + (k + b) % 2]

        d_x = [sem(f"d_x{b}") for b in range(B)]
        d_wtok, d_w, d_cols, d_rows, d_txt = (sem(n) for n in ("d_wtok", "d_w", "d_cols", "d_rows", "d_txt"))
        d_gam = [sem(f"d_gam{s}") for s in range(TT)]
        d_wv, d_late, d_two, d_mrow, d_out = (sem(n) for n in ("d_wv", "d_late", "d_two", "d_mrow", "d_out"))
        s_const = sem("s_const")
        s_split1 = sem("s_split1")
        s_wh = sem("s_wh")
        s_split2 = sem("s_split2")
        s_tproj = sem("s_tproj")
        s_tround = sem("s_tround")
        s_tlow = sem("s_tlow")
        s_tv = sem("s_tv")
        s_tsc = sem("s_tsc")
        s_tpt = sem("s_tpt")
        s_tph = sem("s_tph")
        s_tpl = [sem("s_tpl_dve"), sem("s_tpl_pool")]
        s_tpv = sem("s_tpv")
        s_tret = sem("s_tret")
        s_ty = sem("s_ty")
        s_th = sem("s_th")
        s_cen = sem("s_cen")
        s_sq = sem("s_sq")
        s_var = sem("s_var")
        s_sd = sem("s_sd")
        s_u = sem("s_u")
        s_tr = sem("s_tr")
        s_uhi = sem("s_uhi")
        s_us = sem("s_us")
        s_wp = sem("s_wp")
        s_wph = sem("s_wph")
        s_wps = sem("s_wps")
        s_bvr = sem("s_bvr")
        s_cst = sem("s_cst")
        s_v = sem("s_v")
        s_vx = [sem("s_vx_act"), sem("s_vx_dve")]
        s_wsl = sem("s_wsl")
        s_a = sem("s_a")
        s_ar = sem("s_ar")
        s_af = sem("s_af")
        s_kh = sem("s_kh")
        s_mneg = sem("s_mneg")
        s_st = sem("s_st")
        s_vs = sem("s_vs")
        s_ex = sem("s_ex")
        s_pv = sem("s_pv")
        s_of = sem("s_of")
        s_to = sem("s_to")
        s_nf = sem("s_nf")
        s_r = sem("s_r")
        s_wb = sem("s_wb")
        s_gelu = sem("s_gelu")
        s_rd = sem("s_rd")
        s_wt = sem("s_wt")
        s_cmp = sem("s_cmp")
        s_rk = sem("s_rk")
        s_rr = sem("s_rr")
        s_rt = sem("s_rt")
        s_rtf = sem("s_rtf")
        s_skip = sem("s_skip")
        s_cv = sem("s_cv")
        s_cvf = sem("s_cvf")
        s_ush = sem("s_ush")
        s_gt_mm = sem("s_gt_mm")
        s_gt = sem("s_gt")
        s_g = sem("s_g")
        s_gf = sem("s_gf")
        s_d = sem("s_d")
        s_ed = sem("s_ed")
        s_hh = sem("s_hh")
        s_ha = sem("s_ha")
        s_hd = sem("s_hd")
        s_hu = sem("s_hu")
        s_yf = sem("s_yf")
        s_fin = sem("s_fin")
        s_toep = sem("s_toep")
        s_b2 = sem("s_b2")
        s_dve = sem("s_dve")
        s_dvl = sem("s_dvl")
        s_dvm = sem("s_dvm")
        s_pool = sem("s_pool")
        s_step = sem("s_step")

        block = ctx.enter_context(nc.Block())

        @block.sync
        def _(sp):
            for half in range(2):
                sp.dma_start(WR[64 * half:64 * half + 64, 0:O_Q], ins["w64"][:, 0:O_Q]).then_inc(d_wtok, 16)
                sp.dma_start(XR[64 * half:64 * half + 64, 0:T], ins["xT"][:, 0:T]).then_inc(d_x[0], 16)
            for half in range(2):
                sp.dma_start(XR[64 * half:64 * half + 64, T:B * T], ins["xT"][:, T:B * T]).then_inc(d_x[1], 16)
            sp.dma_start(cols[:], ins["cols"]).then_inc(d_cols, 16)
            sp.dma_start(rows[:], ins["rows"].broadcast_to([P, NROW])).then_inc(d_rows, 16)
            for s in range(TT):
                sp.dma_start(gam[:, s, :], ins["gammaT"][P * s:P * s + P, :]).then_inc(d_gam[s], 16)
            for half in range(2):
                sp.dma_start(two[64 * half:64 * half + 64, :], ins["two"]).then_inc(d_two, 16)
            sp.wait_ge(s_const, 1)
            for b in range(B):
                sp.dma_start(h[0:TXT, b * NT + TT, :], ins["txt"][b]).then_inc(d_txt, 16)
            for half in range(2):
                sp.dma_start(WR[64 * half:64 * half + 64, O_Q:NW], ins["w64"][:, O_Q:NW]).then_inc(d_w, 16)
            for half in range(2):
                sp.dma_start(wvT[:, :, half, :], ins["wvT"]).then_inc(d_wv, 16)
            sp.dma_start(bvT[:], ins["bvT"]).then_inc(d_wv, 16)
            sp.dma_start(wu[:], ins["wu"]).then_inc(d_wv, 16)
            sp.dma_start(w2[:], ins["w2"]).then_inc(d_late, 16)
            sp.dma_start(ew2[:], ins["ew2"]).then_inc(d_late, 16)
            for k in range(3):
                sp.dma_start(b2raw[32 * k:32 * k + 1, :], ins["eb2"]).then_inc(d_late, 16)
            sp.wait_ge(s_th, B)
            sp.wait_ge(s_split2, 1)
            sp.wait_ge(s_wps, 2)
            sp.dma_start(hank[:], bass.AP(ins["cpad"].tensor, 0, [[1, P], [3 * D, D], [1, D]])).then_inc(d_late, 16)

            def put_mrow(v, b):
                sp.wait_ge(s_af, NA * (v + 1) + 2)
                sp.dma_start(ql[b][D:D + 1, :].bitcast(F32).rearrange("o (t p) -> o t p", p=P),
                             mrow[b][:].bitcast(F32)).then_inc(d_mrow, 16)

            put_mrow(0, 0)
            put_mrow(1, 1)
            with sp.Fori(0, NH - 1) as i:
                put_mrow(2 * i + 2, 0)
                put_mrow(2 * i + 3, 1)

            for b in range(B):
                sp.wait_ge(s_fin, -(-(b * NT + TT) // 2))
                sp.dma_start(out[b, 0:T, :].rearrange("(t p) d -> p t d", p=P),
                             h[:, b * NT:b * NT + TT, :]).then_inc(d_out, 16)
                sp.wait_ge(s_fin, -(-(b * NT + NT) // 2))
                sp.dma_start(out[b, T:S, :], h[0:TXT, b * NT + TT, :]).then_inc(d_out, 16)
            sp.wait_ge(d_out, 16 * 2 * B)

        @block.gpsimd
        def _(pool):
            n = [0]

            def link(instruction):
                n[0] += 1
                instruction.then_inc(s_pool, 1)
                pool.wait_ge(s_pool, n[0])

            nc.gpsimd.memset(h[:, TT:G:NT, :], 0.0).then_inc(s_const, 1)
            link(nc.gpsimd.memset(ones[:], 1.0))
            link(nc.gpsimd.memset(zerob[:], 0.0))
            link(nc.gpsimd.affine_select(out=ident[:], in_=ones[:], compare_op=ALU.is_equal, fill=0.0,
                                         base=0, pattern=[[-1, P]], channel_multiplier=1))
            link(nc.gpsimd.affine_select(out=mask_s[:], in_=zerob[:], compare_op=ALU.is_gt, fill=NEG,
                                         base=0, pattern=[[-1, P]], channel_multiplier=1))
            link(nc.gpsimd.affine_select(out=mask_t[:], in_=zerob[:], compare_op=ALU.is_gt, fill=NEG,
                                         base=0, pattern=[[1, P]], channel_multiplier=-1))
            link(nc.gpsimd.affine_select(out=after[:], in_=ones[:], compare_op=ALU.is_gt, fill=0.0,
                                         base=0, pattern=[[1, P]], channel_multiplier=-1))
            for e in range(NE):
                nc.gpsimd.memset(desc[:, e:e + 1], float(NE - e))
            link(nc.gpsimd.tensor_copy(identb[:], ident[:]))
            link(nc.gpsimd.memset(onesb[:], 1.0))
            nc.gpsimd.memset(b2p[:], 0.0).then_inc(s_const, 1)
            for m in range(B * NB):
                if m % 3:
                    pool.wait_ge(s_tph, m + 1)
                    if m >= TSLOTS:
                        pool.wait_ge(s_tpv, m - TSLOTS + 1)
                    nc.gpsimd.tensor_tensor(ptl[:, m % TSLOTS], ptt[:, m % TSLOTS], pth[:, m % TSLOTS],
                                            ALU.subtract).then_inc(s_tpl[1], 1)
            pool.wait_ge(s_wh, 1)
            nc.gpsimd.tensor_tensor(WL[:, O_Q:O_WR], WR[0:D, O_Q:O_WR], WH[0:D, O_Q:O_WR],
                                    ALU.subtract).then_inc(s_split2, 1)

            pool.wait_ge(s_th, B)
            pool.wait_ge(s_wps, 2)
            pool.wait_ge(s_cen, 1)
            for b in range(B):
                link(nc.gpsimd.memset(kh[b][D:D + 1, :].bitcast(F32), 1.0))
            link(nc.gpsimd.memset(VX[:, :, :, :, D:D + 1], 1.0))

            def slices(hd, guard):
                if guard is not None:
                    pool.wait_ge(s_a, guard)
                    pool.sem_inc(s_step, 1)
                for k, off in enumerate((O_Q, O_K)):
                    nc.gpsimd.tensor_copy(wqk_h[:, k], WH[:, bass.ds(hd * D + off, D)]).then_inc(s_wsl, 1)
                    nc.gpsimd.tensor_copy(wqk_l[:, k], WL[:, bass.ds(hd * D + off, D)]).then_inc(s_wsl, 1)

            def copy_keys(v, b, before=None):
                pool.wait_ge(s_ar, NC * (v + 1))
                if before is None:
                    pool.wait_ge(s_vs, v + 1)
                else:
                    pool.wait_ge(*before)
                pool.sem_inc(s_step, 1)
                nc.gpsimd.tensor_copy(kh[b][0:D, :], ks[b][D:P, :]).then_inc(s_kh, 1)
                pool.wait_ge(s_kh, v + 1)
                pool.sem_inc(s_step, 1)

            def copy_values(v, b):
                pool.wait_ge(s_pv, NS * (v - 1) + 6)
                pool.sem_inc(s_step, 1)
                nc.gpsimd.tensor_copy(vs[b][:], VX[:, b, :, bass.ds(head_of[0], 1), :]
                                      .rearrange("p t o d -> p t (o d)")).then_inc(s_vs, 1)

            head_of = [0]
            slices(0, None)
            pool.wait_ge(s_cen, B)
            for b in range(B):
                link(nc.gpsimd.tensor_tensor(alone[:, b], h[0:1, b * NT, :], rows[0:1, R_BU:R_BU + D], ALU.add))
            nc.gpsimd.tensor_tensor(h[:], h[:], cst[:].unsqueeze(1).broadcast_to([P, G, D]),
                                    ALU.add).then_inc(s_cst, 1)
            copy_keys(0, 0, before=(s_cst, 1))
            pool.wait_ge(s_vx[0], G - len(V_ON_DVE))
            pool.wait_ge(s_vx[1], len(V_ON_DVE))
            for b in range(B):
                nc.gpsimd.tensor_copy(vs[b][:], VX[:, b, :, 0, :]).then_inc(s_vs, 1)
            copy_keys(1, 1)
            with pool.Fori(0, NH - 1) as i:
                head_of[0] = i + 1
                slices(i + 1, NA * (2 * i + 1) + NC)
                copy_values(2 * i + 2, 0)
                copy_keys(2 * i + 2, 0)
                copy_values(2 * i + 3, 1)
                copy_keys(2 * i + 3, 1)

            pool.wait_ge(d_late, 16 * 6)
            nc.gpsimd.tensor_copy(toep[:], hank[:, :, ::-1]).then_inc(s_toep, 1)
            pool.wait_ge(s_toep, 1)
            for k in range(3):
                r = slice(32 * k, 32 * k + 1)
                for _ in range(k):
                    link(nc.gpsimd.tensor_copy(b2p[r], b2raw[r]))
                    link(nc.gpsimd.tensor_tensor(b2raw[r], b2raw[r], b2p[r], ALU.subtract))
                nc.gpsimd.tensor_copy(b2p[r], b2raw[r]).then_inc(s_b2, 1)
                pool.wait_ge(s_b2, k + 1)

            for b in range(B):
                pool.wait_ge(s_u, B + b + 1)
                g = slice(b * NT, b * NT + NT)
                nc.gpsimd.tensor_tensor(h[:, g], h[:, g], u[:, g], ALU.add).then_inc(s_skip, 1)

        @block.scalar
        def _(act):
            act.wait_ge(d_cols, 16)

            def token_roundings(b):
                for i in range(4):
                    act.wait_ge(s_tproj, 5 * b + TPROJ.index(TORDER[i]) + 1)
                    k = TORDER[i]
                    dst = (tq if k < 2 else tk)[:, 512 * (k % 2):512 * (k % 2) + 512]
                    bias = cols[:, C_TBQ:C_TBQ + 1] if k < 2 else cols[:, C_TBK:C_TBK + 1]
                    nc.scalar.activation(dst, ps[:, k, :], ACT.Identity, bias=bias).then_inc(s_tround, 1)

            token_roundings(0)
            for b in range(B):
                for m in range(NB * b, NB * b + NB):
                    act.wait_ge(s_tpt, m + 1)
                    if m >= TSLOTS:
                        act.wait_ge(s_tpv, m - TSLOTS + 1)
                    nc.scalar.activation(pth[:, m % TSLOTS], ptt[:, m % TSLOTS], ACT.Copy).then_inc(s_tph, 1)
                act.wait_ge(s_tpv, NB * (b + 1))
                for k in range(2):
                    nc.scalar.activation(tret[:, 512 * k:512 * k + 512], ps[:, k, :], ACT.Copy).then_inc(s_tret, 1)
                if b == 0:
                    token_roundings(1)
                    act.wait_ge(d_wv, 64)
                    nc.scalar.activation(bvrep[:], bvT[:].unsqueeze(2).broadcast_to([D, NH, P]),
                                         ACT.Copy).then_inc(s_bvr, 1)
                    act.wait_ge(s_wp, 1)
                    nc.scalar.activation(WPH[:], ps[:, 2, :], ACT.Copy).then_inc(s_wph, 1)
            act.wait_ge(d_w, 32)
            nc.scalar.activation(WH[:, O_Q:O_WR], WR[:, O_Q:O_WR], ACT.Copy).then_inc(s_wh, 1)

            def squares(k, b):
                act.wait_ge(s_cen, B * k + b + 1)
                g = slice(b * NT, b * NT + NT)
                nc.scalar.activation(sq[:, g], u[:, g], ACT.Square).then_inc(s_sq, 1)

            def root(k):
                act.wait_ge(s_var, k + 1)
                nc.scalar.activation(stat[:, 3], stat[:, 2], ACT.Sqrt).then_inc(s_sd, 1)

            def squares_and_root(k):
                for b in range(B):
                    squares(k, b)
                root(k)

            def high(k):
                for c in range(NC):
                    b, m = k % 2, NC * k + c
                    act.wait_ge(s_tr, m + 1)
                    nc.scalar.activation(US[0:D, b * SP_ + CW * c:b * SP_ + CW * c + CW], ps[0:D, c, 0:CW],
                                         ACT.Copy).then_inc(s_uhi, 1)

            squares_and_root(0)
            high(0)
            high(1)

            def rounding(v, b, k):
                act.wait_ge(s_a, NA * v + k + 1)
                act.sem_inc(s_step, 1)
                cs = slice(CW * k, CW * k + CW)
                for half, dst, col in ((slice(0, D), qs, C_BQ), (slice(D, P), ks, C_BK)):
                    last = nc.scalar.activation(dst[b][half, cs], a_bank(b, k)[half, 0:CW], ACT.Identity,
                                                bias=cols[half, bass.ds(col + head_of[0], 1)])
                last.then_inc(s_ar, 1)

            def exp(w, s):
                c, j = STEPS[s]
                lo = max(P * j, CW * c) - CW * c
                act.wait_ge(s_st, NS * w + s + 1)
                act.wait_ge(s_pv, NS * w + s + 1)
                nc.scalar.activation(pt[:, s % 6, lo:CW], ps[:, s % 3, lo:CW],
                                     ACT.Exp, scale=D ** -0.5).then_inc(s_ex, 1)

            def copy_output(w, b, c):
                o = (c + NC * b) % 2
                act.wait_ge(s_pv, NS * w + LAST[c] + 1 + 6)
                act.wait_ge(s_to, NC * w + c + 1)
                nc.scalar.activation(ot[:, o, :], ps[0:D + 1, 6 + o, 0:CW], ACT.Copy).then_inc(s_of, 1)

            def slot(w, b, first=False, follow=True):
                for s in range(NS):
                    if follow:
                        for k in PROJECT_AT.get(s, ()):
                            rounding(w + 1, 1 - b, k)
                    exp(w, s)
                    for c in range(NC):
                        if COPY_AT[c] == s:
                            copy_output(w, b, c)
                        if COPY_AT[c] == s + NS and not first:
                            copy_output(w - 1, 1 - b, c)
                    if not follow and s == EARLY_LN:
                        squares(1, 0)

            head_of = [0]
            act.sem_inc(s_ex, 3)
            act.sem_inc(s_of, 2)
            for k in range(G):
                if k < NC:
                    rounding(0, 0, k)
                if k not in V_ON_DVE:
                    act.wait_ge(s_v, k + 1)
                    nc.scalar.activation(VX[:, k // NT, k % NT, :, 0:D], ps[:, V_BANKS[k % 3], :]
                                         .rearrange("p (h d) -> p h d", d=D), ACT.Copy).then_inc(s_vx[0], 1)
            slot(0, 0, first=True)
            with act.Fori(0, NH - 1) as i:
                head_of[0] = i + 1
                slot(2 * i + 1, 1)
                slot(2 * i + 2, 0)
            slot(2 * NH - 1, 1, follow=False)
            copy_output(2 * NH - 1, 1, NC - 1)

            squares(1, 1)
            root(1)
            for b in range(B):
                high(2 + b)
            for k in range(B * NC):
                act.wait_ge(s_r, k + 1)
                nc.scalar.activation(wbc[:, k // NC, CW * (k % NC):CW * (k % NC) + CW], ps[:, 3 + k % 4, 0:CW],
                                     ACT.Identity, bias=cols[:, C_BR:C_BR + 1]).then_inc(s_wb, 1)
            for b in range(B):
                for k in range(2 * NC):
                    m, c = divmod(k, NC)
                    item = B * NC + 3 * NC * b + k
                    act.wait_ge(s_r, item + 1)
                    nc.scalar.activation(hT[:, m, CW * c:CW * c + CW], ps[:, 3 + item % 4, 0:CW],
                                         ACT.Gelu_apprx_tanh,
                                         bias=cols[:, C_B1 + m:C_B1 + m + 1]).then_inc(s_gelu, 1)
                act.wait_ge(s_rk, NT * (b + 1))
                for c in range(NC):
                    nc.scalar.activation(rrow[:, b, CW * c:CW * c + CW], ps[0:1, c, 0:CW], ACT.Copy).then_inc(s_rr, 1)
            squares_and_root(2)
            squares_and_root(3)
            act.sem_inc(s_ha, 2)
            for b in range(B):
                high(4 + b)
            for k, bank in enumerate(GATE_BANKS):
                act.wait_ge(s_gt_mm, k + 1)
                cs = slice(512 * k, min(512 * k + 512, B * SP_))
                nc.scalar.activation(gT[:, cs], ps[0:NE, bank, 0:cs.stop - cs.start], ACT.Copy).then_inc(s_gt, 1)

            def relu(t, e):
                act.wait_ge(s_hh, NE * t + e + 1)
                act.wait_ge(s_hu, NE * t + e + 1)
                for m in range(2):
                    ins_ = nc.scalar.activation(eh[:, e, m, :], ps[:, 4 + e % 4, 256 * m:256 * m + 256], ACT.Relu,
                                                bias=cols[:, C_EB1 + 2 * e + m:C_EB1 + 2 * e + m + 1])
                ins_.then_inc(s_ha, 1)

            for e in range(0, NE, 2):
                relu(0, e)
            act.wait_ge(s_d, 1)
            nc.scalar.activation(stat[:, 5, :], stat[:, 4, :], ACT.Exp).then_inc(s_ed, 1)
            with act.Fori(0, G // 2 - 1) as t:
                for e in range(0, NE, 2):
                    relu(t + 1, e)

        @block.tensor
        def _(pe):
            mm = nc.tensor.matmul

            def split2(dst, hi2, split, lo, split_hi, start, stop):
                mm(dst, hi2, split, start=start, stop=False)
                return mm(dst, lo, split_hi, start=False, stop=stop)

            def token_projections(b):
                x0 = b * T
                for k in TPROJ:
                    if k == "v":
                        for t in range(TT):
                            cs = slice(x0 + P * t, x0 + P * t + P)
                            last = split2(ps[:, 7, D * t:D * t + D], XS[:, cs], WH[:, O_TV:O_TV + D],
                                          XS[0:D, cs], WL[:, O_TV:O_TV + D], t == 0, t == TT - 1)
                        last.then_inc(s_tproj, 1)
                        continue
                    if b and k < 2:
                        pe.wait_ge(s_tret, 2 * b)
                    off = O_TQ if k < 2 else O_TK
                    cs = slice(x0 + 512 * (k % 2), x0 + 512 * (k % 2) + 512)
                    split2(ps[:, k, :], WH[:, off:off + P], XS[:, cs], WL[:, off:off + P], XS[0:D, cs],
                           True, True).then_inc(s_tproj, 1)

            pe.wait_ge(s_split1, 2)
            token_projections(0)
            for b in range(B):
                pe.wait_ge(s_tlow, 4 * (b + 1))

                def retain(n):
                    m = NB * b + n
                    bank, v_parts = ps[:, n % 2, :], tvs[:, n // 2].rearrange("p i d -> p (i d)")
                    pe.wait_ge(s_tph, m + 1)
                    mm(bank, v_parts, pth[:, m % TSLOTS], start=n < 2, stop=False)
                    engine, count = lows(m)
                    pe.wait_ge(s_tpl[engine], count)
                    mm(bank, v_parts, ptl[:, m % TSLOTS], start=False, stop=n >= NB - 2).then_inc(s_tpv, 1)

                for n in range(16):
                    m = 16 * b + n
                    s, half = n // 2, n % 2
                    if m >= 3:
                        pe.wait_ge(s_tpt, m - 2)
                    if n < 3 and m % 3 == 2:
                        pe.wait_ge(s_tv, b + 1)
                    ss, hs = slice(P * s, P * s + P), slice(512 * half, 512 * half + 512)
                    split2(ps[:, 5 + m % 3, :], tk[:, ss], tq[:, hs], tk[0:D, ss], tql[:, hs],
                           True, True).then_inc(s_tsc, 1)
                    if n >= TLAG:
                        retain(n - TLAG)
                for n in range(NB - TLAG, NB):
                    retain(n)
                if b == 0:
                    pe.wait_ge(s_tpt, NB)
                    pe.wait_ge(s_split1, 4)
                    token_projections(1)
                pe.wait_ge(s_tret, 2 * (b + 1))
                if b:
                    pe.wait_ge(s_th, b)
                pe.wait_ge(d_two, 32)
                for t in range(TT):
                    last = mm(ps[:, 4, D * t:D * t + D], tret[:, P * t:P * t + P], two[:],
                              start=t == 0, stop=t == TT - 1)
                last.then_inc(s_ty, 1)
                if b == 0:
                    pe.wait_ge(d_wv, 64)
                    pe.wait_ge(s_bvr, 1)
                    pe.wait_ge(s_tlow, 6)
                    for hd in range(NH):
                        mm(ps[:, 2, D * hd:D * hd + D], wvT[:, hd], wu[:, hd, :], start=hd == 0, stop=hd == NH - 1)
                    for hd in range(NH):
                        last = mm(ps[:, 3, 0:D], bvrep[:, hd, :], wu[:, hd, :], start=hd == 0, stop=hd == NH - 1)
                    last.then_inc(s_wp, 1)

            def turn(k):
                for c in range(NC):
                    pe.wait_ge(s_u, k + 1 if k < 4 else k + 3)
                    if k:
                        pe.wait_ge(s_us, NC * (k - 1) + c + 1)
                    for t in range(TPC):
                        last = nc.tensor.transpose(ps[0:D, c, P * t:P * t + P], u[:, (k % 2) * NT + TPC * c + t, :], ident[:])
                    last.then_inc(s_tr, 1)

            pe.wait_ge(s_th, B)
            pe.wait_ge(s_wps, 2)
            pe.wait_ge(s_const, 2)
            turn(0)
            turn(1)

            def values(n):
                pe.wait_ge(s_us, NC * (n // NT) + n % NT // TPC + 1)
                if n >= 3:
                    engine, count = v_taken(n - 3)
                    pe.wait_ge(s_vx[engine], count)
                cs = slice(n * P, n * P + P)
                split2(ps[:, V_BANKS[n % 3], :], US[:, cs], WPH[:], US[0:D, cs], WPL[:], True, True).then_inc(s_v, 1)

            pe.sem_inc(s_pv, 6)
            pe.sem_inc(s_to, 2)

            def project(v, b, k):
                if k == 0:
                    pe.wait_ge(s_wsl, 4 * (head_of[0] + 1))
                pe.wait_ge(s_af, NA * v + k + 1)
                cs = slice(b * SP_ + CW * k, b * SP_ + CW * k + CW)
                split2(a_bank(b, k)[:, 0:CW], wqk_h[:].rearrange("p i d -> p (i d)"), US[:, cs],
                       wqk_l[:].rearrange("p i d -> p (i d)"), US[0:D, cs], True, True).then_inc(s_a, 1)

            def scores_for_max(v, b, k):
                i, a, z = SMAX[k]
                if k == 0:
                    pe.wait_ge(s_af, NA * v + NC + 2)
                pe.wait_ge(s_af, NA * v + NC + k + 1)
                bank = a_bank(b, NC + k)
                diag = z == P * (i + 1)
                last = mm(bank[:, 0:z - a], qs[b][:, P * i:P * i + P], ks[b][:, a:z], start=True, stop=not diag)
                if diag:
                    last = mm(bank[:, z - a - P:z - a], identb[:], mask_s[:], start=False, stop=True)
                last.then_inc(s_a, 1)

            def turn_max(v, b):
                pe.wait_ge(s_af, NA * v + NA)
                pe.wait_ge(s_mneg, v + 1)
                nc.tensor.transpose(a_bank(b, NA - 1)[0:NT, 0:P], mneg[:, b], ident[:]).then_inc(s_a, 1)

            def scores(w, b, s):
                c, j = STEPS[s]
                lo = max(P * j, CW * c)
                z = CW * (c + 1)
                bank = ps[:, s % 3]
                if s == 0:
                    pe.wait_ge(d_mrow, 16 * (w + 1))
                    pe.wait_ge(s_kh, w + 1)
                pe.wait_ge(s_ex, NS * w + s + 1)
                dst = bank[:, lo - CW * c:CW]
                js = slice(P * j, P * j + P)
                mm(dst, ks[b][:, js], qs[b][:, lo:z], start=True, stop=False)
                last = mm(dst, kh[b][:, js], ql[b][:, lo:z], start=False, stop=j < TPC * c)
                if j >= TPC * c:
                    last = mm(bank[:, lo - CW * c:lo - CW * c + P], identb[:], mask_t[:], start=False, stop=True)
                last.then_inc(s_st, 1)

            def weigh(w, b, s):
                c, j = STEPS[s]
                o = (c + NC * b) % 2
                lo = max(P * j, CW * c) - CW * c
                pe.wait_ge(s_ex, NS * w + s + 4)
                if s == 0:
                    pe.wait_ge(s_vs, w + 1)
                if j == 0:
                    pe.wait_ge(s_of, NC * w + c + 1)
                mm(ps[0:D + 1, 6 + o, lo:CW], vs[b][:, j, :], pt[:, s % 6, lo:CW], start=j == 0,
                   stop=s == LAST[c]).then_inc(s_pv, 1)

            def turn_back(w, b, c):
                o = (c + NC * b) % 2
                pe.wait_ge(s_of, NC * w + c + 3)
                pe.wait_ge(s_nf, NC * w + c + 1)
                for r in range(TPC):
                    last = nc.tensor.transpose(ps[:, 3, (D + 1) * r:(D + 1) * (r + 1)], ot[:, o, P * r:P * r + P],
                                               ident[0:D + 1, 0:D + 1])
                last.then_inc(s_to, 1)

            def slot(w, b, first=False, follow=True):
                for s in range(NS):
                    if s:
                        scores(w, b, s)
                    if follow:
                        for k in PROJECT_AT.get(s, ()):
                            project(w + 1, 1 - b, k)
                        for k in MAX_AT.get(s, ()):
                            scores_for_max(w + 1, 1 - b, k)
                        if s == TURN_MAX_AT:
                            turn_max(w + 1, 1 - b)
                    if s >= LAG:
                        weigh(w, b, s - LAG)
                    elif not first:
                        weigh(w - 1, 1 - b, s - LAG + NS)
                    if s == 0:
                        scores(w, b, s)
                    for c in range(NC):
                        if BACK_AT[c] == s:
                            turn_back(w, b, c)
                        if BACK_AT[c] == s + NS and not first:
                            turn_back(w - 1, 1 - b, c)

            head_of = [0]
            pe.wait_ge(s_split2, 1)
            pe.wait_ge(s_us, NC)
            for k in range(NA):
                if k < NC:
                    project(0, 0, k)
                elif k < NC + NM:
                    scores_for_max(0, 0, k - NC)
                else:
                    turn_max(0, 0)
                if k < G:
                    values(k)
            pe.wait_ge(s_vx[0], G - len(V_ON_DVE))
            pe.wait_ge(s_vx[1], len(V_ON_DVE))
            slot(0, 0, first=True)
            with pe.Fori(0, NH - 1) as i:
                head_of[0] = i + 1
                slot(2 * i + 1, 1)
                slot(2 * i + 2, 0)
            slot(2 * NH - 1, 1, follow=False)
            for s in range(NS - LAG, NS):
                weigh(2 * NH - 1, 1, s)
            turn_back(2 * NH - 1, 1, NC - 1)

            turn(2)
            turn(3)
            pe.wait_ge(d_late, 16 * 6)

            def free_bank(item):
                old = item - 4
                if 0 <= old < B * NC:
                    pe.wait_ge(s_wb, old + 1)
                elif old >= 0:
                    b, k = divmod(old - B * NC, 3 * NC)
                    if k < 2 * NC:
                        pe.wait_ge(s_gelu, 2 * NC * b + k + 1)
                    else:
                        pe.wait_ge(s_rd, NC * b + k - 2 * NC + 1)
                return ps[:, 3 + item % 4, 0:CW]

            for k in range(B * NC):
                pe.wait_ge(s_us, B * NC + k + 1)
                cs = slice(CW * k, CW * k + CW)
                split2(free_bank(k), WRH[:], US[:, cs], WRL[:], US[0:D, cs], True, True).then_inc(s_r, 1)
            for b in range(B):
                pe.wait_ge(s_wb, NC * (b + 1))
                for t in range(NT):
                    last = nc.tensor.transpose(ps[:, 7, NT * b + t:NT * b + t + 1], wbc[0:1, b, P * t:P * t + P],
                                               ident[0:1, 0:1])
                last.then_inc(s_wt, 1)

            def rank(b, t):
                k = min(P, S - P * t)
                pe.wait_ge(s_cmp, NT * b + t + 1)
                sl = (NT * b + t) % 3
                if b and t == 0:
                    pe.wait_ge(s_rr, NC * b)
                for c in range(NC):
                    mm(ps[0:1, c, 0:CW], onesb[0:k, 0:1], above[0:k, sl, CW * c:CW * c + CW],
                       start=t == 0, stop=t == NT - 1, skip_group_check=True)
                mm(ps[0:1, t // TPC, P * (t % TPC):P * (t % TPC) + P], onesb[0:k, 0:1], tie[0:k, sl, :],
                   start=False, stop=t == NT - 1, skip_group_check=True).then_inc(s_rk, 1)

            def turn_ranks(b):
                pe.wait_ge(s_rr, NC * (b + 1))
                if b:
                    pe.wait_ge(s_rtf, b)
                for t in range(NT):
                    last = nc.tensor.transpose(ps[:, 7, G + NT * b + t:G + NT * b + t + 1],
                                               rrow[:, b, P * t:P * t + P], ident[0:1, 0:1])
                last.then_inc(s_rt, 1)

            def ffn_hidden(b, k):
                m, c = divmod(k, NC)
                bank = free_bank(B * NC + 3 * NC * b + k)
                cs = slice(b * SP_ + CW * c, b * SP_ + CW * c + CW)
                ws = slice(O_W1 + P * m, O_W1 + P * m + P)
                split2(bank, WH[:, ws], US[:, cs], WL[:, ws], US[0:D, cs], True, True).then_inc(s_r, 1)

            for b in range(B):
                for t in range(NT):
                    if t < 2 * NC:
                        ffn_hidden(b, t)
                    rank(b, t)
                    if b and t == 3:
                        turn_ranks(b - 1)
                for c in range(NC):
                    bank = free_bank(B * NC + 3 * NC * b + 2 * NC + c)
                    pe.wait_ge(s_gelu, 2 * NC * b + NC + c + 1)
                    for i in range(TPC):
                        for m in range(2):
                            ts = slice(P * (TPC * c + i), P * (TPC * c + i) + P)
                            last = mm(bank[:, D * i:D * i + D], hT[:, m, ts], w2[:, m, :],
                                      start=(i == 0 and m == 0), stop=(i == TPC - 1 and m == 1), skip_group_check=True)
                    last.then_inc(s_r, 1)
                    if b and c == 1:
                        turn_ranks(b)

            pe.wait_ge(s_ush, B)
            pe.wait_ge(s_toep, 1)
            for ch in range(D):
                k, r = divmod(ch, 14)
                if r == 0 and k >= 3:
                    pe.wait_ge(s_rd, B * NC)
                last = mm(ps[0:D, k, 2 * G * r:2 * G * (r + 1)], toep[:, ch, :], UU[:, :, :, ch],
                          start=r == 0, stop=(r == 13 or ch == D - 1), skip_group_check=True)
                if r == 13 or ch == D - 1:
                    last.then_inc(s_cv, 1)

            pe.wait_ge(s_cvf, 10)
            turn(4)
            turn(5)
            pe.wait_ge(s_us, NC * 6)
            pe.sem_inc(s_hu, NE)
            relu_done = (s_ha, s_hd)

            def hidden(t, e, guard=False):
                if guard:
                    pe.wait_ge(s_gt, len(GATE_BANKS))
                tokens = bass.ds(t * 256, 256)
                pe.wait_ge(relu_done[e % 2], (NE // 2) * t + e // 2 + 1)
                for m in range(2):
                    ws = slice(O_E + HID * e + P * m, O_E + HID * e + P * m + P)
                    last = split2(ps[:, 4 + e % 4, 256 * m:256 * m + 256], WH[:, ws], US[:, tokens], WL[:, ws],
                                  US[0:D, tokens], m == 0, m == 1)
                last.then_inc(s_hh, 1)

            def down(t, e, y):
                pe.wait_ge(relu_done[e % 2], (NE // 2) * t + e // 2 + 3)
                for r in range(2):
                    for m in range(2):
                        last = mm(ps[:, 2 * y + r, D * e:D * e + D], eh[:, e, m, P * r:P * r + P], ew2[:, m, e, :],
                                  start=False, stop=(e == NE - 1 and m == 1), skip_group_check=True)
                last.then_inc(s_hu, 1)

            def bias_rows(t, y):
                pe.wait_ge(s_yf, t + 1)
                for r in range(2):
                    mm(ps[:, 2 * y + r, :], onesb[0:65], b2p[:], start=True, stop=False, skip_group_check=True)

            def hiddens(t, first=False):
                for e in range(NE):
                    hidden(t, e, guard=first and e == 3)

            def downs(t, y):
                bias_rows(t, y)
                for e in range(NE):
                    down(t, e, y)

            for k, bank in enumerate(GATE_BANKS):
                cs = slice(512 * k, min(512 * k + 512, B * SP_))
                split2(ps[0:NE, bank, 0:cs.stop - cs.start], WH[:, O_G:O_G + NE], US[:, cs], WL[:, O_G:O_G + NE],
                       US[0:D, cs], True, True).then_inc(s_gt_mm, 1)
            hiddens(0, first=True)
            for g in range(G):
                if g % 4 == 0:
                    pe.wait_ge(s_gt, g // 4 + 1)
                last = nc.tensor.transpose(ps[:, 3, NE * g:NE * g + NE], gT[:, P * g:P * g + P], ident[0:NE, 0:NE])
            last.then_inc(s_g, 1)
            pe.wait_ge(s_b2, 3)
            downs(0, 0)
            with pe.Fori(0, G // 4) as i:
                for y in range(1, 3):
                    hiddens(2 * i + y)
                    downs(2 * i + y, y % 2)

        @block.vector
        def _(dve):
            n = [0]
            tt, ts, stt = nc.vector.tensor_tensor, nc.vector.tensor_scalar, nc.vector.scalar_tensor_tensor

            def link(instruction):
                n[0] += 1
                instruction.then_inc(s_dve, 1)
                dve.wait_ge(s_dve, n[0])

            def wide(col, k):
                return col.unsqueeze(2).broadcast_to([P, k, D])

            def split_weights(a, z):
                link(nc.vector.tensor_copy(WH[:, a:z], WR[:, a:z]))
                link(tt(WL[:, a:z], WR[0:D, a:z], WH[0:D, a:z], ALU.subtract))

            dve.wait_ge(d_wtok, 32)
            split_weights(0, O_Q)
            for b in range(B):
                dve.wait_ge(d_x[b], 32)
                xb = slice(T * b, T * b + T)
                nc.vector.tensor_copy(XS[:, xb], XR[:, xb]).then_inc(s_split1, 1)
                dve.wait_ge(s_split1, 2 * b + 1)
                tt(XS[D:P, xb], XR[D:P, xb], XS[D:P, xb], ALU.subtract).then_inc(s_split1, 1)
            dve.wait_ge(d_rows, 16)
            dve.wait_ge(d_cols, 16)

            def token_lows(b):
                for i in range(4):
                    dve.wait_ge(s_tround, 4 * b + i + 1)
                    k = TORDER[i]
                    cs = slice(512 * (k % 2), 512 * (k % 2) + 512)
                    if k < 2:
                        stt(tql[:, cs], ps[0:D, k, :], cols[0:D, C_TBQ:C_TBQ + 1], tq[0:D, cs], ALU.add,
                            ALU.subtract).then_inc(s_tlow, 1)
                    else:
                        stt(tk[D:P, cs], ps[D:P, k, :], cols[D:P, C_TBK:C_TBK + 1], tk[D:P, cs], ALU.add,
                            ALU.subtract).then_inc(s_tlow, 1)
                dve.wait_ge(s_tproj, 5 * b + TPROJ.index("v") + 1)
                link(tt(tv[:], ps[:, 7, :].rearrange("p (t d) -> p t d", d=D),
                        rows[:, R_TBV:R_TBV + D].unsqueeze(1).broadcast_to([P, TT, D]), ALU.add))
                link(nc.vector.tensor_copy(tvs[:, :, 0], tv[:]))
                tt(tvs[:, :, 1], tv[:], tvs[:, :, 0], ALU.subtract).then_inc(s_tv, 1)

            def block_low(m):
                dve.wait_ge(s_tph, m + 1)
                if m >= TSLOTS:
                    dve.wait_ge(s_tpv, m - TSLOTS + 1)
                tt(ptl[:, m % TSLOTS], ptt[:, m % TSLOTS], pth[:, m % TSLOTS], ALU.subtract).then_inc(s_tpl[0], 1)

            token_lows(0)
            for b in range(B):
                for k in range(NB):
                    m = NB * b + k
                    s, half = k // 2, k % 2
                    if b == 0 and half == 0:
                        dve.wait_ge(d_gam[s], 16)
                    dve.wait_ge(s_tsc, m + 1)
                    if m >= TSLOTS:
                        engine, count = lows(m - TSLOTS)
                        dve.wait_ge(s_tpl[engine], count)
                    tt(ptt[:, m % TSLOTS], ps[:, 5 + m % 3, :], gam[:, s, 512 * half:512 * half + 512],
                       ALU.mult).then_inc(s_tpt, 1)
                    if k and (m - 1) % 3 == 0:
                        block_low(m - 1)
                if m % 3 == 0:
                    block_low(m)
                if b == 0:
                    token_lows(1)
                dve.wait_ge(s_ty, b + 1)
                hb, yb = h[:, b * NT:b * NT + TT, :], sq[:, 0:TT, :]
                link(tt(yb, ps[:, 4, :].rearrange("p (t d) -> p t d", d=D),
                        rows[:, R_TBO:R_TBO + D].unsqueeze(1).broadcast_to([P, TT, D]), ALU.add))
                link(ts(hb, yb, 0.0, cols[:, C_A:C_A + 1], ALU.min, ALU.mult))
                stt(hb, yb, 0.0, hb, ALU.max, ALU.add).then_inc(s_th, 1)
                dve.wait_ge(s_th, b + 1)
                if b == 0:
                    dve.wait_ge(s_wp, 1)
                    tt(cst[:], ps[:, 3, 0:D], rows[:, R_BU:R_BU + D], ALU.add).then_inc(s_wps, 1)
                    dve.wait_ge(s_wph, 1)
                    tt(WPL[:], ps[0:D, 2, :], WPH[0:D, :], ALU.subtract).then_inc(s_wps, 1)

            def centre(k, batches):
                g = slice(batches[0] * NT, batches[-1] * NT + NT)
                link(nc.vector.tensor_reduce(stat[:, 0, g], h[:, g], AX.X, ALU.add))
                link(ts(stat[:, 1, g], stat[:, 0, g], -1.0 / D, None, ALU.mult))
                for b in batches:
                    g = slice(b * NT, b * NT + NT)
                    tt(u[:, g], h[:, g], wide(stat[:, 1, g], NT), ALU.add).then_inc(s_cen, 1)

            def spread(k, batches):
                for b in batches:
                    g = slice(b * NT, b * NT + NT)
                    dve.wait_ge(s_sq, B * k + b + 1)
                    nc.vector.tensor_reduce(stat[:, 9, g], sq[:, g], AX.X, ALU.add).then_inc(s_dve, 1)
                    n[0] += 1
                dve.wait_ge(s_dve, n[0])

            def normalise(k):
                st = [stat[:, r] for r in range(10)]
                ts(st[2], st[9], 1.0 / D, EPS, ALU.mult, ALU.add).then_inc(s_var, 1)
                dve.wait_ge(s_var, k + 1)
                dve.wait_ge(s_sd, k + 1)
                link(nc.vector.reciprocal(st[6], st[3]))
                link(tt(st[7], st[2], st[6], ALU.mult))
                link(tt(st[8], st[7], st[3], ALU.add))
                link(nc.vector.reciprocal(st[6], st[8]))
                for b in range(B):
                    g = slice(b * NT, b * NT + NT)
                    stt(u[:, g], u[:, g], 2.0, wide(stat[:, 6, g], NT), ALU.mult, ALU.mult).then_inc(s_u, 1)

            def layernorm(k):
                centre(k, range(B))
                spread(k, range(B))
                normalise(k)

            def low(k):
                for c in range(NC):
                    m, b = NC * k + c, k % 2
                    cs = slice(b * SP_ + CW * c, b * SP_ + CW * c + CW)
                    dve.wait_ge(s_uhi, m + 1)
                    tt(US[D:P, cs], ps[0:D, c, 0:CW], US[0:D, cs], ALU.subtract).then_inc(s_us, 1)

            dve.wait_ge(s_const, 2)
            dve.wait_ge(d_w, 32)
            link(ts(wr_rep[:], ones[:], WR[:, O_WR:O_WR + 1], None, ALU.mult))
            link(nc.vector.tensor_copy(WRH[:], wr_rep[:]))
            link(tt(WRL[:], wr_rep[0:D, :], WRH[0:D, :], ALU.subtract))
            link(nc.vector.memset(mpart[:], -3e38))
            for b in range(B):
                link(nc.vector.memset(UU[0:D, 0, b * NT, :], 0.0))
            dve.wait_ge(d_txt, 32)
            layernorm(0)
            low(0)
            low(1)
            dve.wait_ge(s_split2, 1)

            dve.sem_inc(s_yf, 2)
            dve.sem_inc(s_hd, 2)
            dve.sem_inc(s_af, 2)
            dve.sem_inc(s_nf, 1)
            base, m = [0], [0]

            def chain(instruction):
                m[0] += 1
                instruction.then_inc(s_dvl, 1)
                dve.wait_ge(s_dvl, base[0] + m[0])

            def low_part(v, b, k):
                dve.wait_ge(s_ar, NC * v + k + 1)
                cs = slice(CW * k, CW * k + CW)
                src = a_bank(b, k)[:, 0:CW]
                nc.vector.tensor_copy(qs[b][D:P, cs], qs[b][0:D, cs])
                stt(ql[b][0:D, cs], src[0:D], head_col(C_BQ)[0:D], qs[b][0:D, cs], ALU.add, ALU.subtract)
                stt(ks[b][0:D, cs], src[D:P], head_col(C_BK)[D:P], ks[b][D:P, cs], ALU.add,
                    ALU.subtract).then_inc(s_af, 1)

            def head_col(col):
                return cols[:, bass.ds(head_of[0] + col, 1)]

            def maximum(v, b, k):
                i, a, z = SMAX[k]
                dve.wait_ge(s_a, NA * v + NC + k + 1)
                nc.vector.tensor_reduce(mpart[:, b, i, a // 512:a // 512 + 1], a_bank(b, NC + k)[:, 0:z - a], AX.X,
                                        ALU.max).then_inc(s_af, 1)

            def whole_maximum(v, b):
                dve.wait_ge(s_af, NA * v + NA + 1)
                chain(nc.vector.tensor_reduce(mneg[:, b], mpart[:, b], AX.X, ALU.max))
                ts(mneg[:, b], mneg[:, b], -1.0, None, ALU.mult).then_inc(s_mneg, 1)

            def take_row(v, b):
                dve.wait_ge(s_a, NA * v + NA)
                nc.vector.tensor_copy(mrow[b][:], a_bank(b, NA - 1)[0:NT, 0:P]).then_inc(s_af, 1)

            def output(w, b, c):
                dve.wait_ge(s_to, NC * w + c + 3)
                o = ps[:, 3, 0:TPC * (D + 1)].rearrange("p (r d) -> p r d", d=D + 1)
                chain(nc.vector.reciprocal(rden[:, c % 2], o[:, :, D]))
                tt(onrm[:, c % 2], o[:, :, 0:D], wide(rden[:, c % 2], TPC), ALU.mult).then_inc(s_nf, 1)
                dve.wait_ge(s_nf, NC * w + c + 2)
                hc = h[:, b * NT + TPC * c:b * NT + TPC * c + TPC, :]
                chain(tt(hc, hc, onrm[:, c % 2], ALU.add))

            def slot(w, b, first=False, follow=True):
                for s in range(NS):
                    if follow:
                        for k in PROJECT_AT.get(s, ()):
                            low_part(w + 1, 1 - b, k)
                        for k in MAX_AT.get(s, ()):
                            maximum(w + 1, 1 - b, k)
                        if s == WHOLE_AT:
                            whole_maximum(w + 1, 1 - b)
                        if s == TURN_MAX_AT:
                            take_row(w + 1, 1 - b)
                    for c in range(NC):
                        if BACK_AT[c] == s:
                            output(w, b, c)
                        if BACK_AT[c] == s + NS and not first:
                            output(w - 1, 1 - b, c)
                    if not follow and s == max(x - NS for x in BACK_AT):
                        link(nc.vector.tensor_copy(h[0:1, 0, :], alone[:, 0]))
                        centre(1, [0])
                    if not follow and s == EARLY_LN + 5:
                        spread(1, [0])

            head_of = [0]
            for k in range(G):
                if k < NC:
                    low_part(0, 0, k)
                elif k < NC + NM:
                    maximum(0, 0, k - NC)
                if k in V_ON_DVE:
                    dve.wait_ge(s_v, k + 1)
                    nc.vector.tensor_copy(VX[:, k // NT, k % NT, :, 0:D], ps[:, V_BANKS[k % 3], :]
                                          .rearrange("p (h d) -> p h d", d=D)).then_inc(s_vx[1], 1)
            for k in range(G - NC, NM):
                maximum(0, 0, k)
            whole_maximum(0, 0)
            take_row(0, 0)
            dve.wait_ge(s_cst, 1)
            slot(0, 0, first=True)
            before_loop, per_slot = m[0], 1 + 2 * NC
            with dve.Fori(0, NH - 1) as i:
                head_of[0], base[0], m[0] = i + 1, i * (2 * per_slot) + before_loop, 0
                slot(2 * i + 1, 1)
                slot(2 * i + 2, 0)
                assert m[0] == 2 * per_slot
            base[0], m[0] = (NH - 1) * 2 * per_slot + before_loop, 0
            slot(2 * NH - 1, 1, follow=False)
            output(2 * NH - 1, 1, NC - 1)

            link(nc.vector.tensor_copy(h[0:1, NT, :], alone[:, 1]))

            centre(1, [1])
            spread(1, [1])
            normalise(1)
            low(2)
            low(3)

            def compare(b, t):
                m = NT * b + t
                sl, w = m % 3, wcol[:, b, t:t + 1]
                if m >= 3:
                    dve.wait_ge(s_rk, m - 2)
                behind = P * t + P
                ts(above[:, sl, 0:behind], wbc[:, b, 0:behind], w, None, ALU.is_lt)
                if behind < SP_:
                    ts(above[:, sl, behind:SP_], wbc[:, b, behind:SP_], w, None, ALU.is_le)
                stt(tie[:, sl, :], wbc[:, b, P * t:behind], w, after[:], ALU.is_equal, ALU.mult).then_inc(s_cmp, 1)

            def take_y(b):
                for c in range(NC):
                    item = B * NC + 3 * NC * b + 2 * NC + c
                    dve.wait_ge(s_r, item + 1)
                    gc = slice(b * NT + TPC * c, b * NT + TPC * c + TPC)
                    tt(sq[:, gc], ps[:, 3 + item % 4, 0:TPC * D].rearrange("p (t d) -> p t d", d=D),
                       rows[:, R_B2:R_B2 + D].unsqueeze(1).broadcast_to([P, TPC, D]), ALU.add).then_inc(s_rd, 1)

            def add_y(b):
                g = slice(b * NT, b * NT + NT)
                dve.wait_ge(s_rt, b + 1)
                stt(sel[:, b], ps[:, 7, G + NT * b:G + NT * b + NT], float(KK), wcol[:, b], ALU.is_lt,
                    ALU.mult).then_inc(s_rtf, 1)
                dve.wait_ge(s_rtf, b + 1)
                dve.wait_ge(s_rd, NC * (b + 1))
                link(tt(sq[:, g], sq[:, g], wide(sel[:, b], NT), ALU.mult))
                dve.wait_ge(s_skip, b + 1)
                link(tt(h[:, g], h[:, g], sq[:, g], ALU.add))

            for b in range(B):
                dve.wait_ge(s_wt, b + 1)
            link(nc.vector.tensor_copy(wcol[:], ps[:, 7, 0:G].rearrange("p (b t) -> p b t", t=NT)))
            for t in range(NT):
                compare(0, t)
            for t in range(NT):
                compare(1, t)
                if t == 2:
                    take_y(0)
            add_y(0)
            centre(2, [0])
            take_y(1)
            add_y(1)

            centre(2, [1])
            spread(2, range(B))
            normalise(2)
            for b in range(B):
                dve.wait_ge(s_u, 2 * B + b + 1)
                g0, g1 = b * NT, b * NT + NT
                link(nc.vector.tensor_copy(UU[0:D, 0, g0 + 1:g1, :], UU[D:P, 1, g0:g1 - 1, :]))
                nc.vector.tensor_copy(UU[D:P, 0, g0:g1, :], UU[0:D, 1, g0:g1, :]).then_inc(s_ush, 1)
            for k in range(5):
                c0, c1 = 14 * k, min(14 * k + 14, D)
                dve.wait_ge(s_cv, k + 1)
                y = ps[0:D, k, 0:2 * G * (c1 - c0)].rearrange("p (c g) -> p g c", g=2 * G)
                tt(h[0:D, :, c0:c1], y[:, 0:G, :], h[0:D, :, c0:c1], ALU.add).then_inc(s_cvf, 1)
                tt(h[D:P, :, c0:c1], y[:, G:2 * G, :], h[D:P, :, c0:c1], ALU.add).then_inc(s_cvf, 1)
            dve.wait_ge(s_cvf, 10)

            layernorm(3)
            low(4)
            low(5)

            def relu(t, e):
                dve.wait_ge(s_hh, NE * t + e + 1)
                dve.wait_ge(s_hu, NE * t + e + 1)
                for k in range(2):
                    ins_ = ts(eh[:, e, k, :], ps[:, 4 + e % 4, 256 * k:256 * k + 256],
                              cols[:, C_EB1 + 2 * e + k:C_EB1 + 2 * e + k + 1], 0.0, ALU.add, ALU.max)
                ins_.then_inc(s_hd, 1)

            for e in range(1, NE, 2):
                relu(0, e)
            dve.wait_ge(s_g, 1)
            tt(gate[:], ps[:, 3, 0:G * NE].rearrange("p (g e) -> p g e", e=NE),
               rows[:, R_BG:R_BG + NE].unsqueeze(1).broadcast_to([P, G, NE]), ALU.add).then_inc(s_gf, 1)
            dve.wait_ge(s_gf, 1)
            narrow = lambda r: stat[:, r, :].unsqueeze(2).broadcast_to([P, G, NE])
            order = desc[:].unsqueeze(1).broadcast_to([P, G, NE])

            def first_of(gates, top, where):
                link(nc.vector.tensor_reduce(stat[:, top, :], gates, AX.X, ALU.max))
                link(tt(eq[:], gates, narrow(top), ALU.is_equal))
                link(tt(eq[:], eq[:], order, ALU.mult))
                link(nc.vector.tensor_reduce(stat[:, 9, :], eq[:], AX.X, ALU.max))
                link(tt(where, order, narrow(9), ALU.is_equal))

            first_of(gate[:], 1, is0[:])
            link(stt(gate[:], is0[:], -3e38, gate[:], ALU.mult, ALU.add))
            first_of(gate[:], 0, is1[:])
            tt(stat[:, 4, :], stat[:, 0, :], stat[:, 1, :], ALU.subtract).then_inc(s_d, 1)
            dve.wait_ge(s_ed, 1)
            link(ts(stat[:, 6, :], stat[:, 5, :], 1.0, None, ALU.add))
            link(nc.vector.reciprocal(stat[:, 7, :], stat[:, 6, :]))
            link(tt(stat[:, 8, :], stat[:, 7, :], stat[:, 5, :], ALU.mult))
            link(tt(comb[:], is0[:], narrow(7), ALU.mult))
            link(tt(is1[:], is1[:], narrow(8), ALU.mult))
            link(tt(comb[:], comb[:], is1[:], ALU.add))
            def combine(t, y):
                dve.wait_ge(s_hu, NE * t + 2 * NE)
                for r in range(2):
                    ins_ = tt(yw[:, r], ps[:, 2 * y + r, :].rearrange("p (e d) -> p e d", d=D),
                              comb[:, bass.ds(2 * t + r, 1), :].rearrange("p o e -> p (o e)").unsqueeze(2)
                              .broadcast_to([P, NE, D]), ALU.mult)
                ins_.then_inc(s_yf, 1)
                dve.wait_ge(s_yf, t + 3)
                nc.vector.tensor_reduce(ysum[:], yw[:].rearrange("p r e d -> p r d e"), AX.X,
                                        ALU.add).then_inc(s_dvm, 1)
                dve.wait_ge(s_dvm, t + 1)
                hb = h[:, bass.ds(2 * t, 2), :]
                tt(hb, hb, ysum[:], ALU.add).then_inc(s_fin, 1)
                dve.wait_ge(s_fin, t + 1)

            with dve.Fori(0, G // 4) as i:
                for y in range(2):
                    for e in range(1, NE, 2):
                        relu(2 * i + y + 1, e)
                    combine(2 * i + y, y)
            combine(G // 2 - 1, 0)


def kernel(**inputs):
    import numpy as np
    import concourse.bacc as bacc
    from concourse.bass_utils import run_bass_kernel_spmd

    a = {k: np.asarray(v) for k, v in inputs.items()}
    cat = np.concatenate
    t_q, t_k = a["L0_tok_Wq"], a["L0_tok_Wk"]
    column = lambda v: v.reshape(-1, D).T
    twice = lambda m: cat([m, m], axis=0)
    laid = {
        "xT": a["x"].reshape(B, T, D).transpose(2, 0, 1).reshape(D, B * T),
        "txt": a["txt"],
        "gammaT": a["L0_tok_d_gamma_batched"].T,
        "w64": cat([t_q, t_q, t_k, t_k, a["L0_tok_Wv"], a["L0_attn_Wq"], a["L0_attn_Wk"], a["L0_ffn_w1"],
                    a["L1_ffn_Wg"].T, a["L1_ffn_W1"].transpose(2, 0, 1).reshape(D, NE * HID), a["L0_ffn_wr"]], axis=1),
        "cols": cat([twice(column(a["L0_tok_bq"])), twice(column(a["L0_tok_bk"])),
                     twice(column(a["L0_attn_bq"])), twice(column(a["L0_attn_bk"])),
                     a["L0_ffn_b1"].reshape(2, P).T, a["L1_ffn_b1"].reshape(2 * NE, P).T,
                     np.tile(a["L0_tok_prelu_a"].reshape(1, 1), (P, 1)),
                     np.tile(a["L0_ffn_br"].reshape(1, 1), (P, 1))], axis=1),
        "rows": cat([a["L0_tok_bv"], a["L0_tok_bo"], a["L0_attn_bu"], a["L0_ffn_b2"], a["L1_ffn_bg"]]).reshape(1, NROW),
        "wvT": a["L0_attn_Wv"].reshape(D, NH, D).transpose(2, 1, 0),
        "bvT": column(a["L0_attn_bv"]),
        "wu": a["L0_attn_Wu"].reshape(NH, D, D).transpose(1, 0, 2),
        "two": a["L0_tok_Wo"],
        "w2": a["L0_ffn_w2"].reshape(2, P, D).transpose(1, 0, 2),
        "ew2": a["L1_ffn_W2"].transpose(2, 0, 1).reshape(2, P, NE, D).transpose(1, 0, 2, 3),
        "eb2": a["L1_ffn_b2"].reshape(1, NE * D),
        "cpad": np.pad(a["L1_attn_c"][0][:, ::-1], ((0, 0), (D, D))).reshape(-1),
    }
    laid = {k: np.ascontiguousarray(v) for k, v in laid.items()}
    nc = bacc.Bacc("TRN2", target_bir_lowering=False, num_devices=1)
    ins = {k: nc.dram_tensor(f"in_{k}", v.shape, F32, kind="ExternalInput").ap() for k, v in laid.items()}
    out = nc.dram_tensor("out", (B, S, D), F32, kind="ExternalOutput").ap()
    early_fusion(nc, ins, out)
    r = run_bass_kernel_spmd(nc, [{f"in_{k}": v for k, v in laid.items()}], core_ids=[0])
    return r.results[0]["out"]
```
